# Optimizing a Trainium2 kernel written in Bass

```python
import numpy as np
import jax
import jax.numpy as jnp

def _softmax(x, axis=-1):
    return jax.nn.softmax(x, axis=axis)

def _gelu(x):
    return jax.nn.gelu(x, approximate=True)

def _silu(x):
    return jax.nn.silu(x)

def _sigmoid(x):
    return jax.nn.sigmoid(x)

def _layernorm(x, axis=-1, eps=1e-05):
    m = jnp.mean(x, axis=axis, keepdims=True)
    v = jnp.var(x, axis=axis, keepdims=True)
    return (x - m) / jnp.sqrt(v + eps)

def _scatter_add(tgt, idx, src, axis=0):
    return tgt.at[idx].add(src)

def _segment_sum(src, seg, n):
    return jax.ops.segment_sum(src, seg, n)
kernel_name = 'mk_early_fusion_d1_tok_img768_r4_aaea8b'

def setup_inputs(seed: int=0):
    np.random.seed(seed)
    _w = jnp.asarray

    def _rec_inputs():
        import jax
        import jax.numpy as jnp
        _rk = jax.random.key(seed)
        x = -0.00016672 + 0.999947 * jax.random.normal(jax.random.fold_in(_rk, 1), (8, 3, 96, 96), jnp.float32)
        txt = 7.79078e-05 + 0.554693 * jax.random.normal(jax.random.fold_in(_rk, 2), (8, 128, 192), jnp.float32)
        return (x, txt)
    x, txt = _rec_inputs()

    def _L0_tok_setup():
        import jax, jax.numpy as jnp
        import numpy as np
        PATCH = 16
        key = jax.random.key(seed)
        k1, k2, k3, k4 = jax.random.split(key, 4)
        B, C, H, W = (64, 3, 96, 96)
        embed_dim = 192
        num_patches = H // PATCH * (W // PATCH)
        patch_flat = PATCH * PATCH * 3
        x = jax.random.normal(k1, (B, C, H, W), dtype=jnp.float32)
        proj_w = jax.random.normal(k2, (embed_dim, patch_flat), dtype=jnp.float32) * 0.02
        proj_b = jax.random.normal(k3, (embed_dim,), dtype=jnp.float32) * 0.02
        pos_embed = jax.random.normal(k4, (1, num_patches, embed_dim), dtype=jnp.float32) * 0.02
        return {'x': x, 'proj_w': proj_w, 'proj_b': proj_b, 'pos_embed': pos_embed}
    _L0_tok_all = _L0_tok_setup()
    _L0_tok_in = {k: v for k, v in _L0_tok_all.items() if k in ('proj_w', 'proj_b', 'pos_embed')}
    del _L0_tok_all

    def _L0_attn_setup():
        import jax, jax.numpy as jnp
        import numpy as np
        import math
        B, S, E = (2, 512, 192)
        H = 12
        V = 50257
        EPS = 1e-05

        def _layernorm(x, w):
            mu = jnp.mean(x, axis=-1, keepdims=True)
            var = jnp.mean(jnp.square(x - mu), axis=-1, keepdims=True)
            return (x - mu) * jax.lax.rsqrt(var + EPS) * w
        key = jax.random.key(seed)
        ks = jax.random.split(key, 7)
        x = jax.random.normal(ks[0], (B, S, E), dtype=jnp.float32)
        e = jax.random.normal(ks[1], (B, S, E), dtype=jnp.float32)
        p = jax.random.normal(ks[2], (B, S, E), dtype=jnp.float32)
        ln_w = jnp.ones((E,), dtype=jnp.float32)
        W_qk = 0.02 * jax.random.normal(ks[3], (H, E), dtype=jnp.float32)
        W_o = 0.02 / math.sqrt(2 * 12) * jax.random.normal(ks[4], (E, H * E), dtype=jnp.float32)
        wte = 0.02 * jax.random.normal(ks[5], (V, E), dtype=jnp.float32)
        return {'x': x, 'e': e, 'p': p, 'ln_w': ln_w, 'W_qk': W_qk, 'W_o': W_o, 'wte': wte}
    _L0_attn_all = _L0_attn_setup()
    _L0_attn_in = {k: v for k, v in _L0_attn_all.items() if k in ('e', 'p', 'ln_w', 'W_qk', 'W_o', 'wte')}
    del _L0_attn_all

    def _L0_ffn_setup():
        import jax, jax.numpy as jnp
        import numpy as np
        B, S, D, F, E = (8, 512, 192, 768, 16)
        CAP = 64
        EPS = 1e-06

        def _switch_moe_block(x, ln_w, w_router, wi, wo):
            var = jnp.mean(jnp.square(x.astype(jnp.float32)), axis=-1, keepdims=True)
            normed = (x * jax.lax.rsqrt(var + EPS)).astype(x.dtype) * ln_w
            logits = jnp.einsum('bsd,de->bse', normed.astype(jnp.float32), w_router.astype(jnp.float32))
            probs = jax.nn.softmax(logits, axis=-1)
            expert_idx = jnp.argmax(probs, axis=-1)
            onehot = jax.nn.one_hot(expert_idx, E, dtype=jnp.float32)
            priority = jnp.cumsum(onehot, axis=1)
            keep = onehot * (priority <= CAP)
            pos = (priority - 1.0).astype(jnp.int32)
            dispatch = keep[..., None] * jax.nn.one_hot(pos, CAP, dtype=jnp.float32)
            expert_in = jnp.einsum('bsec,bsd->becd', dispatch, normed)
            h = jax.nn.relu(jnp.einsum('becd,edf->becf', expert_in, wi))
            expert_out = jnp.einsum('becf,efd->becd', h, wo)
            combined = jnp.einsum('bsec,becd->bsd', dispatch, expert_out)
            routed = jnp.sum(dispatch, axis=(2, 3)) > 0
            next_states = jnp.where(routed[..., None], combined.astype(x.dtype), normed)
            router_prob = jnp.max(probs, axis=-1, keepdims=True).astype(x.dtype)
            return x + router_prob * next_states
        key = jax.random.key(seed)
        k_x, k_r, k_wi, k_wo = jax.random.split(key, 4)
        x = jax.random.normal(k_x, (B, S, D), dtype=jnp.float32)
        ln_w = jnp.ones((D,), dtype=jnp.float32)
        w_router = jax.random.normal(k_r, (D, E), dtype=jnp.float32) * 0.02
        wi = jax.random.normal(k_wi, (E, D, F), dtype=jnp.float32) * D ** (-0.5)
        wo = jax.random.normal(k_wo, (E, F, D), dtype=jnp.float32) * F ** (-0.5)
        return {'x': x, 'ln_w': ln_w, 'w_router': w_router, 'wi': wi, 'wo': wo}
    _L0_ffn_all = _L0_ffn_setup()
    _L0_ffn_in = {k: v for k, v in _L0_ffn_all.items() if k in ('ln_w', 'w_router', 'wi', 'wo')}
    del _L0_ffn_all
    return {'x': x, 'txt': txt, 'L0_tok_proj_w': _L0_tok_in['proj_w'], 'L0_tok_proj_b': _L0_tok_in['proj_b'], 'L0_tok_pos_embed': _L0_tok_in['pos_embed'], 'L0_attn_e': _L0_attn_in['e'], 'L0_attn_p': _L0_attn_in['p'], 'L0_attn_ln_w': _L0_attn_in['ln_w'], 'L0_attn_W_qk': _L0_attn_in['W_qk'], 'L0_attn_W_o': _L0_attn_in['W_o'], 'L0_attn_wte': _L0_attn_in['wte'], 'L0_ffn_ln_w': _L0_ffn_in['ln_w'], 'L0_ffn_w_router': _L0_ffn_in['w_router'], 'L0_ffn_wi': _L0_ffn_in['wi'], 'L0_ffn_wo': _L0_ffn_in['wo']}

def reference(x, txt, L0_tok_proj_w, L0_tok_proj_b, L0_tok_pos_embed, L0_attn_e, L0_attn_p, L0_attn_ln_w, L0_attn_W_qk, L0_attn_W_o, L0_attn_wte, L0_ffn_ln_w, L0_ffn_w_router, L0_ffn_wi, L0_ffn_wo):
    import jax
    import jax.numpy as jnp

    def _L0_tok_ref(x, proj_w, proj_b, pos_embed):
        import jax, jax.numpy as jnp
        import numpy as np
        PATCH = 16
        p = PATCH
        B, C, H, W = x.shape
        x = x.reshape(B, C, H // p, p, W // p, p).transpose(0, 1, 2, 4, 3, 5)
        x = x.reshape(B, C, -1, p * p)
        x = jnp.swapaxes(x, 2, 3)
        x = x.reshape(B, -1, p * p * 3)
        x = jnp.einsum('bnd,ed->bne', x, proj_w) + proj_b
        return x + pos_embed

    def _L0_attn_ref(x, e, p, ln_w, W_qk, W_o, wte):
        import jax, jax.numpy as jnp
        import numpy as np
        import math
        B, S, E = (2, 512, 192)
        H = 12
        V = 50257
        EPS = 1e-05

        def _layernorm(x, w):
            mu = jnp.mean(x, axis=-1, keepdims=True)
            var = jnp.mean(jnp.square(x - mu), axis=-1, keepdims=True)
            return (x - mu) * jax.lax.rsqrt(var + EPS) * w
        xb, sb, eb = x.shape
        xn = _layernorm(x, ln_w)
        avg_wte = jnp.mean(wte, axis=0)
        Q = xn[:, None, :, :] * W_qk[None, :, None, :]
        attn = jnp.einsum('bhse,bhte->bhst', Q, Q) / math.sqrt(eb)
        causal = jnp.tril(jnp.ones((sb, sb), dtype=bool))
        attn = jnp.where(causal[None, None], attn, -jnp.inf)
        attn = jax.nn.softmax(attn, axis=-1)
        Vv = xn[:, None, :, :] - avg_wte[None, None, None, :]
        out = jnp.einsum('bhst,bhte->bhse', attn, Vv)
        N_reg = 1.0 / jnp.arange(1, sb + 1, dtype=jnp.float32)
        out = out * N_reg[None, None, :, None]
        out = out.transpose(0, 2, 1, 3).reshape(xb, sb, H * eb)
        out = out @ W_o.T
        return out

    def _L0_ffn_ref(x, ln_w, w_router, wi, wo):
        import jax, jax.numpy as jnp
        import numpy as np
        B, S, D, F, E = (8, 512, 192, 768, 16)
        CAP = 64
        EPS = 1e-06

        def _switch_moe_block(x, ln_w, w_router, wi, wo):
            var = jnp.mean(jnp.square(x.astype(jnp.float32)), axis=-1, keepdims=True)
            normed = (x * jax.lax.rsqrt(var + EPS)).astype(x.dtype) * ln_w
            logits = jnp.einsum('bsd,de->bse', normed.astype(jnp.float32), w_router.astype(jnp.float32))
            probs = jax.nn.softmax(logits, axis=-1)
            expert_idx = jnp.argmax(probs, axis=-1)
            onehot = jax.nn.one_hot(expert_idx, E, dtype=jnp.float32)
            priority = jnp.cumsum(onehot, axis=1)
            keep = onehot * (priority <= CAP)
            pos = (priority - 1.0).astype(jnp.int32)
            dispatch = keep[..., None] * jax.nn.one_hot(pos, CAP, dtype=jnp.float32)
            expert_in = jnp.einsum('bsec,bsd->becd', dispatch, normed)
            h = jax.nn.relu(jnp.einsum('becd,edf->becf', expert_in, wi))
            expert_out = jnp.einsum('becf,efd->becd', h, wo)
            combined = jnp.einsum('bsec,becd->bsd', dispatch, expert_out)
            routed = jnp.sum(dispatch, axis=(2, 3)) > 0
            next_states = jnp.where(routed[..., None], combined.astype(x.dtype), normed)
            router_prob = jnp.max(probs, axis=-1, keepdims=True).astype(x.dtype)
            return x + router_prob * next_states
        return _switch_moe_block(x, ln_w, w_router, wi, wo)
    h = _L0_tok_ref(x, L0_tok_proj_w, L0_tok_proj_b, L0_tok_pos_embed)
    h = jnp.concatenate([h, txt], axis=1)
    h = h + _L0_attn_ref(_layernorm(h, axis=-1), L0_attn_e, L0_attn_p, L0_attn_ln_w, L0_attn_W_qk, L0_attn_W_o, L0_attn_wte)
    h = h + _L0_ffn_ref(_layernorm(h, axis=-1), L0_ffn_ln_w, L0_ffn_w_router, L0_ffn_wi, L0_ffn_wo)
    return h

_drawn_inputs = setup_inputs


def setup_inputs(seed=0):
    import zlib

    import numpy as np

    out = dict(_drawn_inputs(seed))
    spreads = {'L0_attn_ln_w': (1.0, 0.6), 'L0_ffn_ln_w': (1.0, 0.593)}
    factors = {'L0_tok_proj_b': 3.221,
     'L0_tok_pos_embed': 3.212,
     'L0_attn_W_qk': 64.0,
     'L0_attn_wte': 64.0}
    for name, (base, spread) in spreads.items():
        noise = np.random.default_rng([zlib.crc32(name.encode()), seed]).standard_normal(out[name].shape)
        drawn = base * np.exp(spread * noise) if base else spread * noise
        out[name] = jnp.asarray(drawn.astype(out[name].dtype))
    for name, factor in factors.items():
        out[name] = (out[name] * factor).astype(out[name].dtype)
    return out
```

```python
import numpy as np
import concourse.bass as bass
from concourse import mybir
from contextlib import ExitStack

NBATCH, SEQ, EMB, HEADS = 8, 164, 192, 12
IMG = 36
SA = 128
SB = SEQ - SA
EC = 96
E0, E1 = 128, EMB - 128
HB = 3
NG = HEADS // HB
WCH = HEADS + HEADS // 2
NBT = 3
BP = NBATCH * SB // NBT
SLOTS = NBATCH + NBT
EXP, FF, CAP, T = 16, 768, 64, 128
FC = FF // 128
TOK = NBATCH * SEQ
MAXB = EXP + (TOK - EXP) // T
VOCAB = 50257
WR = 14
WCHUNKS = VOCAB // 128 // WR
WTAIL = VOCAB - 128 * WR * WCHUNKS
WBUF = 4
XROWS = (MAXB + 1) * T
TRASH = XROWS

C_ID, C_NA, C_NB, C_NBP, C_EM, C_VAL, C_TR, C_BI = 0, 128, 129, 130, 133, 149, 160, 171
NCST = C_BI + MAXB
PAIRS = [(i, b) for i in range(NBT) for b in range(NBATCH) if b * SB < (i + 1) * BP and (b + 1) * SB > i * BP]
M_ID, M_ONE, M_TRI, M_MA, M_MB, M_BB, M_BX, M_BA = 0, 1, 2, 3, 4, 6, 9, 11
NMAT = M_BA + len(PAIRS)
NEG = -1e30


def program(nc, patches, projw, projb, pos, txtA, txtB, txtBp, wqk, lnw, lnc, wte, wo_attn,
            flnw, wrt, wi, wo, cst_d, mat_d, out):
    f32, bf16, i32 = mybir.dt.float32, mybir.dt.bfloat16, mybir.dt.int32
    ALU, ACT = mybir.AluOpType, mybir.ActivationFunctionType
    X = mybir.AxisListType.X
    ds = bass.ds

    xd = nc.dram_tensor("dispatched", (XROWS + SLOTS * 128, EMB), f32).ap()
    yd = nc.dram_tensor("expert_out", (MAXB * T, EMB), f32).ap()

    ctx = ExitStack()
    with ctx:
        def sb(name, shape, dt=f32):
            return ctx.enter_context(nc.sbuf_tensor(name, shape, dt))

        def pb(name):
            return ctx.enter_context(nc.psum_tensor(name, [128, 512], f32))

        def sem(name):
            return ctx.enter_context(nc.semaphore(name))

        cst = sb("cst", [128, NCST])
        mat = sb("mat", [128, NMAT, 128], bf16)
        ident = cst[:, C_ID:C_ID + 128]
        H = sb("H", [128, SLOTS, EMB])
        hB = sb("hB", [SB, NBATCH, EMB])
        wo_sb = sb("wo_sb", [128, WCH, EMB])
        ws = sb("ws", [128, 2, EMB])
        acc = sb("acc", [128, WR, EMB])
        lncol = sb("lncol", [128, 2])
        flnb = sb("flnb", [128, EMB])
        wr_sb = sb("wr_sb", [EC, 2, EXP])
        rstd = sb("rstd", [128, 2, NBATCH])
        nmr = sb("nmr", [128, 2, NBATCH])
        zA, zB = sb("zA", [128, EMB]), sb("zB", [SB, EMB])
        vA, vB = sb("vA", [128, EMB]), sb("vB", [SB, EMB])
        zT = sb("zT", [EC, 2, SEQ])
        w2 = sb("w2", [EC, 2, HEADS])
        Awf = sb("AwA", [128, 2 * HEADS * SA])
        AwA, AwB = Awf[0:EC, :].rearrange("p (k h s) -> p k h s", k=2, h=HEADS), sb("AwB", [EC, 2, HEADS, SB])
        mat32 = Awf[:, 0:NMAT * 128]
        PA, PB = sb("PA", [128, HEADS, SA]), sb("PB", [HB * SB, NG, SEQ])
        PTA = sb("PTA", [128, HEADS, SA])
        PTB0, PTB1 = sb("PTB0", [128, HEADS, SB]), sb("PTB1", [SB, HEADS, SB])
        negmax, lsum, rn = sb("negmax", [128, 16]), sb("lsum", [128, 16]), sb("rn", [128, 16])
        rinv = sb("rinv", [128, 16])
        oTA = sb("oTA", [128, WCH, SA])
        oTB = sb("oTB", [128, WCH, NBATCH * SB])
        wbuf = sb("wbuf", [128, WBUF * WR * EMB])
        wchunk = [wbuf[:, i * WR * EMB:(i + 1) * WR * EMB] for i in range(WBUF)]
        WIN, WON = 2 * FC * 128, FC * EMB
        wi_sb = [wbuf[0:EC, p * WIN:(p + 1) * WIN].rearrange("p (k c m) -> p k c m", k=2, c=FC) for p in range(2)]
        wo_x = [wbuf[:, 2 * WIN + p * WON:2 * WIN + (p + 1) * WON].rearrange("p (c e) -> p c e", c=FC) for p in range(2)]
        wtail = sb("wtail", [WTAIL, EMB])
        flat = oTB[:, :, :].rearrange("p c s -> p (c s)")
        pat_sb = flat[:, 0:6 * 288].rearrange("p (k n) -> p k n", k=6)
        pw_sb = flat[:, 1728:1728 + 6 * EMB].rearrange("p (k e) -> p k e", k=6)
        embT = flat[0:EC, 2880:2880 + 576].rearrange("p (k n) -> p k n", k=2)
        posb = flat[0:IMG, 3456:3456 + EMB]
        pbb = flat[0:IMG, 3648:3648 + EMB]
        st6 = sb("st6", [128, 2, NBATCH, 6])
        mv = sb("mv", [128, 2, NBATCH, 2])
        nT = Awf[0:EC, 0:2 * SLOTS * 128].rearrange("p (k n) -> p k n", k=2)
        paf = PA[:, :, :].rearrange("p h s -> p (h s)")
        pta = PTA[:, :, :].rearrange("p h s -> p (h s)")
        norm = sb("norm", [128, SLOTS, EMB])
        otf = oTA[:, :, :].rearrange("p c s -> p (c s)")
        base = otf[:, 0:SLOTS * EMB].rearrange("p (j e) -> p j e", j=SLOTS)
        yg = flat[:, 0:SLOTS * EMB].rearrange("p (j e) -> p j e", j=SLOTS)
        xb = [paf[:, p * EMB:(p + 1) * EMB] for p in range(2)]
        ysb = [paf[:, (2 + p) * EMB:(3 + p) * EMB] for p in range(2)]
        xT = paf[0:EC, 4 * EMB:4 * EMB + 2 * T].rearrange("p (k n) -> p k n", k=2)
        hT = pta[:, 0:FC * T].rearrange("p (c n) -> p c n", c=FC)
        fst = sb("fst", [128, SLOTS, 6])
        fmv = sb("fmv", [128, SLOTS, 2])
        sm = sb("sm", [128, 16, SLOTS])
        lg = sb("lg", [128, SLOTS, EXP])
        w16 = [sb(f"w16_{i}", [128, SLOTS, EXP]) for i in range(3)]
        oh, kp = sb("oh", [128, SLOTS, EXP], bf16), sb("kp", [128, SLOTS, EXP], bf16)
        nexp = sb("nexp", [128, 6, EXP])
        nexi = sb("nexi", [128, 2, EXP], i32)
        bex = sb("bex", [128, MAXB, EXP])
        beF, beI = sb("beF", [128, MAXB]), sb("beI", [128, MAXB + 1], i32)
        nbI = beI[:, MAXB:MAXB + 1]
        posI, gI = sb("posI", [128, SLOTS], i32), sb("gI", [128, SLOTS], i32)
        avg = sb("avg", [128, 2])
        cN = sb("cN", [128, EMB])
        zeros = sb("zeros", [128, 9 * EMB])
        ln96, one = sb("ln96", [EC, 2]), sb("one", [128, 1])
        mhalf = sb("mhalf", [128, 32])
        wsum = sb("wsum", [128, EMB])

        bS = [pb("bS0"), pb("bS1")]
        bT = [pb("bT0"), pb("bT1")]
        bO = [pb("bO0"), pb("bO1")]
        bE = pb("bE")
        bJ = pb("bJ")

        cst_in, mat_in, pat_in, txt_in, small_in, wo_in = (sem(n) for n in
            ("cst_in", "mat_in", "pat_in", "txt_in", "small_in", "wo_in"))
        wte_in = [sem(f"wte_in{i}") for i in range(WBUF)]
        wtail_in, wte_added, dve_step, pool_step = (sem(n) for n in ("wtail_in", "wte_added", "dve_step", "pool_step"))
        emb_ready, embT_ready, tok_ready, stats_ready = (sem(n) for n in ("emb_ready", "embT_ready", "tok_ready", "stats_ready"))
        z_ready, v_ready, aw_ready = sem("z_ready"), sem("v_ready"), sem("aw_ready")
        score_ready, max_ready, exp_ready, rn_ready, p_ready = (sem(n) for n in
            ("score_ready", "max_ready", "exp_ready", "rn_ready", "p_ready"))
        t_ready, t_used = sem("t_ready"), sem("t_used")
        o_ready, o_used, e_ready, e_used = (sem(n) for n in ("o_ready", "o_used", "e_ready", "e_used"))
        j_ready, j_used, jb_ready = sem("j_ready"), sem("j_used"), sem("jb_ready")
        acc_ready, avg_sum, avg_ready, c_ready = (sem(n) for n in ("acc_ready", "avg_sum", "avg_ready", "c_ready"))
        rinv_ready, w2_ready, mat_ready = sem("rinv_ready"), sem("w2_ready"), sem("mat_ready")
        var_ready, pow_ready = sem("var_ready"), sem("pow_ready")
        norm_ready, nT_sum, nT_ready, lg_ready, le_ready, lx_ready = (sem(n) for n in
            ("norm_ready", "nT_sum", "nT_ready", "lg_ready", "le_ready", "lx_ready"))
        oh_ready, rank_ready, kp_ready, grank_ready, pos_ready, tab_ready = (sem(n) for n in
            ("oh_ready", "rank_ready", "kp_ready", "grank_ready", "pos_ready", "tab_ready"))
        zero_ready, zero_done, scattered = sem("zero_ready"), sem("zero_done"), sem("scattered")
        wi_in, wox_in, x_in = ([sem(f"{n}{p}") for p in range(2)] for n in ("wi_in", "wox_in", "x_in"))
        xT_sum, xT_ready = sem("xT_sum"), sem("xT_ready")
        h0_sum, h1_sum, h0_ready, h1_ready, y_sum, y_ready = (sem(n) for n in
            ("h0_sum", "h1_sum", "h0_ready", "h1_ready", "y_sum", "y_ready"))
        y_out = [sem(f"y_out{p}") for p in range(2)]
        got, res_ready, out_done = [sem(f"got{j}") for j in range(SLOTS)], sem("res_ready"), sem("out_done")
        even_stored, odd_stored = sem("even_stored"), sem("odd_stored")
        base_ready, stored = sem("base_ready"), sem("stored")

        def is0(b):
            return isinstance(b, int) and b == 0

        block = ctx.enter_context(nc.Block())
        SPR = 5
        TPB = 6


        @block.sync
        def _(sp):
            sp.dma_start(pat_sb, patches).then_inc(pat_in, 16)
            sp.dma_start(pw_sb, projw).then_inc(pat_in, 16)
            sp.dma_start(H[IMG:128, 0:NBATCH, :], txtA).then_inc(txt_in, 16)
            sp.dma_start(hB[:], txtB).then_inc(txt_in, 16)
            sp.dma_start(H[0:BP, NBATCH:SLOTS, :], txtBp).then_inc(txt_in, 16)
            wv = wte[0:128 * WR * WCHUNKS, :].rearrange("(p c r) e -> p c (r e)", p=128, c=WCHUNKS)

            def load_wte(c, s):
                sp.dma_start(wchunk[s], wv[:, ds(c, 1), :].rearrange("p c x -> p (c x)")).then_inc(wte_in[s], 16)

            for s in range(WBUF):
                load_wte(s, s)
                if s == 1:
                    sp.dma_start(wo_sb[:], wo_attn).then_inc(wo_in, 16)
                    sp.dma_start(wtail[:], wte[VOCAB - WTAIL:VOCAB, :]).then_inc(wtail_in, 16)
            sp.wait_ge(zero_ready, 1)
            for dst, rows in ((xd, MAXB + 1), (yd, MAXB)):
                for n in range(0, rows, 9):
                    m = min(9, rows - n)
                    sp.dma_start(dst[n * 128:(n + m) * 128, :].rearrange("(p n) e -> p (n e)", n=m),
                                 zeros[:, 0:m * EMB]).then_inc(zero_done, 16)
            with sp.Fori(1, WCHUNKS // WBUF) as i:
                for s in range(WBUF):
                    sp.wait_ge(wte_added, (i - 1) * (2 * WBUF) + 2 * (s + 1))
                    load_wte(i * WBUF + s, s)
            sp.wait_ge(wte_added, 2 * WCHUNKS)
            sp.wait_ge(tab_ready, 1)
            nb = sp.value_load(nbI[0:1, :], min_val=1, max_val=MAXB)

            def weights(b, p, used):
                e = sp.value_load(beI[0:1, ds(b, 1)], min_val=0, max_val=EXP - 1)
                if used is not None:
                    sp.wait_ge(h1_sum, used)
                sp.dma_start(wi_sb[p], wi[ds(e, 1)].rearrange("x p k c m -> (x p) k c m")).then_inc(wi_in[p], 16)
                if used is not None:
                    sp.wait_ge(y_sum, used)
                sp.dma_start(wo_x[p], wo[ds(e, 1)].rearrange("x p c e -> (x p) c e")).then_inc(wox_in[p], 16)

            def rows(b, p):
                sp.dma_start(xb[p], xd[ds(b * T, T), :]).then_inc(x_in[p], 16)

            weights(0, 0, None)
            sp.wait_ge(scattered, 16 * SLOTS)
            rows(0, 0)
            rows(1, 1)
            with sp.If(1 < nb):
                weights(1, 1, None)
                sp.wait_ge(xT_sum, 1)
                rows(2, 0)
            with sp.If(2 < nb):
                weights(2, 0, 1)
            with sp.Fori(1, MAXB // 2) as i:
                for p in range(2):
                    b = i * 2 + p
                    with sp.If(b < nb):
                        sp.wait_ge(xT_sum, b)
                        rows(b + 1, 1 - p)
                    with sp.If(b + 1 < nb):
                        weights(b + 1, 1 - p, b)
            sp.wait_ge(y_out[0], (nb + 1) // 2 * 16)
            sp.sem_inc(even_stored, 1)
            with sp.If(1 < nb):
                sp.wait_ge(y_out[1], nb // 2 * 16)
                sp.sem_inc(odd_stored, 1)
            sp.sem_inc(stored, 1)
            for j in range(SLOTS):
                sp.wait_ge(res_ready, j + 1)
                n = 128 if j < NBATCH else BP
                r0 = j * 128 if j < NBATCH else NBATCH * 128 + (j - NBATCH) * BP
                sp.dma_start(out[r0:r0 + n, :], yg[0:n, j, :]).then_inc(out_done, 16)
            sp.wait_ge(out_done, 16 * SLOTS)

        @block.gpsimd
        def _(pool):
            nc.gpsimd.memset(zeros[:], 0.0).then_inc(zero_ready, 1)
            nc.gpsimd.memset(mhalf[:], -0.5).then_inc(pool_step, 1)
            pool.wait_ge(pool_step, 1)

            def rsqrt(y, x, n, k):
                pool.wait_ge(var_ready, k)
                nc.gpsimd.tensor_tensor(y, x, mhalf[:, 0:n], ALU.pow).then_inc(pow_ready, 1)

            rsqrt(rstd[:, :, :].rearrange("p a b -> p (a b)"),
                  nmr[:, :, :].rearrange("p a b -> p (a b)"), 2 * NBATCH, 1)

            def weigh(b, n):
                pool.wait_ge(t_used, n)
                for g in range(4):
                    hs, ss, dst = (slice(4 * g, 4 * g + 4), slice(0, SA), AwA) if g < 3 else (slice(0, HEADS), slice(SA, SEQ), AwB)
                    for k in range(2):
                        o = dst[:, k, hs, :]
                        nc.gpsimd.tensor_tensor(o, zT[:, k, ss].unsqueeze(1).to_broadcast(list(o.shape)),
                                                w2[:, k, hs].unsqueeze(2).to_broadcast(list(o.shape)),
                                                ALU.mult).then_inc(aw_ready, 1)

            def normalise(b):
                for r in range(SPR):
                    pool.wait_ge(rn_ready, SPR * b + r + 1)
                    if r < 3:
                        t, q = PA[:, 4 * r:4 * r + 4, :], rn[:, 4 * r:4 * r + 4]
                    else:
                        q0 = 2 * (r - 3)
                        t, q = PB[:, q0:q0 + 2, :], rn[0:HB * SB, 12 + q0:14 + q0]
                    nc.gpsimd.tensor_tensor(t, t, q.unsqueeze(2).to_broadcast(list(t.shape)), ALU.mult).then_inc(p_ready, 1)

            pool.wait_ge(mat_in, 16)
            nc.gpsimd.tensor_copy(mat[:, :, :].rearrange("p m s -> p (m s)"), mat32).then_inc(mat_ready, 1)
            pool.wait_ge(mat_ready, 1)
            pool.wait_ge(w2_ready, 1)
            weigh(0, 1)
            normalise(0)
            with pool.Fori(0, NBATCH - 1) as b:
                weigh(b + 1, TPB * b + 2)
                normalise(b + 1)

            rsqrt(sm[:, 2:4, :].rearrange("p a b -> p (a b)"),
                  sm[:, 0:2, :].rearrange("p a b -> p (a b)"), 2 * SLOTS, 2)
            pool.wait_ge(zero_done, 96)
            pool.wait_ge(pos_ready, 1)
            for j in range(SLOTS):
                n = 128 if j < NBATCH else BP
                nc.gpsimd.indirect_dma_start(out=xd[:, :], out_offset=bass.IndirectOffsetOnAxis(ap=posI[0:n, j:j + 1], axis=0),
                                             in_=norm[0:n, j, :], in_offset=None).then_inc(scattered, 16)
            pool.wait_ge(stored, 1)
            pool.wait_ge(base_ready, 1)
            for j in range(SLOTS):
                n = 128 if j < NBATCH else BP
                nc.gpsimd.indirect_dma_start(out=yg[0:n, j, :], out_offset=None, in_=yd[:, :],
                                             in_offset=bass.IndirectOffsetOnAxis(ap=gI[0:n, j:j + 1], axis=0)).then_inc(got[j], 16)

        @block.scalar
        def _(act):
            act.dma_start(cst[:], cst_d).then_inc(cst_in, 16)
            act.dma_start(mat32, mat_d).then_inc(mat_in, 16)
            for dst, src in ((posb, pos), (pbb, projb), (w2[:], wqk), (ln96[:], lnw), (lncol[:], lnc),
                             (flnb[:], flnw), (wr_sb[:], wrt)):
                act.dma_start(dst, src).then_inc(small_in, 16)
            for k in range(2):
                act.wait_ge(emb_ready, k + 1)
                nc.scalar.activation(embT[:, k, :], bO[k][0:EC, 0:NBATCH * IMG], ACT.Copy).then_inc(embT_ready, 1)
            act.wait_ge(small_in, 16 * 7)

            def zt_copy(n, par):
                act.wait_ge(t_ready, n)
                nc.scalar.activation(zT[:, :, :], bT[par][0:EC, 0:2 * SEQ].rearrange("p (k s) -> p k s", k=2),
                                     ACT.Copy).then_inc(t_used, 1)

            def values(b):
                act.wait_ge(z_ready, 2 * (b + 1))
                if not is0(b):
                    act.wait_ge(e_ready, 4 * b)
                nc.scalar.activation(vA[:], zA[:], ACT.Copy).then_inc(v_ready, 1)
                nc.scalar.activation(vB[:], zB[:], ACT.Copy).then_inc(v_ready, 1)

            def exps(b):
                for r in range(SPR):
                    act.wait_ge(max_ready, SPR * b + r + 1)
                    bank = bS[r % 2]
                    if r < 3:
                        for j in range(4):
                            h = 4 * r + j
                            last = nc.scalar.activation(PA[:, h, :], bank[:, j * SA:(j + 1) * SA], ACT.Exp,
                                                        bias=negmax[:, h:h + 1], accum_out=lsum[:, h:h + 1])
                    else:
                        for j in range(2):
                            q = 2 * (r - 3) + j
                            last = nc.scalar.activation(PB[:, q, :], bank[0:HB * SB, j * SEQ:(j + 1) * SEQ], ACT.Exp,
                                                        bias=negmax[0:HB * SB, 12 + q:13 + q],
                                                        accum_out=lsum[0:HB * SB, 12 + q:13 + q])
                    last.then_inc(exp_ready, 1)

            def attn_copies(b, n, par):
                def t_copy(q):
                    act.wait_ge(t_ready, n + q + 1)
                    bank = bT[(par + q) % 2]
                    if q < 3:
                        dst, src = PTA[:, 4 * q:4 * q + 4, :], bank[:, 0:4 * SA].rearrange("p (h s) -> p h s", h=4)
                    elif q == 3:
                        dst, src = PTB0[:, :, :], bank[:, 0:HEADS * SB].rearrange("p (h s) -> p h s", h=HEADS)
                    else:
                        dst, src = PTB1[:, :, :], bank[0:SB, 0:HEADS * SB].rearrange("p (h s) -> p h s", h=HEADS)
                    nc.scalar.activation(dst, src, ACT.Copy).then_inc(t_used, 1)

                def o_copy(g):
                    act.wait_ge(o_ready, 4 * b + g + 1)
                    if g < 3:
                        dst, src = oTA[:, 4 * g:4 * g + 4, :], bO[g % 2][:, 0:4 * SA].rearrange("p (h s) -> p h s", h=4)
                    else:
                        dst, src = oTB[:, 0:HEADS, ds(b * SB, SB)], bO[1][:, 0:HEADS * SB].rearrange("p (h s) -> p h s", h=HEADS)
                    nc.scalar.activation(dst, src, ACT.Copy, scale=lncol[:, 0:1]).then_inc(o_used, 1)

                t_copy(0)
                t_copy(1)
                o_copy(0)
                t_copy(2)
                o_copy(1)
                t_copy(3)
                o_copy(2)
                t_copy(4)
                o_copy(3)

            zt_copy(1, 0)
            values(0)
            exps(0)
            def iteration(b):
                zt_copy(TPB * b + 2, 1)
                attn_copies(b, TPB * b + 2, 0)
                values(b + 1)
                exps(b + 1)

            iteration(0)
            with act.Fori(1, NBATCH - 1) as b:
                iteration(b)
            attn_copies(NBATCH - 1, TPB * (NBATCH - 1) + 1, 1)

            for g in range(3):
                m = min(4, SLOTS - 4 * g)
                for k in range(2):
                    act.wait_ge(nT_sum, 2 * g + k + 1)
                    bank = (bS, bT, bS)[g][k]
                    nc.scalar.activation(nT[:, k, 512 * g:512 * g + m * 128], bank[0:EC, 0:m * 128], ACT.Copy).then_inc(nT_ready, 1)
            act.wait_ge(le_ready, 1)
            nc.scalar.activation(w16[0][:, :, :], lg[:, :, :], ACT.Exp).then_inc(lx_ready, 1)
            act.wait_ge(zero_done, 96)
            act.wait_ge(tab_ready, 1)
            nb = act.value_load(nbI[0:1, :], min_val=1, max_val=MAXB)
            def block_step(b, p):
                act.wait_ge(h0_sum, b + 1)
                nc.scalar.activation(hT[:, 0:4, :], bO[0][:, :].rearrange("p (c n) -> p c n", c=4), ACT.Relu).then_inc(h0_ready, 1)
                act.wait_ge(y_ready, b + 1)
                act.dma_start(yd[ds(b * T, T), :], ysb[p]).then_inc(y_out[p], 16)

            block_step(0, 0)
            with act.If(1 < nb):
                block_step(1, 1)
            with act.Fori(1, MAXB // 2) as i:
                for p in range(2):
                    with act.If(i * 2 + p < nb):
                        block_step(i * 2 + p, p)

        @block.vector
        def _(dve):
            chain = [0]

            def link(ins):
                chain[0] += 1
                ins.then_inc(dve_step, 1)
                dve.wait_ge(dve_step, chain[0])

            def newton(x, y, t):
                link(nc.vector.tensor_tensor(t, y, y, ALU.mult))
                link(nc.vector.tensor_tensor(t, t, x, ALU.mult))
                link(nc.vector.tensor_scalar(t, t, -0.5, 1.5, ALU.mult, ALU.add))
                link(nc.vector.tensor_tensor(y, y, t, ALU.mult))

            accf = acc[:, :, :].rearrange("p r e -> p (r e)")
            HALF = WR * EMB // 2
            nc.vector.memset(accf, 0.0)
            nc.vector.memset(one[:], 1.0)
            nc.vector.memset(mv[:, :, :, :].rearrange("p a b c -> p (a b c)"), 1.0)
            link(nc.vector.memset(H[BP:128, NBATCH:SLOTS, :], 0.0))
            dve.wait_ge(small_in, 16 * 7)
            link(nc.vector.tensor_tensor(posb, posb, pbb, ALU.add))
            link(nc.vector.tensor_tensor(w2[:, :, :], w2[:, :, :], ln96[:, :].unsqueeze(2).to_broadcast([EC, 2, HEADS]), ALU.mult))
            link(nc.vector.tensor_tensor(w2[:, :, :], w2[:, :, :], w2[:, :, :], ALU.mult))
            nc.vector.tensor_scalar(w2[:, :, :], w2[:, :, :], float(EMB) ** -0.5, None, ALU.mult).then_inc(w2_ready, 1)
            dve.wait_ge(txt_in, 48)
            for b in range(NBATCH):
                nc.vector.bn_stats(st6[0:SB, 1, b, :], hB[:, b, :])
            for j in range(4):
                dve.wait_ge(tok_ready, j + 1)
                bank = (bT[0], bT[1], bS[0], bS[1])[j]
                link(nc.vector.tensor_tensor(H[0:IMG, 2 * j:2 * j + 2, :],
                                             bank[0:IMG, 0:2 * EMB].rearrange("p (b e) -> p b e", b=2),
                                             posb.unsqueeze(1).to_broadcast([IMG, 2, EMB]), ALU.add))
                nc.vector.bn_stats(st6[:, 0, 2 * j, :], H[:, 2 * j, :])
                last = nc.vector.bn_stats(st6[:, 0, 2 * j + 1, :], H[:, 2 * j + 1, :])
            link(last)
            for b in range(NBATCH):
                nc.vector.bn_aggr(mv[:, 0, b, :], st6[:, 0, b, :])
                last = nc.vector.bn_aggr(mv[0:SB, 1, b, :], st6[0:SB, 1, b, :])
            link(last)
            eps = 1e-5
            nc.vector.tensor_scalar(nmr[:, :, :], mv[:, :, :, 1], 1.0 + eps, eps * eps, ALU.mult, ALU.add).then_inc(var_ready, 1)
            dve.wait_ge(pow_ready, 1)
            newton(nmr[:, :, :], rstd[:, :, :], mv[:, :, :, 1])
            link(nc.vector.tensor_scalar(nmr[:, :, :], mv[:, :, :, 0], -1.0, None, ALU.mult))
            link(nc.vector.tensor_tensor(nmr[:, :, :], nmr[:, :, :], rstd[:, :, :], ALU.mult))

            def z(b):
                nc.vector.tensor_scalar(zA[:, :], H[:, ds(b, 1), :].rearrange("p b e -> p (b e)"), rstd[:, 0, ds(b, 1)],
                                        nmr[:, 0, ds(b, 1)], ALU.mult, ALU.add).then_inc(z_ready, 1)
                nc.vector.tensor_scalar(zB[:, :], hB[:, ds(b, 1), :].rearrange("p b e -> p (b e)"), rstd[0:SB, 1, ds(b, 1)],
                                        nmr[0:SB, 1, ds(b, 1)], ALU.mult, ALU.add).then_inc(z_ready, 1)

            def row_max(b, r):
                dve.wait_ge(score_ready, SPR * b + r + 1)
                if r < 3:
                    nc.vector.tensor_reduce(negmax[:, 4 * r:4 * r + 4], bS[r % 2][:, :].rearrange("p (h s) -> p h s", h=4),
                                            X, ALU.max, negate=True).then_inc(max_ready, 1)
                else:
                    q = 12 + 2 * (r - 3)
                    nc.vector.tensor_reduce(negmax[0:HB * SB, q:q + 2], bS[r % 2][0:HB * SB, 0:2 * SEQ].rearrange("p (h s) -> p h s", h=2),
                                            X, ALU.max, negate=True).then_inc(max_ready, 1)

            def row_factor(b, r):
                dve.wait_ge(exp_ready, SPR * b + r + 1)
                n, q0, q1, c = (128, 4 * r, 4 * r + 4, C_NA) if r < 3 else (HB * SB, 6 + 2 * r, 8 + 2 * r, C_NB)
                nc.vector.reciprocal(rinv[0:n, q0:q1], lsum[0:n, q0:q1]).then_inc(rinv_ready, 1)
                dve.wait_ge(rinv_ready, SPR * b + r + 1)
                nc.vector.tensor_scalar(rn[0:n, q0:q1], rinv[0:n, q0:q1], cst[0:n, c:c + 1], None, ALU.mult).then_inc(rn_ready, 1)

            def e_copy(b, g):
                dve.wait_ge(e_ready, 4 * b + g + 1)
                if g < 3:
                    dst, src = oTA[:, HEADS + 2 * g:HEADS + 2 * g + 2, :], bE[:, 0:2 * SA].rearrange("p (h s) -> p h s", h=2)
                else:
                    dst, src = oTB[:, HEADS:WCH, ds(b * SB, SB)], bE[:, 0:6 * SB].rearrange("p (h s) -> p h s", h=6)
                nc.vector.tensor_scalar(dst, src, lncol[:, 1:2], None, ALU.mult).then_inc(e_used, 1)

            def wte_add(b, k):
                s, h = k // 2, k % 2
                if h == 0:
                    dve.wait_ge(wte_in[s], 16 * (b + 1))
                if k or not is0(b):
                    dve.wait_ge(wte_added, 2 * WBUF * b + k)
                part = slice(h * HALF, (h + 1) * HALF)
                nc.vector.tensor_tensor(accf[:, part], accf[:, part], wchunk[s][:, part], ALU.add).then_inc(wte_added, 1)

            def residual(b):
                dve.wait_ge(j_ready, b + 1)
                row = H[:, ds(b, 1), :].rearrange("p b e -> p (b e)")
                nc.vector.tensor_tensor(row, bJ[:, 0:EMB], row, ALU.add).then_inc(j_used, 1)

            z(0)
            row_max(0, 0)
            for r in range(1, SPR):
                row_max(0, r)
                row_factor(0, r - 1)
            row_factor(0, SPR - 1)
            dve.wait_ge(v_ready, 2)
            dve.wait_ge(t_ready, 1)
            z(1)

            def iteration(b, more):
                wte_add(b, 0)
                e_copy(b, 0)
                wte_add(b, 1)
                e_copy(b, 1)
                wte_add(b, 2)
                e_copy(b, 2)
                wte_add(b, 3)
                e_copy(b, 3)
                row_max(b + 1, 0)
                wte_add(b, 4)
                row_max(b + 1, 1)
                row_factor(b + 1, 0)
                wte_add(b, 5)
                row_max(b + 1, 2)
                row_factor(b + 1, 1)
                if more:
                    dve.wait_ge(v_ready, 2 * (b + 2))
                    dve.wait_ge(t_ready, TPB * b + 2)
                    z(b + 2)
                row_max(b + 1, 3)
                row_factor(b + 1, 2)
                wte_add(b, 6)
                row_max(b + 1, 4)
                row_factor(b + 1, 3)
                wte_add(b, 7)
                row_factor(b + 1, 4)
                residual(b)

            iteration(0, True)
            with dve.Fori(1, NBATCH - 2) as b:
                iteration(b, True)
            iteration(NBATCH - 2, False)
            dve.wait_ge(wte_added, 2 * WCHUNKS)
            link(nc.vector.tensor_reduce(wsum[:, :], acc[:, :, :].rearrange("p r e -> p e r"), X, ALU.add))
            dve.wait_ge(wtail_in, 16)
            nc.vector.tensor_tensor(wsum[0:WTAIL, :], wsum[0:WTAIL, :], wtail[:, :], ALU.add).then_inc(acc_ready, 1)
            b = NBATCH - 1
            e_copy(b, 0)
            e_copy(b, 1)
            e_copy(b, 2)
            e_copy(b, 3)
            dve.wait_ge(wo_in, 16)
            nc.vector.tensor_reduce(ws[:, 0, :], wo_sb[:, 0:HEADS, :].rearrange("p h e -> p e h"), X, ALU.add)
            nc.vector.tensor_reduce(ws[:, 1, :], wo_sb[:, HEADS:WCH, :].rearrange("p h e -> p e h"), X, ALU.add)
            dve.wait_ge(avg_sum, 1)
            nc.vector.tensor_scalar(avg[:, :], bE[:, 0:2], 1.0 / VOCAB, None, ALU.mult).then_inc(avg_ready, 1)
            residual(b)
            dve.wait_ge(jb_ready, 1)
            nc.vector.tensor_tensor(H[0:BP, NBATCH:NBATCH + 2, :], bO[0][0:BP, 0:2 * EMB].rearrange("p (j e) -> p j e", j=2),
                                    H[0:BP, NBATCH:NBATCH + 2, :], ALU.add)
            link(nc.vector.tensor_tensor(H[0:BP, NBATCH + 2, :], bO[1][0:BP, 0:EMB], H[0:BP, NBATCH + 2, :], ALU.add))
            dve.wait_ge(c_ready, 1)
            link(nc.vector.tensor_scalar(cN[:, :], bS[1][:, 0:EMB], cst[:, C_NA:C_NA + 1], -1.0, ALU.mult, ALU.mult))
            nc.vector.tensor_tensor(H[:, 0:NBATCH, :], H[:, 0:NBATCH, :], cN[:, :].unsqueeze(1).to_broadcast([128, NBATCH, EMB]), ALU.add)
            for i in range(NBT):
                j = NBATCH + i
                last = nc.vector.scalar_tensor_tensor(H[0:BP, j, :], bS[1][0:BP, 0:EMB], cst[0:BP, C_NBP + i:C_NBP + i + 1],
                                                      H[0:BP, j, :], ALU.mult, ALU.add)
            link(last)
            for j in range(SLOTS):
                last = nc.vector.bn_stats(fst[:, j, :], H[:, j, :])
            link(last)
            for j in range(SLOTS):
                last = nc.vector.bn_aggr(fmv[:, j, :], fst[:, j, :])
            link(last)
            link(nc.vector.tensor_scalar(sm[:, 0, :], fmv[:, :, 1], 1e-5, None, ALU.add))
            link(nc.vector.reciprocal(sm[:, 1, :], sm[:, 0, :]))
            link(nc.vector.tensor_tensor(sm[:, 1, :], sm[:, 1, :], fmv[:, :, 1], ALU.mult))
            nc.vector.tensor_scalar(sm[:, 1, :], sm[:, 1, :], 1e-6, None, ALU.add).then_inc(var_ready, 1)
            dve.wait_ge(pow_ready, 2)
            newton(sm[:, 0:2, :], sm[:, 2:4, :], sm[:, 4:6, :])
            for j in range(SLOTS):
                link(nc.vector.tensor_scalar(base[:, j, :], H[:, j, :], fmv[:, j, 0:1], sm[:, 2, j:j + 1], ALU.subtract, ALU.mult))
                nc.vector.scalar_tensor_tensor(norm[:, j, :], base[:, j, :], sm[:, 3, j:j + 1], flnb[:, :], ALU.mult, ALU.mult).then_inc(norm_ready, 1)
            dve.wait_ge(norm_ready, SLOTS)
            link(nc.vector.tensor_tensor(base, base, H[:, :, :], ALU.add))
            dve.wait_ge(lg_ready, 1)
            logits = bJ[:, 0:SLOTS * EXP].rearrange("p (j x) -> p j x", j=SLOTS)
            bc = [128, SLOTS, EXP]
            em = cst[:, C_EM:C_EM + EXP].unsqueeze(1).to_broadcast(bc)
            link(nc.vector.tensor_reduce(sm[:, 6, :], logits, X, ALU.max))
            nc.vector.tensor_tensor(lg[:, :, :], logits, sm[:, 6, :].unsqueeze(2).to_broadcast(bc), ALU.subtract).then_inc(le_ready, 1)
            dve.wait_ge(le_ready, 1)
            link(nc.vector.scalar_tensor_tensor(w16[1][:, :, :], lg[:, :, :], 0.0, em, ALU.is_ge, ALU.mult))
            link(nc.vector.tensor_reduce(sm[:, 7, :], w16[1][:, :, :], X, ALU.min))
            link(nc.vector.tensor_tensor(w16[1][:, :, :], em, sm[:, 7, :].unsqueeze(2).to_broadcast(bc), ALU.is_equal))
            nc.vector.tensor_tensor(oh[:, :, :], w16[1][:, :, :], cst[:, C_VAL:C_VAL + SLOTS].unsqueeze(2).to_broadcast(bc),
                                    ALU.mult).then_inc(oh_ready, 1)
            dve.wait_ge(oh_ready, 1)
            dve.wait_ge(lx_ready, 1)
            link(nc.vector.tensor_reduce(sm[:, 8, :], w16[0][:, :, :], X, ALU.add))
            link(nc.vector.reciprocal(sm[:, 9, :], sm[:, 8, :]))
            dve.wait_ge(rank_ready, 1)
            nc.vector.scalar_tensor_tensor(kp[:, :, :], bT[0][:, 0:SLOTS * EXP].rearrange("p (j x) -> p j x", j=SLOTS),
                                           float(CAP), oh[:, :, :], ALU.is_lt, ALU.mult).then_inc(kp_ready, 1)
            dve.wait_ge(kp_ready, 1)
            link(nc.vector.tensor_reduce(sm[:, 10, :], kp[:, :, :], X, ALU.add))
            link(nc.vector.tensor_scalar(sm[:, 11, :], sm[:, 10, :], -1.0, 1.0, ALU.mult, ALU.add))
            link(nc.vector.tensor_tensor(sm[:, 12, :], sm[:, 11, :], cst[:, C_TR:C_TR + SLOTS], ALU.mult))
            dve.wait_ge(grank_ready, 1)
            cnt = bT[1][:, SLOTS * EXP:(SLOTS + 1) * EXP]
            link(nc.vector.tensor_scalar(nexi[:, 0, :], cnt, float(T - 1), None, ALU.add))
            link(nc.vector.tensor_scalar(nexi[:, 1, :], nexi[:, 0, :], T.bit_length() - 1, None, ALU.logical_shift_right))
            link(nc.vector.tensor_copy(nexp[:, 0, :], nexi[:, 1, :]))
            link(nc.vector.memset(nexp[:, 3, :], 1.0))
            link(nc.vector.tensor_tensor_scan(nexp[:, 1, :], nexp[:, 3, :], nexp[:, 0, :], 0.0, ALU.mult, ALU.add))
            link(nc.vector.tensor_tensor(nexp[:, 2, :], nexp[:, 1, :], nexp[:, 0, :], ALU.subtract))
            link(nc.vector.tensor_scalar(nexp[:, 2, :], nexp[:, 2, :], float(T), None, ALU.mult))
            link(nc.vector.tensor_tensor(w16[2][:, :, :], bT[1][:, 0:SLOTS * EXP].rearrange("p (j x) -> p j x", j=SLOTS),
                                         nexp[:, 2, :].unsqueeze(1).to_broadcast(bc), ALU.add))
            link(nc.vector.tensor_tensor(w16[2][:, :, :], w16[2][:, :, :], kp[:, :, :], ALU.mult))
            link(nc.vector.tensor_reduce(sm[:, 13, :], w16[2][:, :, :], X, ALU.add))
            nc.vector.tensor_copy(gI[:, :], sm[:, 13, :])
            nc.vector.tensor_tensor(posI[:, :], sm[:, 13, :], sm[:, 12, :], ALU.add).then_inc(pos_ready, 1)
            bb = [1, MAXB, EXP]
            link(nc.vector.tensor_tensor(bex[0:1, :, :], nexp[0:1, 1, :].unsqueeze(1).to_broadcast(bb),
                                         cst[0:1, C_BI:C_BI + MAXB].unsqueeze(2).to_broadcast(bb), ALU.is_le))
            link(nc.vector.tensor_reduce(beF[0:1, :], bex[0:1, :, :], X, ALU.add))
            nc.vector.tensor_scalar(beI[0:1, 0:MAXB], beF[0:1, :], float(EXP - 1), None, ALU.min)
            nc.vector.tensor_copy(nbI[0:1, :], nexp[0:1, 1, EXP - 1:EXP]).then_inc(tab_ready, 1)
            link(nc.vector.tensor_tensor(sm[:, 14, :], sm[:, 9, :], sm[:, 10, :], ALU.mult))
            link(nc.vector.tensor_tensor(sm[:, 15, :], sm[:, 9, :], sm[:, 11, :], ALU.mult))
            for j in range(SLOTS):
                last = nc.vector.scalar_tensor_tensor(base[:, j, :], norm[:, j, :], sm[:, 15, j:j + 1], base[:, j, :], ALU.mult, ALU.add)
            last.then_inc(base_ready, 1)

            dve.wait_ge(tab_ready, 1)
            nb = dve.value_load(nbI[0:1, :], min_val=1, max_val=MAXB)

            def xt_copy(b):
                dve.wait_ge(xT_sum, b + 1)
                nc.vector.tensor_copy(xT, bT[0][0:EC, 0:2 * T].rearrange("p (k n) -> p k n", k=2)).then_inc(xT_ready, 1)

            xt_copy(0)
            def block_step(i, p):
                b = i * 2 + p
                dve.wait_ge(h1_sum, b + 1)
                nc.vector.tensor_scalar(hT[:, 4:6, :], bO[1][:, 0:2 * T].rearrange("p (c n) -> p c n", c=2), 0.0, None,
                                        ALU.max).then_inc(h1_ready, 1)
                xt_copy(b + 1)
                dve.wait_ge(y_sum, b + 1)
                if not is0(i):
                    dve.wait_ge(y_out[p], i * 16)
                nc.vector.tensor_copy(ysb[p], bE[:, 0:EMB]).then_inc(y_ready, 1)

            block_step(0, 0)
            with dve.If(1 < nb):
                block_step(0, 1)
            with dve.Fori(1, MAXB // 2) as i:
                for p in range(2):
                    with dve.If(i * 2 + p < nb):
                        block_step(i, p)
            for j in range(SLOTS):
                dve.wait_ge(got[j], 16)
                n = 128 if j < NBATCH else BP
                nc.vector.scalar_tensor_tensor(yg[0:n, j, :], yg[0:n, j, :], sm[0:n, 14, j:j + 1], base[0:n, j, :],
                                               ALU.mult, ALU.add).then_inc(res_ready, 1)

        @block.tensor
        def _(pe):
            def mm(o, l, r, start=True, stop=True):
                return nc.tensor.matmul(o, l, r, start=start, stop=stop, skip_group_check=True)

            pe.wait_ge(pat_in, 32)
            for k2 in range(2):
                for k in range(6):
                    last = mm(bO[k2][0:EC, 0:NBATCH * IMG], pw_sb[:, k, k2 * EC:(k2 + 1) * EC], pat_sb[:, k, :], k == 0, k == 5)
                last.then_inc(emb_ready, 1)
            pe.wait_ge(cst_in, 16)
            pe.wait_ge(embT_ready, 2)
            for j in range(4):
                bank = (bT[0], bT[1], bS[0], bS[1])[j]
                for c in range(4):
                    b, k = 2 * j + c // 2, c % 2
                    last = nc.tensor.transpose(bank[0:IMG, c * EC:(c + 1) * EC], embT[:, k, b * IMG:(b + 1) * IMG], ident[0:EC, 0:EC])
                last.then_inc(tok_ready, 1)

            idb, HS = mat[:, M_ID, :], HB * SB
            maskA = mat[:, M_MA, :].unsqueeze(1).to_broadcast([128, 4, SA])
            maskB = mat[:, M_MB:M_MB + 2, :].rearrange("p a s -> p (a s)")[0:HS, 0:SEQ].unsqueeze(1).to_broadcast([HS, 2, SEQ])

            def z_transpose(b, par):
                pe.wait_ge(z_ready, 2 * (b + 1))
                pe.wait_ge(cst_in, 16)
                for k in range(2):
                    nc.tensor.transpose(bT[par][0:EC, k * SEQ:k * SEQ + SA], zA[:, k * EC:(k + 1) * EC], ident)
                    last = nc.tensor.transpose(bT[par][0:EC, k * SEQ + SA:(k + 1) * SEQ], zB[:, k * EC:(k + 1) * EC], ident[0:SB, 0:SB])
                last.then_inc(t_ready, 1)

            def score(b, r, first=False):
                bank = bS[r % 2]
                pe.wait_ge(aw_ready, 8 * b + min(2 * r + 2, 8))
                if not first:
                    pe.wait_ge(exp_ready, SPR * b + max(r - 1, 0))
                if r < 3:
                    mm(bank[:, :].rearrange("p (h s) -> p h s", h=4), idb, maskA, True, False)
                    for j in range(4):
                        for k in range(2):
                            last = mm(bank[:, j * SA:(j + 1) * SA], AwA[:, k, 4 * r + j, :], zT[:, k, 0:SA], False, k == 1)
                else:
                    mm(bank[0:HS, 0:2 * SEQ].rearrange("p (h s) -> p h s", h=2), idb[0:HS, 0:HS], maskB, True, False)
                    for j in range(2):
                        q = 2 * (r - 3) + j
                        for k in range(2):
                            last = mm(bank[0:HS, j * SEQ:(j + 1) * SEQ], AwB[:, k, HB * q:HB * (q + 1), :].rearrange("p h s -> p (h s)"), zT[:, k, :], False, k == 1)
                last.then_inc(score_ready, 1)

            def p_transpose(b, q, n, par):
                if q < 4:
                    pe.wait_ge(p_ready, SPR * b + (q + 1 if q < 3 else SPR))
                    pe.wait_ge(t_used, n + q - 1)
                bank = bT[(par + q) % 2]
                if q < 3:
                    for j in range(4):
                        last = nc.tensor.transpose(bank[:, j * SA:(j + 1) * SA], PA[:, 4 * q + j, :], ident)
                else:
                    for g in range(NG):
                        if q == 3:
                            last = nc.tensor.transpose(bank[:, g * HS:(g + 1) * HS], PB[:, g, 0:SA], ident[0:HS, 0:HS])
                        else:
                            last = nc.tensor.transpose(bank[0:SB, g * HS:(g + 1) * HS], PB[:, g, SA:SEQ], ident[0:HS, 0:HS])
                last.then_inc(t_ready, 1)

            def value(b, g, n):
                if g == 0:
                    pe.wait_ge(v_ready, 2 * (b + 1))
                    if not is0(b):
                        pe.wait_ge(o_used, 4 * b)
                elif g > 1:
                    pe.wait_ge(o_used, 4 * b + g - 1)
                pe.wait_ge(t_used, n + (g + 1 if g < 3 else 5))
                o = bO[g % 2]
                if g < 3:
                    mm(o[:, :].rearrange("p (h s) -> p h s", h=4), vA[:, 0:E0], PTA[:, 4 * g:4 * g + 4, :]).then_inc(o_ready, 1)
                else:
                    oo = o[:, 0:HEADS * SB].rearrange("p (h s) -> p h s", h=HEADS)
                    mm(oo, vA[:, 0:E0], PTB0[:, :, :], True, False)
                    mm(oo, vB[:, 0:E0], PTB1[:, :, :], False, True).then_inc(o_ready, 1)
                if g or not is0(b):
                    pe.wait_ge(e_used, 4 * b + g)
                for odd in range(2):
                    part = slice(odd * E1, (odd + 1) * E1)
                    if g < 3:
                        last = mm(bE[part, 0:2 * SA].rearrange("p (h s) -> p h s", h=2), vA[:, E0:EMB], PTA[:, 4 * g + odd:4 * g + 4:2, :])
                    else:
                        ee = bE[part, 0:6 * SB].rearrange("p (h s) -> p h s", h=6)
                        mm(ee, vA[:, E0:EMB], PTB0[:, odd:HEADS:2, :], True, False)
                        last = mm(ee, vB[:, E0:EMB], PTB1[:, odd:HEADS:2, :], False, True)
                last.then_inc(e_ready, 1)

            def attend(b, n, par):
                p_transpose(b, 0, n, par)
                p_transpose(b, 1, n, par)
                value(b, 0, n)
                p_transpose(b, 2, n, par)
                value(b, 1, n)
                p_transpose(b, 3, n, par)
                value(b, 2, n)
                p_transpose(b, 4, n, par)
                value(b, 3, n)

            def project(b, c0, c1):
                if c0 == 0:
                    pe.wait_ge(wo_in, 16)
                    if not is0(b):
                        pe.wait_ge(j_used, b)
                    pe.wait_ge(o_used, 4 * b + 3)
                    pe.wait_ge(e_used, 4 * b + 3)
                for c in range(c0, c1):
                    last = mm(bJ[:, 0:EMB], oTA[:, c, :], wo_sb[:, c, :], c == 0, c == WCH - 1)
                if c1 == WCH:
                    last.then_inc(j_ready, 1)

            z_transpose(0, 0)
            pe.wait_ge(mat_ready, 1)
            for r in range(SPR):
                score(0, r, r < 2)

            def iteration(b):
                n = TPB * b + 2
                z_transpose(b + 1, 1)
                attend(b, n, 0)
                pe.wait_ge(t_used, n)
                score(b + 1, 0)
                score(b + 1, 1)
                project(b, 0, 5)
                score(b + 1, 2)
                project(b, 5, 10)
                score(b + 1, 3)
                project(b, 10, 14)
                score(b + 1, 4)
                project(b, 14, WCH)

            iteration(0)
            with pe.Fori(1, NBATCH - 1) as b:
                iteration(b)
            attend(NBATCH - 1, TPB * (NBATCH - 1) + 1, 1)
            project(NBATCH - 1, 0, WCH)
            pe.wait_ge(o_used, 4 * NBATCH)
            pe.wait_ge(e_used, 4 * NBATCH)
            for i in range(NBT):
                for c in range(WCH):
                    last = mm(bO[i // 2][0:BP, (i % 2) * EMB:(i % 2 + 1) * EMB], oTB[:, c, i * BP:(i + 1) * BP], wo_sb[:, c, :],
                              c == 0, c == WCH - 1)
            last.then_inc(jb_ready, 1)
            pe.wait_ge(acc_ready, 1)
            mm(bE[:, 0:1], wsum[:, 0:E0], one[:, :])
            mm(bE[0:E1, 1:2], wsum[:, E0:EMB], one[:, :])
            mm(bE[E1:128, 1:2], wsum[:, E0:EMB], one[:, :]).then_inc(avg_sum, 1)
            pe.wait_ge(avg_ready, 1)
            for k in range(2):
                last = mm(bS[1][:, 0:EMB], avg[:, k:k + 1].to_broadcast([128, 128]), ws[:, k, :], k == 0, k == 1)
            last.then_inc(c_ready, 1)

            for g in range(3):
                m = min(4, SLOTS - 4 * g)
                for k in range(2):
                    bank = (bS, bT, bS)[g][k]
                    if g == 2:
                        pe.wait_ge(nT_ready, k + 1)
                    for j in range(m):
                        pe.wait_ge(norm_ready, 4 * g + j + 1)
                        last = nc.tensor.transpose(bank[0:EC, j * 128:(j + 1) * 128], norm[:, 4 * g + j, k * EC:(k + 1) * EC], ident)
                    last.then_inc(nT_sum, 1)
            for j in range(SLOTS):
                pe.wait_ge(nT_ready, 2 * (j // 4) + 2)
                for k in range(2):
                    last = mm(bJ[:, j * EXP:(j + 1) * EXP], nT[:, k, j * 128:(j + 1) * 128], wr_sb[:, k, :], k == 0, k == 1)
            last.then_inc(lg_ready, 1)
            pe.wait_ge(oh_ready, 1)
            rk = bT[0]
            mm(rk[:, 0:NBATCH * EXP], mat[:, M_TRI, :], oh[:, 0:NBATCH, :].rearrange("p j x -> p (j x)"), True, False)
            for i in range(NBT):
                o = rk[0:BP, (NBATCH + i) * EXP:(NBATCH + i + 1) * EXP]
                mm(o, mat[:, M_BB + i, 0:BP], oh[:, NBATCH + i, :], False, False)
                if i:
                    mm(o, mat[:, M_BX + i - 1, 0:BP], oh[:, NBATCH + i - 1, :], False, False)
                for m, (ii, b) in enumerate(PAIRS):
                    if ii == i:
                        last = mm(o, mat[:, M_BA + m, 0:BP], oh[:, b, :], False, (i, b) == PAIRS[-1])
            last.then_inc(rank_ready, 1)
            pe.wait_ge(kp_ready, 1)
            gk = bT[1]
            kf = kp[:, :, :].rearrange("p j x -> p (j x)")
            mm(gk[:, 0:SLOTS * EXP], mat[:, M_TRI, :], kf, True, False)
            for d in range(1, SLOTS):
                mm(gk[:, d * EXP:SLOTS * EXP], mat[:, M_ONE, :], kf[:, 0:(SLOTS - d) * EXP], False, False)
            for j in range(SLOTS):
                last = mm(gk[:, SLOTS * EXP:(SLOTS + 1) * EXP], mat[:, M_ONE, :], kp[:, j, :], False, j == SLOTS - 1)
            last.then_inc(grank_ready, 1)

            pe.wait_ge(tab_ready, 1)
            nb = pe.value_load(nbI[0:1, :], min_val=1, max_val=MAXB)

            def x_transpose(p, at):
                pe.wait_ge(x_in[p], at)
                for k in range(2):
                    last = nc.tensor.transpose(bT[0][0:EC, k * T:(k + 1) * T], xb[p][:, k * EC:(k + 1) * EC], ident)
                last.then_inc(xT_sum, 1)

            x_transpose(0, 16)
            def block_step(i, p):
                b = i * 2 + p
                pe.wait_ge(xT_ready, b + 1)
                pe.wait_ge(wi_in[p], i * 16 + 16)
                for c in range(FC):
                    bank, cc = (bO[0], c) if c < 4 else (bO[1], c - 4)
                    for k in range(2):
                        last = mm(bank[:, cc * T:(cc + 1) * T], wi_sb[p][:, k, c, :], xT[:, k, :], k == 0, k == 1)
                    if c == 3:
                        last.then_inc(h0_sum, 1)
                last.then_inc(h1_sum, 1)
                x_transpose(1 - p, i * 16 + 16 * (1 + p))
                pe.wait_ge(wox_in[p], i * 16 + 16)
                pe.wait_ge(h0_ready, b + 1)
                if not is0(b):
                    pe.wait_ge(y_ready, b)
                for c in range(FC):
                    if c == 4:
                        pe.wait_ge(h1_ready, b + 1)
                    last = mm(bE[:, 0:EMB], hT[:, c, :], wo_x[p][:, c, :], c == 0, c == FC - 1)
                last.then_inc(y_sum, 1)

            block_step(0, 0)
            with pe.If(1 < nb):
                block_step(0, 1)
            with pe.Fori(1, MAXB // 2) as i:
                for p in range(2):
                    with pe.If(i * 2 + p < nb):
                        block_step(i, p)


def constants():
    p = np.arange(128)
    c = np.zeros((128, NCST), np.float32)
    c[:, C_ID:C_ID + 128] = np.eye(128)
    c[:, C_NA] = 1.0 / (p + 1)
    c[:, C_NB] = 1.0 / (SA + p % SB + 1)
    for i in range(NBT):
        c[:, C_NBP + i] = -1.0 / (SA + (i * BP + p) % SB + 1)
    c[:, C_EM:C_EM + EXP] = np.arange(EXP) - EXP
    for j in range(SLOTS):
        c[:, C_VAL + j] = (p < (128 if j < NBATCH else BP))
        c[:, C_TR + j] = TRASH + j * 128 + p
    c[:, C_BI:C_BI + MAXB] = np.arange(MAXB)
    m = np.zeros((128, NMAT, 128), np.float32)
    m[:, M_ID] = np.eye(128)
    m[:, M_ONE] = 1
    m[:, M_TRI] = p[:, None] < p[None, :]
    m[:, M_MA] = np.where(p[None, :] > p[:, None], NEG, 0)
    t = np.arange(256)
    m[:, M_MB:M_MB + 2] = np.where(t[None, :] > SA + p[:, None] % SB, NEG, 0).reshape(128, 2, 128)

    def batch(i):
        return np.where(p < BP, (i * BP + p) // SB, -1 - i)
    for i in range(NBT):
        same = batch(i)[:, None] == batch(i)[None, :]
        m[:, M_BB + i] = same & (p[:, None] < p[None, :]) & (p[:, None] < BP)
        if i:
            m[:, M_BX + i - 1] = batch(i - 1)[:, None] == batch(i)[None, :]
    for n, (i, b) in enumerate(PAIRS):
        m[:, M_BA + n] = (batch(i) == b)[None, :]
    return c, m.reshape(128, NMAT * 128)


def kernel(**inputs):
    import concourse.bacc as bacc
    from concourse.bass_utils import run_bass_kernel_spmd as run

    a = {k: np.asarray(v) for k, v in inputs.items()}
    con = np.ascontiguousarray
    P, G = 16, 6
    x = a["x"].reshape(NBATCH, 3, G, P, G, P).transpose(0, 1, 3, 5, 2, 4).reshape(NBATCH, IMG, 768)
    pat = con(x.reshape(NBATCH * IMG, 6, 128).transpose(2, 1, 0))
    projw = con(a["L0_tok_proj_w"].reshape(EMB, 6, 128).transpose(2, 1, 0))
    txt, cut = a["txt"], SA - IMG
    tail = txt[:, cut:]
    ln = a["L0_attn_ln_w"]
    wo4 = a["L0_attn_W_o"].reshape(EMB, HEADS, EMB).transpose(1, 2, 0)
    wo_attn = np.concatenate([wo4[:, :E0], wo4[:, E0:].reshape(HEADS // 2, 128, EMB)], 0).transpose(1, 0, 2)
    cst, mat = constants()
    arrays = {
        "patches": pat, "projw": projw,
        "projb": con(np.broadcast_to(a["L0_tok_proj_b"], (IMG, EMB))), "pos": con(a["L0_tok_pos_embed"][0]),
        "txtA": con(txt[:, :cut].transpose(1, 0, 2)), "txtB": con(tail.transpose(1, 0, 2)),
        "txtBp": con(tail.reshape(NBT, BP, EMB).transpose(1, 0, 2)),
        "wqk": con(a["L0_attn_W_qk"].reshape(HEADS, 2, EC).transpose(2, 1, 0)),
        "lnw": con(ln.reshape(2, EC).T), "lnc": con(np.stack([ln[:E0], np.concatenate([ln[E0:], ln[E0:]])], 1)),
        "wte": a["L0_attn_wte"], "wo_attn": con(wo_attn),
        "flnw": con(np.broadcast_to(a["L0_ffn_ln_w"], (128, EMB))),
        "wrt": con(a["L0_ffn_w_router"].reshape(2, EC, EXP).transpose(1, 0, 2)),
        "wi": con(a["L0_ffn_wi"].reshape(EXP, 2, EC, FC, 128).transpose(0, 2, 1, 3, 4)),
        "wo": con(a["L0_ffn_wo"].reshape(EXP, FC, 128, EMB).transpose(0, 2, 1, 3)),
        "cst": cst, "mat": mat,
    }
    nc = bacc.Bacc("TRN2", target_bir_lowering=False, num_devices=1)
    args = [nc.dram_tensor("in_" + k, v.shape, mybir.dt.from_np(v.dtype), kind="ExternalInput").ap() for k, v in arrays.items()]
    out = nc.dram_tensor("out", (TOK, EMB), mybir.dt.float32, kind="ExternalOutput").ap()
    program(nc, *args, out)
    r = run(nc, [{"in_" + k: v for k, v in arrays.items()}], core_ids=[0])
    y = r.results[0]["out"]
    ya = y[:NBATCH * SA].reshape(NBATCH, SA, EMB)
    yb = y[NBATCH * SA:].reshape(NBATCH, SB, EMB)
    return np.concatenate([ya, yb], 1)
```

```python
import numpy as np
import concourse.bass as bass
from concourse import mybir
from contextlib import ExitStack

NBATCH, SEQ, EMB, HEADS = 8, 164, 192, 12
IMG = 36
SA = 128
SB = SEQ - SA
EC = 96
E0, E1 = 128, EMB - 128
HB = 3
NG = HEADS // HB
WCH = HEADS + HEADS // 2
NBT = 3
BP = NBATCH * SB // NBT
SLOTS = NBATCH + NBT
EXP, FF, CAP, T = 16, 768, 64, 128
FC = FF // 128
TOK = NBATCH * SEQ
MAXB = EXP + (TOK - EXP) // T
VOCAB = 50257
WR = 14
WCHUNKS = VOCAB // 128 // WR
WTAIL = VOCAB - 128 * WR * WCHUNKS
WBUF = 4
XBUF = 4
XROWS = (MAXB + 1) * T
D_X, D_BASE, D_RP, D_ROW, DW = 0, EMB, 2 * EMB, 2 * EMB + 1, 2 * EMB + 2
BIG = 1 << 20

C_ID, C_MA, C_MB, C_NA, C_NB, C_NBP = 0, 128, 256, 256 + SEQ, 257 + SEQ, 258 + SEQ
NCST = C_NBP + NBT
C_EM, C_ROW, C_BI = 0, EXP, EXP + SLOTS
C_MAT = C_BI + MAXB
PAIRS = [(i, b) for i in range(NBT) for b in range(NBATCH) if b * SB < (i + 1) * BP and (b + 1) * SB > i * BP]
M_TRI, M_BB, M_BX, M_BA = 0, 1, 4, 6
NMAT = M_BA + len(PAIRS)
NCST2 = C_MAT + NMAT * 128
NEG = -1e30
GROUPS = [(0, NBATCH - 1, 128), (NBATCH - 1, NBATCH, 128)] + [(NBATCH + i, NBATCH + i + 1, BP) for i in range(NBT)]


def program(nc, patches, projw, projb, pos, txtA, txtB, txtBp, wqk, lnw, lnc, wte, wo_attn,
            flnw, wrt, wi, wo, cst_d, cst2_d, out):
    f32, bf16, i32 = mybir.dt.float32, mybir.dt.bfloat16, mybir.dt.int32
    ALU, ACT = mybir.AluOpType, mybir.ActivationFunctionType
    X = mybir.AxisListType.X
    ds = bass.ds

    xd = nc.dram_tensor("dispatched", (XROWS + 3 * T, DW), f32).ap()

    ctx = ExitStack()
    with ctx:
        def sb(name, shape, dt=f32):
            return ctx.enter_context(nc.sbuf_tensor(name, shape, dt))

        def pb(name):
            return ctx.enter_context(nc.psum_tensor(name, [128, 512], f32))

        def sem(name):
            return ctx.enter_context(nc.semaphore(name))

        cst = sb("cst", [128, NCST])
        cst2 = sb("cst2", [128, C_MAT])
        mat = sb("mat", [128, NMAT, 128], bf16)
        idb, maskA, maskB = sb("idb", [128, 128], bf16), sb("maskA", [128, SA], bf16), sb("maskB", [128, SEQ], bf16)
        ones = sb("ones", [128, 128], bf16)
        ident = cst[:, C_ID:C_ID + 128]
        H = sb("H", [128, SLOTS, EMB])
        hB = sb("hB", [SB, NBATCH, EMB])
        wo_sb = sb("wo_sb", [128, WCH, EMB])
        ws = sb("ws", [128, 2, EMB])
        acc = sb("acc", [128, WR, EMB])
        lncol = sb("lncol", [128, 2])
        flnb = sb("flnb", [128, EMB])
        wr_sb = sb("wr_sb", [EC, 2, EXP])
        rstd = sb("rstd", [128, 2, NBATCH])
        nmr = sb("nmr", [128, 2, NBATCH])
        zA, zB = sb("zA", [128, EMB]), sb("zB", [SB, EMB])
        vA, vB = sb("vA", [128, EMB]), sb("vB", [SB, EMB])
        zT = sb("zT", [EC, 2, SEQ])
        w2 = sb("w2", [EC, 2, HEADS])
        Awf = sb("AwA", [128, 2 * HEADS * SA])
        AwA, AwB = Awf[0:EC, :].rearrange("p (k h s) -> p k h s", k=2, h=HEADS), sb("AwB", [EC, 2, HEADS, SB])
        PA, PB = sb("PA", [128, HEADS, SA]), sb("PB", [HB * SB, NG, SEQ])
        PTA = sb("PTA", [128, HEADS, SA])
        PTB0, PTB1 = sb("PTB0", [128, HEADS, SB]), sb("PTB1", [SB, HEADS, SB])
        negmax, lsum, rn = sb("negmax", [128, 16]), sb("lsum", [128, 16]), sb("rn", [128, 16])
        rinv = sb("rinv", [128, 16])
        oTA = sb("oTA", [128, WCH, SA])
        oTB = sb("oTB", [128, WCH, NBATCH * SB])
        wbuf = sb("wbuf", [128, WBUF * WR * EMB])
        wchunk = [wbuf[:, i * WR * EMB:(i + 1) * WR * EMB] for i in range(WBUF)]
        WIN, WON = 2 * FC * 128, FC * EMB
        wi_sb = [wbuf[0:EC, p * WIN:(p + 1) * WIN].rearrange("p (k c m) -> p k c m", k=2, c=FC) for p in range(2)]
        wo_x = [wbuf[:, 2 * WIN + p * WON:2 * WIN + (p + 1) * WON].rearrange("p (c e) -> p c e", c=FC) for p in range(2)]
        wtail = sb("wtail", [WTAIL, EMB])
        flat = oTB[:, :, :].rearrange("p c s -> p (c s)")
        pat_sb = flat[:, 0:6 * 288].rearrange("p (k n) -> p k n", k=6)
        pw_sb = flat[:, 1728:1728 + 6 * EMB].rearrange("p (k e) -> p k e", k=6)
        embT = flat[0:EC, 2880:2880 + 576].rearrange("p (k n) -> p k n", k=2)
        posb = flat[0:IMG, 3456:3456 + EMB]
        pbb = flat[0:IMG, 3648:3648 + EMB]
        st6 = sb("st6", [128, 2, NBATCH, 6])
        mv = sb("mv", [128, 2, NBATCH, 2])
        nT = Awf[0:EC, 0:2 * SLOTS * 128].rearrange("p (k n) -> p k n", k=2)
        paf = PA[:, :, :].rearrange("p h s -> p (h s)")
        pta = PTA[:, :, :].rearrange("p h s -> p (h s)")
        pay = sb("pay", [128, SLOTS, DW])
        mat32 = pay[:, :, :].rearrange("p j w -> p (j w)")[:, 0:NMAT * 128]
        norm, base = pay[:, :, D_X:D_X + EMB], pay[:, :, D_BASE:D_BASE + EMB]
        drow = flat[:, 0:SLOTS * EMB].rearrange("p (j e) -> p j e", j=SLOTS)
        xb = [oTA[:, :, :].rearrange("p c s -> p (c s)")[:, q * DW:(q + 1) * DW] for q in range(XBUF)]
        ysb = [paf[:, p * EMB:(p + 1) * EMB] for p in range(2)]
        yrow = [sb(f"yrow{p}", [128, 1], i32) for p in range(2)]
        xT = paf[0:EC, 2 * EMB:2 * EMB + 2 * T].rearrange("p (k n) -> p k n", k=2)
        hT = pta[:, 0:FC * T].rearrange("p (c n) -> p c n", c=FC)
        fst = sb("fst", [128, SLOTS, 6])
        fmv = sb("fmv", [128, SLOTS, 2])
        var = sb("var", [128, 2, SLOTS])
        rsq, nwt = sb("rsq", [128, 2, SLOTS]), sb("nwt", [128, 2, SLOTS])
        rsq1, nmb = sb("rsq1", [128, SLOTS]), sb("nmb", [128, SLOTS])
        lmax, lidx, lsm, kept, drop, posF, dropF = (sb(n, [128, SLOTS]) for n in
            ("lmax", "lidx", "lsm", "kept", "drop", "posF", "dropF"))
        lg, lx, l1, l2 = (sb(n, [128, SLOTS, EXP]) for n in ("lg", "lx", "l1", "l2"))
        oh, kp = sb("oh", [128, SLOTS, EXP], bf16), sb("kp", [128, SLOTS, EXP], bf16)
        capI, capF, cum, first = sb("capI", [128, 2, EXP], i32), sb("capF", [128, 2, EXP]), sb("cum", [128, 2, EXP]), sb("first", [128, 2, EXP])
        oneX = sb("oneX", [128, EXP])
        capB = sb("capB", [128, EXP])
        bex = sb("bex", [1, MAXB, 2, EXP])
        beF, beI = sb("beF", [1, MAXB]), sb("beI", [1, MAXB + 4], i32)
        nbI = sb("nbI", [1, 2], i32)
        posI, dropI = sb("posI", [128, SLOTS], i32), sb("dropI", [128, SLOTS], i32)
        avg = sb("avg", [128, 2])
        cS, cN = sb("cS", [128, EMB]), sb("cN", [128, EMB])
        zeros = sb("zeros", [128, 3, DW])
        ln96, one = sb("ln96", [EC, 2]), sb("one", [128, 1])
        mhalf = sb("mhalf", [128, 32])
        wsum = sb("wsum", [128, EMB])
        nwz = sb("nwz", [128, 2, NBATCH])

        bS = [pb("bS0"), pb("bS1")]
        bT = [pb("bT0"), pb("bT1")]
        bO = [pb("bO0"), pb("bO1")]
        bE = pb("bE")
        bJ = pb("bJ")

        cst_in, cst2_in, mat_in, pat_in, txt_in, small_in, late_in, wo_in = (sem(n) for n in
            ("cst_in", "cst2_in", "mat_in", "pat_in", "txt_in", "small_in", "late_in", "wo_in"))
        wte_in = [sem(f"wte_in{i}") for i in range(WBUF)]
        wtail_in, wte_added, dve_step, pool_step = (sem(n) for n in ("wtail_in", "wte_added", "dve_step", "pool_step"))
        emb_ready, embT_ready, tok_ready, tok_added = (sem(n) for n in ("emb_ready", "embT_ready", "tok_ready", "tok_added"))
        z_ready, v_ready, aw_ready, aw0_ready = sem("z_ready"), sem("v_ready"), sem("aw_ready"), sem("aw0_ready")
        bf_ready, mat_ready = sem("bf_ready"), sem("mat_ready")
        score_ready, max_ready, exp_ready, rn_ready, p_ready = (sem(n) for n in
            ("score_ready", "max_ready", "exp_ready", "rn_ready", "p_ready"))
        t_ready, t_used = sem("t_ready"), sem("t_used")
        o_ready, o_used, e_ready, e_used = (sem(n) for n in ("o_ready", "o_used", "e_ready", "e_used"))
        j_ready, j_used, jb_ready = sem("j_ready"), sem("j_used"), sem("jb_ready")
        acc_ready, avg_sum, avg_ready, c_ready, c_used = (sem(n) for n in ("acc_ready", "avg_sum", "avg_ready", "c_ready", "c_used"))
        rinv_ready, w2_ready = sem("rinv_ready"), sem("w2_ready")
        var_ready, pow_ready, basepar_ready, base_ready = (sem(n) for n in ("var_ready", "pow_ready", "basepar_ready", "base_ready"))
        norm_ready, nT_sum, nT_ready, lg_ready, le_ready, lx_ready = (sem(n) for n in
            ("norm_ready", "nT_sum", "nT_ready", "lg_ready", "le_ready", "lx_ready"))
        oh_ready, rank_ready, kp_ready, grank_ready, pos_ready, tab_ready = (sem(n) for n in
            ("oh_ready", "rank_ready", "kp_ready", "grank_ready", "pos_ready", "tab_ready"))
        ohz_ready, zero_ready, zero_done, scattered = sem("ohz_ready"), sem("zero_ready"), sem("zero_done"), sem("scattered")
        wi_in, wox_in = ([sem(f"{n}{p}") for p in range(2)] for n in ("wi_in", "wox_in"))
        x_in = [sem(f"x_in{q}") for q in range(XBUF)]
        xT_sum, xT_ready = sem("xT_sum"), sem("xT_ready")
        h0_sum, h1_sum, h0_ready, h1_ready, y_sum, y_ready = (sem(n) for n in
            ("h0_sum", "h1_sum", "h0_ready", "h1_ready", "y_sum", "y_ready"))
        y_out = [sem(f"y_out{p}") for p in range(2)]
        drop_ready, drop_out, pool_seq = sem("drop_ready"), sem("drop_out"), sem("pool_seq")
        even_stored, odd_stored = sem("even_stored"), sem("odd_stored")

        def is0(b):
            return isinstance(b, int) and b == 0

        def for_blocks(eng, nb, step):
            step(0, 0)
            for q in range(1, XBUF):
                with eng.If(q < nb):
                    step(0, q)
            with eng.Fori(1, (MAXB + XBUF - 1) // XBUF) as i:
                for q in range(XBUF):
                    with eng.If(i * XBUF + q < nb):
                        step(i, q)

        block = ctx.enter_context(nc.Block())
        SPR = 5
        TPB = 6


        @block.sync
        def _(sp):
            sp.dma_start(pw_sb, projw).then_inc(pat_in, 16)
            sp.dma_start(pat_sb, patches).then_inc(pat_in, 16)
            sp.dma_start(H[IMG:128, 0:NBATCH, :], txtA).then_inc(txt_in, 16)
            wv = wte[0:128 * WR * WCHUNKS, :].rearrange("(p c r) e -> p c (r e)", p=128, c=WCHUNKS)

            def load_wte(c, s):
                sp.dma_start(wchunk[s], wv[:, ds(c, 1), :].rearrange("p c x -> p (c x)")).then_inc(wte_in[s], 16)

            for s in range(WBUF):
                load_wte(s, s)
                if s == 1:
                    sp.dma_start(wo_sb[:], wo_attn).then_inc(wo_in, 16)
            sp.dma_start(H[0:BP, NBATCH:SLOTS, :], txtBp).then_inc(late_in, 16)
            sp.dma_start(mat32, cst2_d[:, C_MAT:NCST2]).then_inc(mat_in, 16)
            sp.dma_start(cst2[:], cst2_d[:, 0:C_MAT]).then_inc(cst2_in, 16)
            sp.dma_start(wtail[:], wte[VOCAB - WTAIL:VOCAB, :]).then_inc(wtail_in, 16)
            sp.wait_ge(zero_ready, 1)
            for n in range(XROWS // 384):
                sp.dma_start(xd[n * 384:(n + 1) * 384, :].rearrange("(p n) e -> p (n e)", n=3),
                             zeros[:, :, :].rearrange("p n e -> p (n e)")).then_inc(zero_done, 16)
            with sp.Fori(1, WCHUNKS // WBUF) as i:
                for s in range(WBUF):
                    sp.wait_ge(wte_added, (i - 1) * (2 * WBUF) + 2 * (s + 1))
                    load_wte(i * WBUF + s, s)
            sp.wait_ge(wte_added, 2 * WCHUNKS)
            sp.wait_ge(tab_ready, 1)
            nb = sp.value_load(nbI[0:1, 0:1], min_val=1, max_val=MAXB)

            def weights(b, p, used):
                e = sp.value_load(beI[0:1, ds(b, 1)], min_val=0, max_val=EXP - 1)
                if used is not None:
                    sp.wait_ge(h1_sum, used)
                sp.dma_start(wi_sb[p], wi[ds(e, 1)].rearrange("x p k c m -> (x p) k c m")).then_inc(wi_in[p], 16)
                if used is not None:
                    sp.wait_ge(y_sum, used)
                sp.dma_start(wo_x[p], wo[ds(e, 1)].rearrange("x p c e -> (x p) c e")).then_inc(wox_in[p], 16)

            def rows(b, q):
                sp.dma_start(xb[q], xd[ds(b * T, T), :]).then_inc(x_in[q], 16)

            weights(0, 0, None)
            sp.wait_ge(scattered, 16 * SLOTS)
            rows(0, 0)
            rows(1, 1)
            with sp.If(1 < nb):
                weights(1, 1, None)

            def block_loads(i, q):
                b = i * XBUF + q
                with sp.If(b + 1 < nb):
                    if isinstance(i, int) and q >= 2 or not isinstance(i, int):
                        sp.wait_ge(y_ready, b - 1)
                    rows(b + 2, (q + 2) % XBUF)
                with sp.If(b + 2 < nb):
                    weights(b + 2, q % 2, b + 1)
            for q in range(XBUF):
                block_loads(0, q)
            with sp.Fori(1, (MAXB + XBUF - 1) // XBUF) as i:
                for q in range(XBUF):
                    block_loads(i, q)
            sp.wait_ge(y_out[0], (nb + 1) // 2 * 16)
            sp.sem_inc(even_stored, 1)
            with sp.If(1 < nb):
                sp.wait_ge(y_out[1], nb // 2 * 16)
                sp.sem_inc(odd_stored, 1)
            sp.wait_ge(drop_out, 16 * SLOTS)

        @block.gpsimd
        def _(pool):
            nc.gpsimd.memset(mhalf[:], -0.5).then_inc(pool_step, 1)
            nc.gpsimd.memset(oh[:, :, :], 0.0).then_inc(ohz_ready, 1)
            nc.gpsimd.memset(kp[:, :, :], 0.0).then_inc(ohz_ready, 1)
            nc.gpsimd.memset(zeros[:], 0.0).then_inc(pool_step, 1)
            pool.wait_ge(pool_step, 2)
            nc.gpsimd.memset(zeros[:, :, D_ROW], float(BIG)).then_inc(zero_ready, 1)

            def rsqrt(y, x, k):
                pool.wait_ge(var_ready, k)
                nc.gpsimd.tensor_tensor(y, x, mhalf[0:y.shape[0], 0:x.shape[1] * x.shape[2]].rearrange("p (a b) -> p a b", a=2),
                                        ALU.pow).then_inc(pow_ready, 1)

            rsqrt(rstd[:, :, 0:2], nmr[:, :, 0:2], 1)

            def weigh(b, n, ks):
                pool.wait_ge(t_used, n)
                for g in range(4):
                    hs, ss, dst = (slice(4 * g, 4 * g + 4), slice(0, SA), AwA) if g < 3 else (slice(0, HEADS), slice(SA, SEQ), AwB)
                    for k in ks:
                        o = dst[:, k, hs, :]
                        nc.gpsimd.tensor_tensor(o, zT[:, k, ss].unsqueeze(1).to_broadcast(list(o.shape)),
                                                w2[:, k, hs].unsqueeze(2).to_broadcast(list(o.shape)),
                                                ALU.mult).then_inc(aw_ready, 1)

            def normalise(b):
                for r in range(SPR):
                    pool.wait_ge(rn_ready, SPR * b + r + 1)
                    if r < 3:
                        t, q = PA[:, 4 * r:4 * r + 4, :], rn[:, 4 * r:4 * r + 4]
                    else:
                        q0 = 2 * (r - 3)
                        t, q = PB[:, q0:q0 + 2, :], rn[0:HB * SB, 12 + q0:14 + q0]
                    nc.gpsimd.tensor_tensor(t, t, q.unsqueeze(2).to_broadcast(list(t.shape)), ALU.mult).then_inc(p_ready, 1)

            pool.wait_ge(w2_ready, 1)
            weigh(0, 1, (1,))
            rsqrt(rstd[:, :, 2:NBATCH], nmr[:, :, 2:NBATCH], 2)
            normalise(0)
            with pool.Fori(0, NBATCH - 1) as b:
                weigh(b + 1, TPB * b + 2, (0, 1))
                normalise(b + 1)

            for g, (j0, j1, n) in enumerate(GROUPS):
                rsqrt(rsq[0:n, :, j0:j1], var[0:n, :, j0:j1], 3 + g)

            def scatter(j):
                n = 128 if j < NBATCH else BP
                nc.gpsimd.indirect_dma_start(out=xd[:, :], out_offset=bass.IndirectOffsetOnAxis(ap=posI[0:n, j:j + 1], axis=0),
                                             in_=pay[0:n, j, :], in_offset=None, bounds_check=XROWS - 1,
                                             oob_is_err=False).then_inc(scattered, 16)

            def to_out(rows, idx, s):
                nc.gpsimd.indirect_dma_start(out=out[:, :], out_offset=bass.IndirectOffsetOnAxis(ap=idx, axis=0),
                                             in_=rows, in_offset=None, bounds_check=TOK - 1, oob_is_err=False).then_inc(s, 16)

            pool.wait_ge(zero_done, 16 * (XROWS // 384))
            pool.wait_ge(pos_ready, 1)
            pool.wait_ge(base_ready, NBATCH)
            for j in range(NBATCH):
                scatter(j)
            pool.wait_ge(pos_ready, 2)
            pool.wait_ge(base_ready, SLOTS)
            for j in range(NBATCH, SLOTS):
                scatter(j)
            pool.wait_ge(drop_ready, 1)
            for j in range(SLOTS):
                n = 128 if j < NBATCH else BP
                to_out(drow[0:n, j, :], dropI[0:n, j:j + 1], drop_out)
            pool.wait_ge(tab_ready, 1)
            nb = pool.value_load(nbI[0:1, 0:1], min_val=1, max_val=MAXB)

            def block_step(i, q):
                pool.wait_ge(y_ready, i * XBUF + q + 1)
                pool.sem_inc(pool_seq, 1)
                to_out(ysb[q % 2], yrow[q % 2][:, 0:1], y_out[q % 2])

            for_blocks(pool, nb, block_step)

        @block.scalar
        def _(act):
            act.dma_start(hB[:], txtB).then_inc(txt_in, 16)
            for dst, src in ((posb, pos), (pbb, projb), (w2[:], wqk), (ln96[:], lnw)):
                act.dma_start(dst, src).then_inc(small_in, 16)
            act.dma_start(cst[:], cst_d).then_inc(cst_in, 16)
            for dst, src in ((lncol[:], lnc), (flnb[:], flnw), (wr_sb[:], wrt)):
                act.dma_start(dst, src).then_inc(late_in, 16)
            for k in range(2):
                act.wait_ge(emb_ready, k + 1)
                nc.scalar.activation(embT[:, k, :], bO[k][0:EC, 0:NBATCH * IMG], ACT.Copy).then_inc(embT_ready, 1)
            act.wait_ge(cst_in, 16)
            nc.scalar.activation(idb[:], ident, ACT.Copy).then_inc(bf_ready, 1)
            nc.scalar.activation(maskA[:], cst[:, C_MA:C_MA + SA], ACT.Copy).then_inc(bf_ready, 1)
            nc.scalar.activation(maskB[:], cst[:, C_MB:C_MB + SEQ], ACT.Copy).then_inc(bf_ready, 1)

            def zt_copy(n, par):
                act.wait_ge(t_ready, n)
                nc.scalar.activation(zT[:, :, :], bT[par][0:EC, 0:2 * SEQ].rearrange("p (k s) -> p k s", k=2),
                                     ACT.Copy).then_inc(t_used, 1)

            def values(b):
                act.wait_ge(z_ready, 2 * (b + 1))
                if not is0(b):
                    act.wait_ge(e_ready, 4 * b)
                nc.scalar.activation(vA[:], zA[:], ACT.Copy).then_inc(v_ready, 1)
                nc.scalar.activation(vB[:], zB[:], ACT.Copy).then_inc(v_ready, 1)

            def exps(b):
                for r in range(SPR):
                    act.wait_ge(max_ready, SPR * b + r + 1)
                    bank = bS[r % 2]
                    if r < 3:
                        for j in range(4):
                            h = 4 * r + j
                            last = nc.scalar.activation(PA[:, h, :], bank[:, j * SA:(j + 1) * SA], ACT.Exp,
                                                        bias=negmax[:, h:h + 1], accum_out=lsum[:, h:h + 1])
                    else:
                        for j in range(2):
                            q = 2 * (r - 3) + j
                            last = nc.scalar.activation(PB[:, q, :], bank[0:HB * SB, j * SEQ:(j + 1) * SEQ], ACT.Exp,
                                                        bias=negmax[0:HB * SB, 12 + q:13 + q],
                                                        accum_out=lsum[0:HB * SB, 12 + q:13 + q])
                    last.then_inc(exp_ready, 1)

            def attn_copies(b, n, par):
                def t_copy(q):
                    act.wait_ge(t_ready, n + q + 1)
                    bank = bT[(par + q) % 2]
                    if q < 3:
                        dst, src = PTA[:, 4 * q:4 * q + 4, :], bank[:, 0:4 * SA].rearrange("p (h s) -> p h s", h=4)
                    elif q == 3:
                        dst, src = PTB0[:, :, :], bank[:, 0:HEADS * SB].rearrange("p (h s) -> p h s", h=HEADS)
                    else:
                        dst, src = PTB1[:, :, :], bank[0:SB, 0:HEADS * SB].rearrange("p (h s) -> p h s", h=HEADS)
                    nc.scalar.activation(dst, src, ACT.Copy).then_inc(t_used, 1)

                def o_copy(g):
                    act.wait_ge(o_ready, 4 * b + g + 1)
                    if g < 3:
                        dst, src = oTA[:, 4 * g:4 * g + 4, :], bO[g % 2][:, 0:4 * SA].rearrange("p (h s) -> p h s", h=4)
                    else:
                        dst, src = oTB[:, 0:HEADS, ds(b * SB, SB)], bO[1][:, 0:HEADS * SB].rearrange("p (h s) -> p h s", h=HEADS)
                    nc.scalar.activation(dst, src, ACT.Copy, scale=lncol[:, 0:1]).then_inc(o_used, 1)

                t_copy(0)
                t_copy(1)
                o_copy(0)
                t_copy(2)
                o_copy(1)
                t_copy(3)
                o_copy(2)
                t_copy(4)
                o_copy(3)

            zt_copy(1, 0)
            values(0)
            exps(0)
            act.wait_ge(late_in, 16 * 4)
            def iteration(b):
                zt_copy(TPB * b + 2, 1)
                attn_copies(b, TPB * b + 2, 0)
                values(b + 1)
                exps(b + 1)

            iteration(0)
            act.wait_ge(mat_in, 16)
            nc.scalar.activation(mat[:, :, :].rearrange("p m s -> p (m s)"), mat32, ACT.Copy).then_inc(mat_ready, 1)
            with act.Fori(1, NBATCH - 1) as b:
                iteration(b)
            attn_copies(NBATCH - 1, TPB * (NBATCH - 1) + 1, 1)

            def bases(g):
                act.wait_ge(basepar_ready, g + 1)
                j0, j1, n = GROUPS[g]
                for j in range(j0, j1):
                    nc.scalar.activation(base[0:n, j, :], H[0:n, j, :], ACT.Identity, bias=nmb[0:n, j:j + 1],
                                         scale=rsq1[0:n, j:j + 1]).then_inc(base_ready, 1)

            def nt_copy(g, k, bank):
                act.wait_ge(nT_sum, 2 * g + k + 1)
                j0, m, n = (4 * g, 4, 128) if g < 2 else (NBATCH, NBT, BP)
                nc.scalar.activation(nT[:, k, j0 * 128:j0 * 128 + m * n], bank[0:EC, 0:m * n], ACT.Copy).then_inc(nT_ready, 1)

            bases(0)
            bases(1)
            for g in range(2):
                for k in range(2):
                    nt_copy(g, k, (bS, bT)[g][k])
            act.wait_ge(le_ready, 1)
            nc.scalar.activation(lx[:, 0:NBATCH, :], lg[:, 0:NBATCH, :], ACT.Exp).then_inc(lx_ready, 1)
            bases(2)
            bases(3)
            for k in range(2):
                nt_copy(2, k, bS[k])
            bases(4)
            act.wait_ge(le_ready, 2)
            nc.scalar.activation(lx[0:BP, NBATCH:SLOTS, :], lg[0:BP, NBATCH:SLOTS, :], ACT.Exp).then_inc(lx_ready, 1)
            act.wait_ge(tab_ready, 1)
            nb = act.value_load(nbI[0:1, 0:1], min_val=1, max_val=MAXB)

            def block_step(i, q):
                act.wait_ge(h0_sum, i * XBUF + q + 1)
                nc.scalar.activation(hT[:, 0:4, :], bO[0][:, :].rearrange("p (c n) -> p c n", c=4), ACT.Relu).then_inc(h0_ready, 1)

            for_blocks(act, nb, block_step)

        @block.vector
        def _(dve):
            chain = [0]

            def link(ins):
                chain[0] += 1
                ins.then_inc(dve_step, 1)
                dve.wait_ge(dve_step, chain[0])

            def newton(x, y, t):
                link(nc.vector.tensor_tensor(t, y, y, ALU.mult))
                link(nc.vector.tensor_tensor(t, t, x, ALU.mult))
                link(nc.vector.tensor_scalar(t, t, -0.5, 1.5, ALU.mult, ALU.add))
                link(nc.vector.tensor_tensor(y, y, t, ALU.mult))

            accf = acc[:, :, :].rearrange("p r e -> p (r e)")
            HALF = WR * EMB // 2
            nc.vector.memset(one[:], 1.0)
            nc.vector.memset(oneX[:], 1.0)
            nc.vector.memset(ones[:], 1.0)
            link(nc.vector.memset(mv[:, :, :, :].rearrange("p a b c -> p (a b c)"), 1.0))
            dve.wait_ge(small_in, 16 * 4)
            link(nc.vector.tensor_tensor(posb, posb, pbb, ALU.add))
            link(nc.vector.tensor_tensor(w2[:, :, :], w2[:, :, :], ln96[:, :].unsqueeze(2).to_broadcast([EC, 2, HEADS]), ALU.mult))
            link(nc.vector.tensor_tensor(w2[:, :, :], w2[:, :, :], w2[:, :, :], ALU.mult))
            nc.vector.tensor_scalar(w2[:, :, :], w2[:, :, :], float(EMB) ** -0.5, None, ALU.mult).then_inc(w2_ready, 1)
            link(nc.vector.memset(accf, 0.0))
            dve.wait_ge(txt_in, 32)
            eps = 1e-5

            def add_patches(j):
                dve.wait_ge(tok_ready, j + 1)
                bank = (bT[0], bE, bJ, bO[1])[j]
                nc.vector.tensor_tensor(H[0:IMG, 2 * j:2 * j + 2, :],
                                        bank[0:IMG, 0:2 * EMB].rearrange("p (b e) -> p b e", b=2),
                                        posb.unsqueeze(1).to_broadcast([IMG, 2, EMB]), ALU.add).then_inc(tok_added, 1)
                dve.wait_ge(tok_added, j + 1)

            def factors(b0, b1, k):
                for b in range(b0, b1):
                    nc.vector.bn_stats(st6[0:SB, 1, b, :], hB[:, b, :])
                    last = nc.vector.bn_stats(st6[:, 0, b, :], H[:, b, :])
                link(last)
                for b in range(b0, b1):
                    nc.vector.bn_aggr(mv[:, 0, b, :], st6[:, 0, b, :])
                    last = nc.vector.bn_aggr(mv[0:SB, 1, b, :], st6[0:SB, 1, b, :])
                link(last)
                x, y, t = nmr[:, :, b0:b1], rstd[:, :, b0:b1], nwz[:, :, b0:b1]
                nc.vector.tensor_scalar(x, mv[:, :, b0:b1, 1], 1.0 + eps, eps * eps, ALU.mult, ALU.add).then_inc(var_ready, 1)
                dve.wait_ge(pow_ready, k)
                newton(x, y, t)
                link(nc.vector.tensor_scalar(x, mv[:, :, b0:b1, 0], -1.0, None, ALU.mult))
                link(nc.vector.tensor_tensor(x, x, y, ALU.mult))

            add_patches(0)
            factors(0, 2, 1)

            def z(b):
                nc.vector.tensor_scalar(zA[:, :], H[:, ds(b, 1), :].rearrange("p b e -> p (b e)"), rstd[:, 0, ds(b, 1)],
                                        nmr[:, 0, ds(b, 1)], ALU.mult, ALU.add).then_inc(z_ready, 1)
                nc.vector.tensor_scalar(zB[:, :], hB[:, ds(b, 1), :].rearrange("p b e -> p (b e)"), rstd[0:SB, 1, ds(b, 1)],
                                        nmr[0:SB, 1, ds(b, 1)], ALU.mult, ALU.add).then_inc(z_ready, 1)

            def row_max(b, r):
                dve.wait_ge(score_ready, SPR * b + r + 1)
                if r < 3:
                    nc.vector.tensor_reduce(negmax[:, 4 * r:4 * r + 4], bS[r % 2][:, :].rearrange("p (h s) -> p h s", h=4),
                                            X, ALU.max, negate=True).then_inc(max_ready, 1)
                else:
                    q = 12 + 2 * (r - 3)
                    nc.vector.tensor_reduce(negmax[0:HB * SB, q:q + 2], bS[r % 2][0:HB * SB, 0:2 * SEQ].rearrange("p (h s) -> p h s", h=2),
                                            X, ALU.max, negate=True).then_inc(max_ready, 1)

            def row_factor(b, r):
                dve.wait_ge(exp_ready, SPR * b + r + 1)
                n, q0, q1, c = (128, 4 * r, 4 * r + 4, C_NA) if r < 3 else (HB * SB, 6 + 2 * r, 8 + 2 * r, C_NB)
                nc.vector.reciprocal(rinv[0:n, q0:q1], lsum[0:n, q0:q1]).then_inc(rinv_ready, 1)
                dve.wait_ge(rinv_ready, SPR * b + r + 1)
                nc.vector.tensor_scalar(rn[0:n, q0:q1], rinv[0:n, q0:q1], cst[0:n, c:c + 1], None, ALU.mult).then_inc(rn_ready, 1)

            def e_copy(b, g):
                dve.wait_ge(e_ready, 4 * b + g + 1)
                if g < 3:
                    dst, src = oTA[:, HEADS + 2 * g:HEADS + 2 * g + 2, :], bE[:, 0:2 * SA].rearrange("p (h s) -> p h s", h=2)
                else:
                    dst, src = oTB[:, HEADS:WCH, ds(b * SB, SB)], bE[:, 0:6 * SB].rearrange("p (h s) -> p h s", h=6)
                nc.vector.tensor_scalar(dst, src, lncol[:, 1:2], None, ALU.mult).then_inc(e_used, 1)

            def wte_add(b, k):
                s, h = k // 2, k % 2
                if h == 0:
                    dve.wait_ge(wte_in[s], 16 * (b + 1))
                if k or not is0(b):
                    dve.wait_ge(wte_added, 2 * WBUF * b + k)
                part = slice(h * HALF, (h + 1) * HALF)
                nc.vector.tensor_tensor(accf[:, part], accf[:, part], wchunk[s][:, part], ALU.add).then_inc(wte_added, 1)

            def residual(b):
                dve.wait_ge(j_ready, b + 1)
                row = H[:, ds(b, 1), :].rearrange("p b e -> p (b e)")
                nc.vector.tensor_tensor(row, bJ[:, 0:EMB], row, ALU.add).then_inc(j_used, 1)

            z(0)
            dve.wait_ge(t_used, 1)
            for g in range(4):
                hs, ss, dst = (slice(4 * g, 4 * g + 4), slice(0, SA), AwA) if g < 3 else (slice(0, HEADS), slice(SA, SEQ), AwB)
                o = dst[:, 0, hs, :]
                nc.vector.tensor_tensor(o, zT[:, 0, ss].unsqueeze(1).to_broadcast(list(o.shape)),
                                        w2[:, 0, hs].unsqueeze(2).to_broadcast(list(o.shape)), ALU.mult).then_inc(aw0_ready, 1)
                if g == 1:
                    row_max(0, 0)
                elif g == 3:
                    row_max(0, 1)
            row_factor(0, 0)
            for r in range(2, SPR):
                row_max(0, r)
                row_factor(0, r - 1)
            row_factor(0, SPR - 1)
            dve.wait_ge(v_ready, 2)
            dve.wait_ge(t_ready, 1)
            z(1)
            for j in range(1, 4):
                add_patches(j)
            factors(2, NBATCH, 2)

            def iteration(b, more):
                wte_add(b, 0)
                e_copy(b, 0)
                wte_add(b, 1)
                e_copy(b, 1)
                wte_add(b, 2)
                e_copy(b, 2)
                wte_add(b, 3)
                e_copy(b, 3)
                row_max(b + 1, 0)
                wte_add(b, 4)
                row_max(b + 1, 1)
                row_factor(b + 1, 0)
                wte_add(b, 5)
                row_max(b + 1, 2)
                row_factor(b + 1, 1)
                if more:
                    dve.wait_ge(v_ready, 2 * (b + 2))
                    dve.wait_ge(t_ready, TPB * b + 2)
                    z(b + 2)
                row_max(b + 1, 3)
                row_factor(b + 1, 2)
                wte_add(b, 6)
                row_max(b + 1, 4)
                row_factor(b + 1, 3)
                wte_add(b, 7)
                row_factor(b + 1, 4)
                residual(b)

            iteration(0, True)
            dve.wait_ge(wo_in, 16)
            nc.vector.tensor_reduce(ws[:, 0, :], wo_sb[:, 0:HEADS, :].rearrange("p h e -> p e h"), X, ALU.add)
            link(nc.vector.tensor_reduce(ws[:, 1, :], wo_sb[:, HEADS:WCH, :].rearrange("p h e -> p e h"), X, ALU.add))
            with dve.Fori(1, NBATCH - 2) as b:
                iteration(b, True)
            iteration(NBATCH - 2, False)
            dve.wait_ge(wte_added, 2 * WCHUNKS)
            link(nc.vector.tensor_reduce(wsum[:, :], acc[:, :, :].rearrange("p r e -> p e r"), X, ALU.add))
            dve.wait_ge(wtail_in, 16)
            nc.vector.tensor_tensor(wsum[0:WTAIL, :], wsum[0:WTAIL, :], wtail[:, :], ALU.add).then_inc(acc_ready, 1)
            LAST = NBATCH - 1
            e_copy(LAST, 0)
            dve.wait_ge(avg_sum, 1)
            nc.vector.tensor_scalar(avg[:, :], bS[0][:, 0:2], 1.0 / VOCAB, None, ALU.mult).then_inc(avg_ready, 1)
            e_copy(LAST, 1)
            dve.wait_ge(c_ready, 1)
            nc.vector.tensor_copy(cS[:, :], bS[1][:, 0:EMB])
            nc.vector.tensor_scalar(cN[:, :], bS[1][:, 0:EMB], cst[:, C_NA:C_NA + 1], -1.0, ALU.mult, ALU.mult).then_inc(c_used, 1)
            dve.wait_ge(c_used, 1)

            def prepare(g):
                j0, j1, n = GROUPS[g]
                rows = H[0:n, j0:j1, :]
                if j0 < NBATCH:
                    link(nc.vector.tensor_tensor(rows, rows, cN[:, :].unsqueeze(1).to_broadcast([128, j1 - j0, EMB]), ALU.add))
                else:
                    i = j0 - NBATCH
                    link(nc.vector.scalar_tensor_tensor(H[0:n, j0, :], cS[0:n, :], cst[0:n, C_NBP + i:C_NBP + i + 1],
                                                        H[0:n, j0, :], ALU.mult, ALU.add))
                for j in range(j0, j1):
                    last = nc.vector.bn_stats(fst[0:n, j, :], H[0:n, j, :])
                link(last)
                for j in range(j0, j1):
                    last = nc.vector.bn_aggr(fmv[0:n, j, :], fst[0:n, j, :])
                link(last)
                v, x, y = fmv[0:n, j0:j1, 1], var[0:n, :, j0:j1], rsq[0:n, :, j0:j1]
                link(nc.vector.tensor_scalar(var[0:n, 0, j0:j1], v, 1e-5, None, ALU.add))
                nc.vector.tensor_scalar(var[0:n, 1, j0:j1], v, 1.0 + 1e-6, 1e-11, ALU.mult, ALU.add).then_inc(var_ready, 1)
                dve.wait_ge(pow_ready, 3 + g)
                newton(x, y, nwt[0:n, :, j0:j1])
                for j in range(j0, j1):
                    last = nc.vector.tensor_scalar(norm[0:n, j, :], H[0:n, j, :], fmv[0:n, j, 0:1], rsq[0:n, 1, j:j + 1],
                                                   ALU.subtract, ALU.mult)
                link(last)
                nc.vector.tensor_tensor(norm[0:n, j0:j1, :], norm[0:n, j0:j1, :],
                                        flnb[0:n, :].unsqueeze(1).to_broadcast([n, j1 - j0, EMB]), ALU.mult).then_inc(norm_ready, 1)
                link(nc.vector.tensor_scalar(rsq1[0:n, j0:j1], rsq[0:n, 0, j0:j1], 1.0, None, ALU.add))
                nc.vector.scalar_tensor_tensor(nmb[0:n, j0:j1], fmv[0:n, j0:j1, 0], -1.0, rsq[0:n, 0, j0:j1], ALU.mult,
                                               ALU.mult).then_inc(basepar_ready, 1)

            def residual_b(i):
                dve.wait_ge(jb_ready, i + 1)
                j = NBATCH + i
                link(nc.vector.tensor_tensor(H[0:BP, j, :], (bO[0], bO[1], bJ)[i][0:BP, 0:EMB], H[0:BP, j, :], ALU.add))

            def part(t, B):
                return t[0:BP, NBATCH:SLOTS] if B else t[:, 0:NBATCH]

            def routed(B):
                n, s = (BP, NBT) if B else (128, NBATCH)
                bc = [n, s, EXP]
                dve.wait_ge(lg_ready, B + 1)
                logits = bE[0:n, B * NBATCH * EXP:(B * NBATCH + s) * EXP].rearrange("p (j x) -> p j x", j=s)
                em = cst2[0:n, C_EM:C_EM + EXP].unsqueeze(1).to_broadcast(bc)
                l, t = part(lg, B), part(l1, B)
                link(nc.vector.tensor_reduce(part(lmax, B), logits, X, ALU.max))
                nc.vector.tensor_tensor(l, logits, part(lmax, B).unsqueeze(2).to_broadcast(bc), ALU.subtract).then_inc(le_ready, 1)
                dve.wait_ge(le_ready, B + 1)
                link(nc.vector.scalar_tensor_tensor(t, l, 0.0, em, ALU.is_ge, ALU.mult))
                link(nc.vector.tensor_reduce(part(lidx, B), t, X, ALU.min))
                nc.vector.tensor_tensor(part(oh, B), em, part(lidx, B).unsqueeze(2).to_broadcast(bc), ALU.is_equal).then_inc(oh_ready, 1)
                dve.wait_ge(lx_ready, B + 1)
                link(nc.vector.tensor_reduce(part(lsm, B), part(lx, B), X, ALU.add))
                link(nc.vector.reciprocal(pay[0:n, B * NBATCH:B * NBATCH + s, D_RP], part(lsm, B)))

            def keep(B):
                n, s = (BP, NBT) if B else (128, NBATCH)
                dve.wait_ge(oh_ready, B + 1)
                dve.wait_ge(rank_ready, B + 1)
                nc.vector.scalar_tensor_tensor(part(kp, B), bO[B][0:n, 0:s * EXP].rearrange("p (j x) -> p j x", j=s),
                                               float(CAP), part(oh, B), ALU.is_lt, ALU.mult).then_inc(kp_ready, 1)
                dve.wait_ge(kp_ready, B + 1)
                link(nc.vector.tensor_reduce(part(kept, B), part(kp, B), X, ALU.add))
                link(nc.vector.tensor_scalar(part(drop, B), part(kept, B), -1.0, 1.0, ALU.mult, ALU.add))

            def place(B):
                n, s = (BP, NBT) if B else (128, NBATCH)
                bc = [n, s, EXP]
                dve.wait_ge(grank_ready, B + 1)
                gk = bT[0][0:n, B * NBATCH * EXP:(B * NBATCH + s) * EXP].rearrange("p (j x) -> p j x", j=s)
                cnt = bT[0][:, SLOTS * EXP:(SLOTS + 1) * EXP]
                link(nc.vector.tensor_scalar(capI[:, B, :], cnt, float(T - 1), None, ALU.add))
                link(nc.vector.tensor_scalar(capI[:, B, :], capI[:, B, :], -T, None, ALU.bitwise_and))
                link(nc.vector.tensor_copy(capF[:, B, :], capI[:, B, :]))
                t, u = part(l1, B), part(l2, B)
                if B:
                    link(nc.vector.tensor_tensor(capB[:, :], capF[:, 1, :], capF[:, 0, :], ALU.subtract))
                    link(nc.vector.tensor_tensor_scan(cum[:, 1, :], oneX[:, :], capB[:, :], cum[:, 0, EXP - 1:EXP], ALU.mult, ALU.add))
                    link(nc.vector.tensor_tensor(first[:, 1, :], cum[:, 1, :], capF[:, 1, :], ALU.subtract))
                    link(nc.vector.tensor_tensor(first[:, 1, :], first[:, 1, :], first[:, 0, :], ALU.subtract))
                    link(nc.vector.tensor_tensor(t, gk, capF[0:n, 0, :].unsqueeze(1).to_broadcast(bc), ALU.is_ge))
                    link(nc.vector.tensor_tensor(t, t, first[0:n, 1, :].unsqueeze(1).to_broadcast(bc), ALU.mult))
                    link(nc.vector.tensor_tensor(t, t, first[0:n, 0, :].unsqueeze(1).to_broadcast(bc), ALU.add))
                    link(nc.vector.tensor_tensor(u, gk, t, ALU.add))
                else:
                    link(nc.vector.tensor_tensor_scan(cum[:, 0, :], oneX[:, :], capF[:, 0, :], 0.0, ALU.mult, ALU.add))
                    link(nc.vector.tensor_tensor(first[:, 0, :], cum[:, 0, :], capF[:, 0, :], ALU.subtract))
                    link(nc.vector.tensor_tensor(u, gk, first[0:n, 0, :].unsqueeze(1).to_broadcast(bc), ALU.add))
                link(nc.vector.tensor_tensor(u, u, part(kp, B), ALU.mult))
                link(nc.vector.tensor_reduce(part(posF, B), u, X, ALU.add))
                nc.vector.scalar_tensor_tensor(part(posI, B), part(drop, B), float(BIG), part(posF, B), ALU.mult, ALU.add).then_inc(pos_ready, 1)

            dve.wait_ge(late_in, 64)
            dve.wait_ge(cst2_in, 16)
            dve.wait_ge(mat_ready, 1)
            nc.vector.tensor_copy(pay[:, :, D_ROW], cst2[:, C_ROW:C_ROW + SLOTS])
            e_copy(LAST, 2)
            e_copy(LAST, 3)
            dve.wait_ge(j_used, LAST)
            prepare(0)
            residual(LAST)
            dve.wait_ge(j_used, NBATCH)
            prepare(1)
            residual_b(0)
            prepare(2)
            dve.wait_ge(ohz_ready, 2)
            routed(0)
            residual_b(1)
            prepare(3)
            keep(0)
            place(0)
            residual_b(2)
            prepare(4)
            routed(1)
            keep(1)
            place(1)
            bb = [1, MAXB, 2, EXP]
            link(nc.vector.tensor_tensor(bex[:, :, :, :], cum[0:1, :, :].unsqueeze(1).to_broadcast(bb),
                                         cst2[0:1, C_BI:C_BI + MAXB].unsqueeze(2).unsqueeze(3).to_broadcast(bb), ALU.is_le))
            link(nc.vector.tensor_reduce(beF[:, :], bex[:, :, :, :].rearrange("p b t x -> p b (t x)"), X, ALU.add))
            link(nc.vector.tensor_copy(beI[:, 0:MAXB], beF[:, :]))
            link(nc.vector.tensor_scalar(beI[:, 0:MAXB], beI[:, 0:MAXB], EXP - 1, None, ALU.bitwise_and))
            link(nc.vector.tensor_copy(nbI[:, 1:2], cum[0:1, 1, EXP - 1:EXP]))
            nc.vector.tensor_scalar(nbI[:, 0:1], nbI[:, 1:2], T.bit_length() - 1, None, ALU.logical_shift_right).then_inc(tab_ready, 1)
            dve.wait_ge(base_ready, SLOTS)
            for j in range(SLOTS):
                n = 128 if j < NBATCH else BP
                nc.vector.scalar_tensor_tensor(drow[0:n, j, :], norm[0:n, j, :], pay[0:n, j, D_RP:D_RP + 1], base[0:n, j, :], ALU.mult, ALU.add)
            link(nc.vector.scalar_tensor_tensor(dropF[:, 0:NBATCH], kept[:, 0:NBATCH], float(BIG), pay[:, 0:NBATCH, D_ROW], ALU.mult, ALU.add))
            link(nc.vector.scalar_tensor_tensor(dropF[0:BP, NBATCH:SLOTS], kept[0:BP, NBATCH:SLOTS], float(BIG), pay[0:BP, NBATCH:SLOTS, D_ROW], ALU.mult, ALU.add))
            nc.vector.tensor_copy(dropI[:, 0:NBATCH], dropF[:, 0:NBATCH])
            nc.vector.tensor_copy(dropI[0:BP, NBATCH:SLOTS], dropF[0:BP, NBATCH:SLOTS]).then_inc(drop_ready, 1)

            dve.wait_ge(tab_ready, 1)
            nb = dve.value_load(nbI[0:1, 0:1], min_val=1, max_val=MAXB)

            def xt_copy(b):
                dve.wait_ge(xT_sum, b + 1)
                nc.vector.tensor_copy(xT, bT[1][0:EC, 0:2 * T].rearrange("p (k n) -> p k n", k=2)).then_inc(xT_ready, 1)

            xt_copy(0)

            def block_step(i, q):
                b, p = i * XBUF + q, q % 2
                dve.wait_ge(h1_sum, b + 1)
                nc.vector.tensor_scalar(hT[:, 4:6, :], bO[1][:, 0:2 * T].rearrange("p (c n) -> p c n", c=2), 0.0, None,
                                        ALU.max).then_inc(h1_ready, 1)
                xt_copy(b + 1)
                if q >= 2 or not is0(i):
                    dve.wait_ge(y_out[p], (i * 2 + q // 2) * 16)
                nc.vector.tensor_copy(yrow[p][:, :], xb[q][:, D_ROW:D_ROW + 1])
                dve.wait_ge(y_sum, b + 1)
                nc.vector.scalar_tensor_tensor(ysb[p], bE[:, 0:EMB], xb[q][:, D_RP:D_RP + 1], xb[q][:, D_BASE:D_BASE + EMB],
                                               ALU.mult, ALU.add).then_inc(y_ready, 1)

            for_blocks(dve, nb, block_step)

        @block.tensor
        def _(pe):
            def mm(o, l, r, start=True, stop=True):
                return nc.tensor.matmul(o, l, r, start=start, stop=stop, skip_group_check=True)

            pe.wait_ge(pat_in, 32)
            for k2 in range(2):
                for k in range(6):
                    last = mm(bO[k2][0:EC, 0:NBATCH * IMG], pw_sb[:, k, k2 * EC:(k2 + 1) * EC], pat_sb[:, k, :], k == 0, k == 5)
                last.then_inc(emb_ready, 1)
            pe.wait_ge(cst_in, 16)
            pe.wait_ge(embT_ready, 2)
            for j in range(4):
                bank = (bT[0], bE, bJ, bO[1])[j]
                for c in range(4):
                    b, k = 2 * j + c // 2, c % 2
                    last = nc.tensor.transpose(bank[0:IMG, c * EC:(c + 1) * EC], embT[:, k, b * IMG:(b + 1) * IMG], ident[0:EC, 0:EC])
                last.then_inc(tok_ready, 1)

            HS = HB * SB
            mask4 = maskA[:, :].unsqueeze(1).to_broadcast([128, 4, SA])
            mask2 = maskB[0:HS, :].unsqueeze(1).to_broadcast([HS, 2, SEQ])

            def z_transpose(b, par):
                pe.wait_ge(z_ready, 2 * (b + 1))
                pe.wait_ge(cst_in, 16)
                for k in range(2):
                    nc.tensor.transpose(bT[par][0:EC, k * SEQ:k * SEQ + SA], zA[:, k * EC:(k + 1) * EC], ident)
                    last = nc.tensor.transpose(bT[par][0:EC, k * SEQ + SA:(k + 1) * SEQ], zB[:, k * EC:(k + 1) * EC], ident[0:SB, 0:SB])
                last.then_inc(t_ready, 1)

            def score(b, r, first=False):
                bank = bS[r % 2]
                if is0(b):
                    pe.wait_ge(aw0_ready, min(r + 1, 4))
                    pe.wait_ge(aw_ready, min(r + 1, 4))
                else:
                    pe.wait_ge(aw_ready, 8 * b - 4 + min(2 * r + 2, 8))
                if not first:
                    pe.wait_ge(exp_ready, SPR * b + max(r - 1, 0))
                if r < 3:
                    mm(bank[:, :].rearrange("p (h s) -> p h s", h=4), idb[:, :], mask4, True, False)
                    for j in range(4):
                        for k in range(2):
                            last = mm(bank[:, j * SA:(j + 1) * SA], AwA[:, k, 4 * r + j, :], zT[:, k, 0:SA], False, k == 1)
                else:
                    mm(bank[0:HS, 0:2 * SEQ].rearrange("p (h s) -> p h s", h=2), idb[0:HS, 0:HS], mask2, True, False)
                    for j in range(2):
                        q = 2 * (r - 3) + j
                        for k in range(2):
                            last = mm(bank[0:HS, j * SEQ:(j + 1) * SEQ], AwB[:, k, HB * q:HB * (q + 1), :].rearrange("p h s -> p (h s)"), zT[:, k, :], False, k == 1)
                last.then_inc(score_ready, 1)

            def p_transpose(b, q, n, par):
                if q < 4:
                    pe.wait_ge(p_ready, SPR * b + (q + 1 if q < 3 else SPR))
                    pe.wait_ge(t_used, n + q - 1)
                bank = bT[(par + q) % 2]
                if q < 3:
                    for j in range(4):
                        last = nc.tensor.transpose(bank[:, j * SA:(j + 1) * SA], PA[:, 4 * q + j, :], ident)
                else:
                    for g in range(NG):
                        if q == 3:
                            last = nc.tensor.transpose(bank[:, g * HS:(g + 1) * HS], PB[:, g, 0:SA], ident[0:HS, 0:HS])
                        else:
                            last = nc.tensor.transpose(bank[0:SB, g * HS:(g + 1) * HS], PB[:, g, SA:SEQ], ident[0:HS, 0:HS])
                last.then_inc(t_ready, 1)

            def value(b, g, n):
                if g == 0:
                    pe.wait_ge(v_ready, 2 * (b + 1))
                    if is0(b):
                        pe.wait_ge(tok_added, 4)
                    else:
                        pe.wait_ge(o_used, 4 * b)
                elif g > 1:
                    pe.wait_ge(o_used, 4 * b + g - 1)
                pe.wait_ge(t_used, n + (g + 1 if g < 3 else 5))
                o = bO[g % 2]
                if g < 3:
                    mm(o[:, :].rearrange("p (h s) -> p h s", h=4), vA[:, 0:E0], PTA[:, 4 * g:4 * g + 4, :]).then_inc(o_ready, 1)
                else:
                    oo = o[:, 0:HEADS * SB].rearrange("p (h s) -> p h s", h=HEADS)
                    mm(oo, vA[:, 0:E0], PTB0[:, :, :], True, False)
                    mm(oo, vB[:, 0:E0], PTB1[:, :, :], False, True).then_inc(o_ready, 1)
                if g or not is0(b):
                    pe.wait_ge(e_used, 4 * b + g)
                for odd in range(2):
                    part = slice(odd * E1, (odd + 1) * E1)
                    if g < 3:
                        last = mm(bE[part, 0:2 * SA].rearrange("p (h s) -> p h s", h=2), vA[:, E0:EMB], PTA[:, 4 * g + odd:4 * g + 4:2, :])
                    else:
                        ee = bE[part, 0:6 * SB].rearrange("p (h s) -> p h s", h=6)
                        mm(ee, vA[:, E0:EMB], PTB0[:, odd:HEADS:2, :], True, False)
                        last = mm(ee, vB[:, E0:EMB], PTB1[:, odd:HEADS:2, :], False, True)
                last.then_inc(e_ready, 1)

            def attend(b, n, par):
                p_transpose(b, 0, n, par)
                p_transpose(b, 1, n, par)
                value(b, 0, n)
                p_transpose(b, 2, n, par)
                value(b, 1, n)
                p_transpose(b, 3, n, par)
                value(b, 2, n)
                p_transpose(b, 4, n, par)
                value(b, 3, n)

            def project(b, c0, c1):
                if c0 == 0:
                    pe.wait_ge(wo_in, 16)
                    if not is0(b):
                        pe.wait_ge(j_used, b)
                    pe.wait_ge(o_used, 4 * b + 3)
                    pe.wait_ge(e_used, 4 * b + 3)
                for c in range(c0, c1):
                    last = mm(bJ[:, 0:EMB], oTA[:, c, :], wo_sb[:, c, :], c == 0, c == WCH - 1)
                if c1 == WCH:
                    last.then_inc(j_ready, 1)

            z_transpose(0, 0)
            pe.wait_ge(bf_ready, 3)
            for r in range(SPR):
                score(0, r, r < 2)

            def iteration(b):
                n = TPB * b + 2
                z_transpose(b + 1, 1)
                attend(b, n, 0)
                pe.wait_ge(t_used, n)
                score(b + 1, 0)
                score(b + 1, 1)
                project(b, 0, 5)
                score(b + 1, 2)
                project(b, 5, 10)
                score(b + 1, 3)
                project(b, 10, 14)
                score(b + 1, 4)
                project(b, 14, WCH)

            iteration(0)
            with pe.Fori(1, NBATCH - 1) as b:
                iteration(b)
            LAST = NBATCH - 1
            n = TPB * LAST + 1
            p_transpose(LAST, 0, n, 1)
            p_transpose(LAST, 1, n, 1)
            value(LAST, 0, n)
            p_transpose(LAST, 2, n, 1)
            value(LAST, 1, n)
            pe.wait_ge(acc_ready, 1)
            pe.wait_ge(exp_ready, SPR * NBATCH)
            mm(bS[0][:, 0:1], wsum[:, 0:E0], one[:, :])
            mm(bS[0][0:E1, 1:2], wsum[:, E0:EMB], one[:, :])
            mm(bS[0][E1:128, 1:2], wsum[:, E0:EMB], one[:, :]).then_inc(avg_sum, 1)
            p_transpose(LAST, 3, n, 1)
            value(LAST, 2, n)
            p_transpose(LAST, 4, n, 1)
            pe.wait_ge(avg_ready, 1)
            for k in range(2):
                last = mm(bS[1][:, 0:EMB], avg[:, k:k + 1].to_broadcast([128, 128]), ws[:, k, :], k == 0, k == 1)
            last.then_inc(c_ready, 1)
            value(LAST, 3, n)
            project(LAST, 0, WCH)

            def project_b(i, c0, c1):
                if c0 == 0 and i == 2:
                    pe.wait_ge(j_used, NBATCH)
                if c0 == 0 and i == 0:
                    pe.wait_ge(o_used, 4 * NBATCH)
                    pe.wait_ge(e_used, 4 * NBATCH)
                for c in range(c0, c1):
                    last = mm((bO[0], bO[1], bJ)[i][0:BP, 0:EMB], oTB[:, c, i * BP:(i + 1) * BP], wo_sb[:, c, :],
                              c == 0, c == WCH - 1)
                if c1 == WCH:
                    last.then_inc(jb_ready, 1)

            def logits(B):
                for j in range(B * NBATCH, SLOTS if B else NBATCH):
                    if B or j % 4 == 0:
                        pe.wait_ge(nT_ready, 2 * (j // 4) + 2)
                    n, c = (BP, NBATCH * 128 + (j - NBATCH) * BP) if B else (128, j * 128)
                    for k in range(2):
                        last = mm(bE[0:n, j * EXP:(j + 1) * EXP], nT[:, k, c:c + n], wr_sb[:, k, :], k == 0, k == 1)
                last.then_inc(lg_ready, 1)

            tri = mat[:, M_TRI, :]

            def batch_rank(B):
                pe.wait_ge(oh_ready, B + 1)
                if not B:
                    mm(bO[0][:, 0:NBATCH * EXP], tri, oh[:, 0:NBATCH, :].rearrange("p j x -> p (j x)")).then_inc(rank_ready, 1)
                    return
                for i in range(NBT):
                    o = bO[1][0:BP, i * EXP:(i + 1) * EXP]
                    mm(o, mat[:, M_BB + i, 0:BP], oh[:, NBATCH + i, :], True, False)
                    if i:
                        mm(o, mat[:, M_BX + i - 1, 0:BP], oh[:, NBATCH + i - 1, :], False, False)
                    own = [m for m, (ii, b) in enumerate(PAIRS) if ii == i]
                    for m in own:
                        last = mm(o, mat[:, M_BA + m, 0:BP], oh[:, PAIRS[m][1], :], False, m == own[-1])
                last.then_inc(rank_ready, 1)

            def expert_rank(B):
                pe.wait_ge(kp_ready, B + 1)
                gk, end = bT[0], (SLOTS + 1) * EXP
                lo, hi = (NBATCH, SLOTS) if B else (0, NBATCH)
                mm(gk[:, lo * EXP:hi * EXP], tri, kp[:, lo:hi, :].rearrange("p j x -> p (j x)"), not B, False)
                for j in range(lo, hi):
                    last = mm(gk[:, (j + 1) * EXP:end].rearrange("p (j x) -> p j x", x=EXP), ones[:, :],
                              kp[:, j, :].unsqueeze(1).to_broadcast([128, SLOTS - j, EXP]), False, j == SLOTS - 1)
                last.then_inc(grank_ready, 1)

            project_b(0, 0, WCH)
            pe.wait_ge(t_used, TPB * NBATCH)
            pe.wait_ge(c_used, 1)
            for g in range(2):
                pe.wait_ge(norm_ready, g + 1)
                for k in range(2):
                    bank = (bS, bT)[g][k]
                    for j in range(4):
                        if g and j == 3:
                            pe.wait_ge(norm_ready, 2)
                        last = nc.tensor.transpose(bank[0:EC, j * 128:(j + 1) * 128], norm[:, 4 * g + j, k * EC:(k + 1) * EC], ident)
                    last.then_inc(nT_sum, 1)
            pe.wait_ge(e_used, 4 * NBATCH)
            project_b(1, 0, 9)
            logits(0)
            project_b(1, 9, WCH)
            pe.wait_ge(mat_ready, 1)
            batch_rank(0)
            project_b(2, 0, 9)
            expert_rank(0)
            project_b(2, 9, WCH)
            pe.wait_ge(norm_ready, len(GROUPS))
            for k in range(2):
                for i in range(NBT):
                    last = nc.tensor.transpose(bS[k][0:EC, i * BP:(i + 1) * BP], norm[0:BP, NBATCH + i, k * EC:(k + 1) * EC], ident[0:BP, 0:BP])
                last.then_inc(nT_sum, 1)
            logits(1)
            batch_rank(1)
            expert_rank(1)

            pe.wait_ge(tab_ready, 1)
            nb = pe.value_load(nbI[0:1, 0:1], min_val=1, max_val=MAXB)

            def x_transpose(q, at):
                pe.wait_ge(x_in[q], at)
                for k in range(2):
                    last = nc.tensor.transpose(bT[1][0:EC, k * T:(k + 1) * T], xb[q][:, k * EC:(k + 1) * EC], ident)
                last.then_inc(xT_sum, 1)

            x_transpose(0, 16)

            def block_step(i, q):
                b, p, turn = i * XBUF + q, q % 2, (i * 2 + q // 2 + 1) * 16
                pe.wait_ge(xT_ready, b + 1)
                pe.wait_ge(wi_in[p], turn)
                for c in range(FC):
                    bank, cc = (bO[0], c) if c < 4 else (bO[1], c - 4)
                    for k in range(2):
                        last = mm(bank[:, cc * T:(cc + 1) * T], wi_sb[p][:, k, c, :], xT[:, k, :], k == 0, k == 1)
                    if c == 3:
                        last.then_inc(h0_sum, 1)
                last.then_inc(h1_sum, 1)
                x_transpose((q + 1) % XBUF, (i + 1 + (q + 1) // XBUF) * 16)
                pe.wait_ge(wox_in[p], turn)
                pe.wait_ge(h0_ready, b + 1)
                if not (is0(i) and q == 0):
                    pe.wait_ge(y_ready, b)
                for c in range(FC):
                    if c == 4:
                        pe.wait_ge(h1_ready, b + 1)
                    last = mm(bE[:, 0:EMB], hT[:, c, :], wo_x[p][:, c, :], c == 0, c == FC - 1)
                last.then_inc(y_sum, 1)

            for_blocks(pe, nb, block_step)


def constants():
    p = np.arange(128)
    c = np.zeros((128, NCST), np.float32)
    c[:, C_ID:C_ID + 128] = np.eye(128)
    c[:, C_MA:C_MA + SA] = np.where(p[None, :] > p[:, None], NEG, 0)
    c[:, C_MB:C_MB + SEQ] = np.where(np.arange(SEQ)[None, :] > SA + p[:, None] % SB, NEG, 0)
    c[:, C_NA] = 1.0 / (p + 1)
    c[:, C_NB] = 1.0 / (SA + p % SB + 1)
    for i in range(NBT):
        c[:, C_NBP + i] = -1.0 / (SA + (i * BP + p) % SB + 1)
    d = np.zeros((128, C_MAT), np.float32)
    d[:, C_EM:C_EM + EXP] = np.arange(EXP) - EXP
    for j in range(NBATCH):
        d[:, C_ROW + j] = j * SEQ + p
    for i in range(NBT):
        t = i * BP + p
        d[:, C_ROW + NBATCH + i] = np.where(p < BP, t // SB * SEQ + SA + t % SB, BIG)
    d[:, C_BI:C_BI + MAXB] = np.arange(MAXB) * T
    m = np.zeros((128, NMAT, 128), np.float32)
    m[:, M_TRI] = p[:, None] < p[None, :]

    def batch(i):
        return np.where(p < BP, (i * BP + p) // SB, -1 - i)
    for i in range(NBT):
        same = batch(i)[:, None] == batch(i)[None, :]
        m[:, M_BB + i] = same & (p[:, None] < p[None, :]) & (p[:, None] < BP)
        if i:
            m[:, M_BX + i - 1] = batch(i - 1)[:, None] == batch(i)[None, :]
    for n, (i, b) in enumerate(PAIRS):
        m[:, M_BA + n] = (batch(i) == b)[None, :]
    return c, np.concatenate([d, m.reshape(128, NMAT * 128)], 1)


def kernel(**inputs):
    import concourse.bacc as bacc
    from concourse.bass_utils import run_bass_kernel_spmd as run

    a = {k: np.asarray(v) for k, v in inputs.items()}
    con = np.ascontiguousarray
    P, G = 16, 6
    x = a["x"].reshape(NBATCH, 3, G, P, G, P).transpose(0, 1, 3, 5, 2, 4).reshape(NBATCH, IMG, 768)
    pat = con(x.reshape(NBATCH * IMG, 6, 128).transpose(2, 1, 0))
    projw = con(a["L0_tok_proj_w"].reshape(EMB, 6, 128).transpose(2, 1, 0))
    txt, cut = a["txt"], SA - IMG
    tail = txt[:, cut:]
    ln = a["L0_attn_ln_w"]
    wo4 = a["L0_attn_W_o"].reshape(EMB, HEADS, EMB).transpose(1, 2, 0)
    wo_attn = np.concatenate([wo4[:, :E0], wo4[:, E0:].reshape(HEADS // 2, 128, EMB)], 0).transpose(1, 0, 2)
    cst, cst2 = constants()
    arrays = {
        "patches": pat, "projw": projw,
        "projb": con(np.broadcast_to(a["L0_tok_proj_b"], (IMG, EMB))), "pos": con(a["L0_tok_pos_embed"][0]),
        "txtA": con(txt[:, :cut].transpose(1, 0, 2)), "txtB": con(tail.transpose(1, 0, 2)),
        "txtBp": con(tail.reshape(NBT, BP, EMB).transpose(1, 0, 2)),
        "wqk": con(a["L0_attn_W_qk"].reshape(HEADS, 2, EC).transpose(2, 1, 0)),
        "lnw": con(ln.reshape(2, EC).T), "lnc": con(np.stack([ln[:E0], np.concatenate([ln[E0:], ln[E0:]])], 1)),
        "wte": a["L0_attn_wte"], "wo_attn": con(wo_attn),
        "flnw": con(np.broadcast_to(a["L0_ffn_ln_w"], (128, EMB))),
        "wrt": con(a["L0_ffn_w_router"].reshape(2, EC, EXP).transpose(1, 0, 2)),
        "wi": con(a["L0_ffn_wi"].reshape(EXP, 2, EC, FC, 128).transpose(0, 2, 1, 3, 4)),
        "wo": con(a["L0_ffn_wo"].reshape(EXP, FC, 128, EMB).transpose(0, 2, 1, 3)),
        "cst": cst, "cst2": cst2,
    }
    nc = bacc.Bacc("TRN2", target_bir_lowering=False, num_devices=1)
    args = [nc.dram_tensor("in_" + k, v.shape, mybir.dt.from_np(v.dtype), kind="ExternalInput").ap() for k, v in arrays.items()]
    out = nc.dram_tensor("out", (TOK, EMB), mybir.dt.float32, kind="ExternalOutput").ap()
    program(nc, *args, out)
    r = run(nc, [{"in_" + k: v for k, v in arrays.items()}], core_ids=[0])
    return r.results[0]["out"].reshape(NBATCH, SEQ, EMB)
```

```python
import numpy as np
import concourse.bass as bass
from concourse import mybir
from contextlib import ExitStack

NBATCH, SEQ, EMB, HEADS = 8, 164, 192, 12
IMG = 36
SA = 128
SB = SEQ - SA
EC = 96
E0, E1 = 128, EMB - 128
HB = 3
NG = HEADS // HB
WCH = HEADS + HEADS // 2
NBT = 3
BP = NBATCH * SB // NBT
SLOTS = NBATCH + NBT
EXP, FF, CAP, T = 16, 768, 64, 112
FC = FF // 128
TOK = NBATCH * SEQ
MAXB = EXP + (TOK - EXP) // T
MINB = NBATCH * CAP // T
VOCAB = 50257
WR = 14
WCHUNKS = VOCAB // 128 // WR
WTAIL = VOCAB - 128 * WR * WCHUNKS
WBUF = 2
XBUF = 4
XROWS = (MAXB + 1) * T
ZB = 4
DIV = -(-(1 << 20) // T)
assert (TOK + T) * DIV < 1 << 24 and (TOK + T) * (DIV * T - (1 << 20)) < 1 << 20 and (MAXB + 1) % ZB == 0
D_X, D_BASE, D_RP, D_ROW, DW = 0, EMB, 2 * EMB, 2 * EMB + 1, 2 * EMB + 2
BIG = 1 << 20

C_ID, C_MA, C_MB, C_NA, C_NB, C_NBP = 0, 128, 256, 256 + SEQ, 257 + SEQ, 258 + SEQ
NCST = C_NBP + NBT
C_EM, C_ROW, C_BI = 0, EXP, EXP + SLOTS
C_MAT = C_BI + 1
PAIRS = [(i, b) for i in range(NBT) for b in range(NBATCH) if b * SB < (i + 1) * BP and (b + 1) * SB > i * BP]
M_TRI, M_BB, M_BX, M_BA = 0, 1, 4, 6
NMAT = M_BA + len(PAIRS)
NCST2 = C_MAT + NMAT * 128
NEG = -1e30
GROUPS = [(0, NBATCH - 1, 128), (NBATCH - 1, NBATCH, 128), (NBATCH, SLOTS - 1, BP), (SLOTS - 1, SLOTS, BP)]


def program(nc, patches, projw, projb, pos, txtA, txtB, txtBp, wqk, lnw, lnc, wte, wo_attn,
            flnw, wrt, wi, wo, cst_d, cst2_d, out):
    f32, f32r, bf16, i32 = mybir.dt.float32, mybir.dt.float32r, mybir.dt.bfloat16, mybir.dt.int32
    ALU, ACT = mybir.AluOpType, mybir.ActivationFunctionType
    X = mybir.AxisListType.X
    ds = bass.ds

    xd = nc.dram_tensor("dispatched", (XROWS + 3 * T, DW), f32).ap()

    ctx = ExitStack()
    with ctx:
        def sb(name, shape, dt=f32):
            return ctx.enter_context(nc.sbuf_tensor(name, shape, dt))

        def pb(name):
            return ctx.enter_context(nc.psum_tensor(name, [128, 512], f32))

        def sem(name):
            return ctx.enter_context(nc.semaphore(name))

        cst = sb("cst", [128, NCST])
        cst2 = sb("cst2", [128, C_MAT])
        mat = sb("mat", [128, NMAT, 128], bf16)
        idb, maskA, maskB = sb("idb", [128, 128], bf16), sb("maskA", [128, SA], bf16), sb("maskB", [128, SEQ], bf16)
        ones = sb("ones", [128, 128], bf16)
        ident = cst[:, C_ID:C_ID + 128]
        H = sb("H", [128, SLOTS, EMB])
        hB = sb("hB", [SB, NBATCH, EMB])
        woH, woL = sb("woH", [128, WCH, EMB], f32r), sb("woL", [128, WCH, EMB], f32r)
        ws = sb("ws", [128, 2, EMB])
        lncol = sb("lncol", [128, 2])
        flnb = sb("flnb", [128, EMB])
        wr_sb = sb("wr_sb", [EC, 2, EXP])
        rstd = sb("rstd", [128, 2, NBATCH])
        nmr = sb("nmr", [128, 2, NBATCH])
        zA, zB = sb("zA", [128, EMB]), sb("zB", [SB, EMB])
        VW = E0 + 3 * E1
        vA, vB = ([sb(f"v{t}{x}", [n, VW], f32r) for x in "HL"] for t, n in (("A", 128), ("B", SB)))
        zT = sb("zT", [EC, 2, SEQ])
        w2 = sb("w2", [EC, 2, HEADS])
        Awf = sb("AwA", [128, 2 * HEADS * SA])
        AwA, AwB = Awf[0:EC, :].rearrange("p (k h s) -> p k h s", k=2, h=HEADS), sb("AwB", [EC, 2, HEADS, SB])
        PA, PB = sb("PA", [128, HEADS, SA]), sb("PB", [HB * SB, NG, SEQ])
        PTA = [sb(f"PTA{x}", [128, HEADS, SA], f32r) for x in "HL"]
        PTB0, PTB1 = ([sb(f"PTB{i}{x}", [n, HEADS, SB], f32r) for x in "HL"] for i, n in ((0, 128), (1, SB)))
        negmax, lsum, rn = sb("negmax", [128, 16]), sb("lsum", [128, 16]), sb("rn", [128, 16])
        rinv = sb("rinv", [128, 16])
        oTA = [sb(f"oTA{x}", [128, WCH, SA], f32r) for x in "HL"]
        oTB = [sb(f"oTB{x}", [128, WCH, NBATCH * SB], f32r) for x in "HL"]
        wbuf = sb("wbuf", [128, WBUF * WR * EMB])
        wchunk = [wbuf[:, i * WR * EMB:(i + 1) * WR * EMB] for i in range(WBUF)]
        WIN, WON = 2 * FC * 128, FC * EMB
        wi_sb = [wbuf[0:EC, p * WIN:(p + 1) * WIN].rearrange("p (k c m) -> p k c m", k=2, c=FC) for p in range(2)]
        wo_x = [wbuf[:, 2 * WIN + p * WON:2 * WIN + (p + 1) * WON].rearrange("p (c e) -> p c e", c=FC) for p in range(2)]
        wtail = sb("wtail", [WTAIL, EMB])
        cS, cN = sb("cS", [128, EMB]), sb("cN", [128, EMB])
        pat_sb = Awf[:, 0:6 * 288].rearrange("p (k n) -> p k n", k=6)
        pw_sb = Awf[:, 1728:1728 + 6 * EMB].rearrange("p (k e) -> p k e", k=6)
        paf = PA[:, :, :].rearrange("p h s -> p (h s)")
        embT = paf[0:EC, 0:576].rearrange("p (k n) -> p k n", k=2)
        posb, pbb = cS[0:IMG, :], cN[0:IMG, :]
        st6 = sb("st6", [128, 2, NBATCH, 6])
        mv = sb("mv", [128, 2, NBATCH, 2])
        nT = Awf[0:EC, 0:2 * TOK].rearrange("p (k n) -> p k n", k=2)
        pay = sb("pay", [128, SLOTS, DW])
        payf = pay[:, :, :].rearrange("p j w -> p (j w)")
        wo32 = payf[:, 0:WCH * EMB].rearrange("p (c e) -> p c e", c=WCH)
        mat32 = payf[:, 0:NMAT * 128]
        norm, base = pay[:, :, D_X:D_X + EMB], pay[:, :, D_BASE:D_BASE + EMB]
        drow = H[:, :, :]
        xb = [Awf[0:T, q * DW:(q + 1) * DW] for q in range(XBUF)]
        ysb = [paf[0:T, p * EMB:(p + 1) * EMB] for p in range(2)]
        yrow = [sb(f"yrow{p}", [T, 1], i32) for p in range(2)]
        xT = paf[0:EC, 2 * EMB:2 * EMB + 2 * T].rearrange("p (k n) -> p k n", k=2)
        hT = Awf[:, XBUF * DW:XBUF * DW + FC * T].rearrange("p (c n) -> p c n", c=FC)
        fst = sb("fst", [128, SLOTS, 6])
        fmv = sb("fmv", [128, SLOTS, 2])
        var = sb("var", [128, 2, SLOTS])
        rsq, nwt = sb("rsq", [128, 2, SLOTS]), sb("nwt", [128, 2, SLOTS])
        rsq1, nmb = sb("rsq1", [128, SLOTS]), sb("nmb", [128, SLOTS])
        lmax, lidx, lsm, kept, drop, posF, dropF = (sb(n, [128, SLOTS]) for n in
            ("lmax", "lidx", "lsm", "kept", "drop", "posF", "dropF"))
        lg, lx = (sb(n, [128, SLOTS, EXP]) for n in ("lg", "lx"))
        l1, l2 = (Awf[:, 2 * TOK + i * SLOTS * EXP:2 * TOK + (i + 1) * SLOTS * EXP].rearrange("p (j x) -> p j x", j=SLOTS)
                  for i in range(2))
        oh, kp = sb("oh", [128, SLOTS, EXP], bf16), sb("kp", [128, SLOTS, EXP], bf16)
        capI, capF, cum, first = sb("capI", [128, 2, EXP], i32), sb("capF", [128, 2, EXP]), sb("cum", [128, 2, EXP]), sb("first", [128, 2, EXP])
        oneX = sb("oneX", [128, EXP])
        capB = sb("capB", [128, EXP])
        bex, beC = sb("bex", [128, 2 * EXP]), sb("beC", [128, 1])
        beI = sb("beI", [1, MAXB + 4], i32)
        nbI, be0 = sb("nbI", [1, 2], i32), sb("be0", [1, 1], i32)
        posI, dropI = sb("posI", [128, SLOTS], i32), sb("dropI", [128, SLOTS], i32)
        avg = sb("avg", [128, 2])
        zeros = sb("zeros", [128, DW])
        ln96, one = sb("ln96", [EC, 2]), sb("one", [128, 1])
        mhalf = sb("mhalf", [128, 32])
        wsum = sb("wsum", [128, EMB])
        nwz = sb("nwz", [128, 2, NBATCH])

        bS = [pb("bS0"), pb("bS1")]
        bT = [pb("bT0"), pb("bT1")]
        bO = [pb("bO0"), pb("bO1")]
        bE = pb("bE")
        bJ = pb("bJ")

        cst_in, cst2_in, mat_in, pat_in, txt_in, small_in, late_in, wo_in = (sem(n) for n in
            ("cst_in", "cst2_in", "mat_in", "pat_in", "txt_in", "small_in", "late_in", "wo_in"))
        wte_in = [sem(f"wte_in{i}") for i in range(WBUF)]
        wte_first = sem("wte_first")
        wtail_in, wte_added, dve_step, pool_step = (sem(n) for n in ("wtail_in", "wte_added", "dve_step", "pool_step"))
        emb_ready, embT_ready, tok_ready, tok_added = (sem(n) for n in ("emb_ready", "embT_ready", "tok_ready", "tok_added"))
        z_ready, v_ready, aw_ready, aw0_ready = sem("z_ready"), sem("v_ready"), sem("aw_ready"), sem("aw0_ready")
        bf_ready, mat_ready = sem("bf_ready"), sem("mat_ready")
        score_ready, max_ready, exp_ready, rn_ready, p_ready = (sem(n) for n in
            ("score_ready", "max_ready", "exp_ready", "rn_ready", "p_ready"))
        t_ready, t_used = sem("t_ready"), sem("t_used")
        o_ready, o_used, e_ready, e_used = (sem(n) for n in ("o_ready", "o_used", "e_ready", "e_used"))
        j_ready, j_used, jb_ready = sem("j_ready"), sem("j_used"), sem("jb_ready")
        acc_ready, avg_sum, avg_ready, c_ready, c_used = (sem(n) for n in ("acc_ready", "avg_sum", "avg_ready", "c_ready", "c_used"))
        tl_used, ol_used, eh_ready, vl_ready, vz_ready = (sem(n) for n in ("tl_used", "ol_used", "eh_ready", "vl_ready", "vz_ready"))
        woh_ready, wol_ready, pay_free = sem("woh_ready"), sem("wol_ready"), sem("pay_free")
        rinv_ready, w2_ready = sem("rinv_ready"), sem("w2_ready")
        var_ready, pow_ready, basepar_ready, base_ready = (sem(n) for n in ("var_ready", "pow_ready", "basepar_ready", "base_ready"))
        norm_ready, nT_sum, nT_ready, lg_ready, le_ready, lx_ready = (sem(n) for n in
            ("norm_ready", "nT_sum", "nT_ready", "lg_ready", "le_ready", "lx_ready"))
        oh_ready, rank_ready, kp_ready, grank_ready, pos_ready, tab_ready = (sem(n) for n in
            ("oh_ready", "rank_ready", "kp_ready", "grank_ready", "pos_ready", "tab_ready"))
        jb_used, hc_ready = sem("jb_used"), sem("hc_ready")
        be_ready, be_row, be0_ready = sem("be_ready"), sem("be_row"), sem("be0_ready")
        ohz_ready, zero_ready, zero_done, scattered = sem("ohz_ready"), sem("zero_ready"), sem("zero_done"), sem("scattered")
        wi_in, wox_in = ([sem(f"{n}{p}") for p in range(2)] for n in ("wi_in", "wox_in"))
        x_in = [sem(f"x_in{q}") for q in range(XBUF)]
        xT_sum, xT_ready = sem("xT_sum"), sem("xT_ready")
        h0_sum, h1_sum, h0_ready, h1_ready, y_sum, y_ready = (sem(n) for n in
            ("h0_sum", "h1_sum", "h0_ready", "h1_ready", "y_sum", "y_ready"))
        y_out = [sem(f"y_out{p}") for p in range(2)]
        drop_ready, drop_out, pool_seq, ones_ready = (sem(n) for n in ("drop_ready", "drop_out", "pool_seq", "ones_ready"))
        even_stored, odd_stored = sem("even_stored"), sem("odd_stored")

        def is0(b):
            return isinstance(b, int) and b == 0

        def for_blocks(eng, nb, step):
            for q in range(XBUF):
                step(0, q)
            with eng.Fori(1, (MAXB + XBUF - 1) // XBUF) as i:
                for q in range(XBUF):
                    with eng.If(i * XBUF + q < nb):
                        step(i, q)

        JBANK = (bJ, bJ, bO[0])

        def pt_round(q, x, bank):
            if q < 3:
                return PTA[x][:, 4 * q:4 * q + 4, :], bank[:, 0:4 * SA].rearrange("p (h s) -> p h s", h=4)
            if q == 3:
                return PTB0[x][:, :, :], bank[:, 0:HEADS * SB].rearrange("p (h s) -> p h s", h=HEADS)
            return PTB1[x][:, :, :], bank[0:SB, 0:HEADS * SB].rearrange("p (h s) -> p h s", h=HEADS)

        def o_round(b, g, x):
            if g < 3:
                return oTA[x][:, 4 * g:4 * g + 4, :], bO[g % 2][:, 0:4 * SA].rearrange("p (h s) -> p h s", h=4)
            return oTB[x][:, 0:HEADS, ds(b * SB, SB)], bO[1][:, 0:HEADS * SB].rearrange("p (h s) -> p h s", h=HEADS)

        def e_round(b, g, x):
            if g < 3:
                return oTA[x][:, HEADS + 2 * g:HEADS + 2 * g + 2, :], bE[:, 0:2 * SA].rearrange("p (h s) -> p h s", h=2)
            return oTB[x][:, HEADS:WCH, ds(b * SB, SB)], bE[:, 0:6 * SB].rearrange("p (h s) -> p h s", h=6)

        wv = wte[0:128 * WR * WCHUNKS, :].rearrange("(p c r) e -> p c (r e)", p=128, c=WCHUNKS)

        block = ctx.enter_context(nc.Block())
        SPR = 5
        TPB = 6
        LAST = NBATCH - 1
        BANK = (1, 0, 0, 1, 0)

        def t_before(b, q):
            if q == "z":
                return TPB * b + 3
            return TPB * b + 1 + q + (q >= 2 and not (isinstance(b, int) and b == LAST))



        @block.sync
        def _(sp):
            sp.dma_start(pw_sb, projw).then_inc(pat_in, 16)
            sp.dma_start(pat_sb, patches).then_inc(pat_in, 16)
            sp.dma_start(H[IMG:128, 0:NBATCH, :], txtA).then_inc(txt_in, 16)
            sp.wait_ge(small_in, 16 * 4)
            sp.wait_ge(cst_in, 16)
            sp.wait_ge(txt_in, 32)
            sp.dma_start(wo32, wo_attn).then_inc(wo_in, 16)
            for s in range(WBUF):
                sp.dma_start(wchunk[s], wv[:, s, :]).then_inc(wte_first, 16)
            sp.dma_start(H[0:BP, NBATCH:SLOTS, :], txtBp).then_inc(late_in, 16)
            sp.dma_start(cst2[:], cst2_d[:, 0:C_MAT]).then_inc(cst2_in, 16)
            sp.dma_start(wtail[:], wte[VOCAB - WTAIL:VOCAB, :]).then_inc(wtail_in, 16)
            sp.wait_ge(zero_ready, 1)
            for n in range(XROWS // (ZB * T)):
                sp.dma_start(xd[n * ZB * T:(n + 1) * ZB * T, :].rearrange("(p n) e -> p n e", n=ZB),
                             zeros[0:T, :].unsqueeze(1).to_broadcast([T, ZB, DW])).then_inc(zero_done, 16)
            sp.wait_ge(pay_free, 1)
            sp.dma_start(mat32, cst2_d[:, C_MAT:NCST2]).then_inc(mat_in, 16)
            sp.wait_ge(acc_ready, 1)
            sp.wait_ge(be0_ready, 1)

            def weights(b, p, used):
                src = be0[0:1, 0:1] if is0(b) else beI[0:1, ds(b, 1)]
                e = sp.value_load(src, min_val=0, max_val=EXP - 1)
                if used is not None:
                    sp.wait_ge(h1_sum, used)
                sp.dma_start(wi_sb[p], wi[ds(e, 1)].rearrange("x p k c m -> (x p) k c m")).then_inc(wi_in[p], 16)
                if used is not None:
                    sp.wait_ge(y_sum, used)
                sp.dma_start(wo_x[p], wo[ds(e, 1)].rearrange("x p c e -> (x p) c e")).then_inc(wox_in[p], 16)

            def rows(b, q):
                sp.dma_start(xb[q], xd[ds(b * T, T), :]).then_inc(x_in[q], 16)

            weights(0, 0, None)
            sp.wait_ge(tab_ready, 1)
            nb = sp.value_load(nbI[0:1, 0:1], min_val=MINB, max_val=MAXB)
            sp.wait_ge(scattered, 16 * SLOTS)
            rows(0, 0)
            rows(1, 1)
            weights(1, 1, None)

            def next_rows(b, q):
                if isinstance(b, int) and b < 2:
                    pass
                else:
                    sp.wait_ge(y_ready, b - 1)
                rows(b + 2, (q + 2) % XBUF)

            def block_loads(i, q):
                b = i * XBUF + q
                if isinstance(b, int) and b + 1 < MINB:
                    next_rows(b, q)
                else:
                    with sp.If(b + 1 < nb):
                        next_rows(b, q)
                if isinstance(b, int) and b + 2 < MINB:
                    weights(b + 2, q % 2, b + 1)
                else:
                    with sp.If(b + 2 < nb):
                        weights(b + 2, q % 2, b + 1)
            for q in range(XBUF):
                block_loads(0, q)
            with sp.Fori(1, (MAXB + XBUF - 1) // XBUF) as i:
                for q in range(XBUF):
                    block_loads(i, q)
            sp.wait_ge(y_out[0], (nb + 1) // 2 * 16)
            sp.sem_inc(even_stored, 1)
            sp.wait_ge(y_out[1], nb // 2 * 16)
            sp.sem_inc(odd_stored, 1)
            sp.wait_ge(drop_out, 16 * SLOTS)

        @block.gpsimd
        def _(pool):
            nc.gpsimd.memset(mhalf[:], -0.5).then_inc(pool_step, 1)
            nc.gpsimd.memset(oh[:, :, :], 0.0).then_inc(ohz_ready, 1)
            nc.gpsimd.memset(kp[:, :, :], 0.0).then_inc(ohz_ready, 1)
            for v in vA + vB:
                for c in (E0, E0 + 2 * E1):
                    nc.gpsimd.memset(v[:, c:c + E1].bitcast(f32), 0.0).then_inc(vz_ready, 1)
            nc.gpsimd.memset(zeros[:], 0.0).then_inc(pool_step, 1)
            pool.wait_ge(pool_step, 2)
            nc.gpsimd.memset(zeros[:, D_ROW:D_ROW + 1], float(BIG)).then_inc(zero_ready, 1)

            def rsqrt(y, x, k):
                pool.wait_ge(var_ready, k)
                nc.gpsimd.tensor_tensor(y, x, mhalf[0:y.shape[0], 0:x.shape[1] * x.shape[2]].rearrange("p (a b) -> p a b", a=2),
                                        ALU.pow).then_inc(pow_ready, 1)

            rsqrt(rstd[:, :, 0:2], nmr[:, :, 0:2], 1)

            def weigh(b, n, ks, gs=range(4)):
                pool.wait_ge(t_used, n)
                for g in gs:
                    hs, ss, dst = (slice(4 * g, 4 * g + 4), slice(0, SA), AwA) if g < 3 else (slice(0, HEADS), slice(SA, SEQ), AwB)
                    for k in ks:
                        o = dst[:, k, hs, :]
                        nc.gpsimd.tensor_tensor(o, zT[:, k, ss].unsqueeze(1).to_broadcast(list(o.shape)),
                                                w2[:, k, hs].unsqueeze(2).to_broadcast(list(o.shape)),
                                                ALU.mult).then_inc(aw_ready, 1)

            def add_wte(c, s, before):
                if is0(before):
                    pool.wait_ge(wte_first, 16 * WBUF)
                else:
                    pool.wait_ge(wte_in[s], 16 * before)
                    pool.sem_inc(pool_seq, 1)
                pool.dma_start(wchunk[s], wv[:, ds(c, 1), :].rearrange("p c x -> p (c x)"), accum_op=ALU.add,
                               max_dma_last_dim=WR * EMB * 4 // 2).then_inc(wte_in[s], 16)

            def normalise(b, rounds=range(SPR)):
                for r in rounds:
                    pool.wait_ge(rn_ready, SPR * b + r + 1)
                    if r < 3:
                        t, q = PA[:, 4 * r:4 * r + 4, :], rn[:, 4 * r:4 * r + 4]
                    else:
                        q0 = 2 * (r - 3)
                        t, q = PB[:, q0:q0 + 2, :], rn[0:HB * SB, 12 + q0:14 + q0]
                    nc.gpsimd.tensor_tensor(t, t, q.unsqueeze(2).to_broadcast(list(t.shape)), ALU.mult).then_inc(p_ready, 1)

            pool.wait_ge(w2_ready, 1)
            weigh(0, 1, (1,))
            add_wte(2, 0, 0)
            add_wte(3, 1, 0)
            normalise(0, range(3))
            rsqrt(rstd[:, :, 2:NBATCH], nmr[:, :, 2:NBATCH], 2)

            def iteration(b, more):
                normalise(b, range(3, SPR))
                for k in range(4):
                    if more:
                        add_wte(4 * b + 4 + k, k % 2, 2 * b + 1 + k // 2)
                    if k == 0:
                        weigh(b + 1, t_before(b, "z") + 1, (0, 1), (0, 1))
                    elif k == 1:
                        weigh(b + 1, t_before(b, "z") + 1, (0, 1), (2,))
                        normalise(b + 1, (0,))
                    elif k == 2:
                        normalise(b + 1, (1,))
                        weigh(b + 1, t_before(b, "z") + 1, (0, 1), (3,))
                    else:
                        normalise(b + 1, (2,))

            with pool.Fori(0, NBATCH - 2) as b:
                iteration(b, True)
            iteration(NBATCH - 2, False)
            normalise(LAST, range(3, SPR))

            j0, j1, n = GROUPS[0]
            pool.wait_ge(c_used, 1)
            pool.wait_ge(j_used, LAST)
            nc.gpsimd.tensor_tensor(H[:, j0:j1, :], H[:, j0:j1, :], cN[:, :].unsqueeze(1).to_broadcast([128, j1 - j0, EMB]),
                                    ALU.add).then_inc(hc_ready, 1)
            for g, (j0, j1, n) in enumerate(GROUPS):
                rsqrt(rsq[0:n, :, j0:j1], var[0:n, :, j0:j1], 3 + g)

            def scatter(j):
                n = 128 if j < NBATCH else BP
                nc.gpsimd.indirect_dma_start(out=xd[:, :], out_offset=bass.IndirectOffsetOnAxis(ap=posI[0:n, j:j + 1], axis=0),
                                             in_=pay[0:n, j, :], in_offset=None, bounds_check=XROWS - 1,
                                             oob_is_err=False).then_inc(scattered, 16)

            def to_out(rows, idx, s):
                nc.gpsimd.indirect_dma_start(out=out[:, :], out_offset=bass.IndirectOffsetOnAxis(ap=idx, axis=0),
                                             in_=rows, in_offset=None, bounds_check=TOK - 1, oob_is_err=False).then_inc(s, 16)

            pool.wait_ge(zero_done, 16 * (XROWS // (ZB * T)))
            pool.wait_ge(pos_ready, 1)
            pool.wait_ge(base_ready, SLOTS - 1)
            for j in range(NBATCH):
                scatter(j)
            pool.wait_ge(pos_ready, 2)
            pool.wait_ge(base_ready, SLOTS)
            for j in range(NBATCH, SLOTS):
                scatter(j)
            pool.wait_ge(drop_ready, 1)
            for j in range(SLOTS):
                n = 128 if j < NBATCH else BP
                to_out(drow[0:n, j, :], dropI[0:n, j:j + 1], drop_out)
            pool.wait_ge(tab_ready, 1)
            nb = pool.value_load(nbI[0:1, 0:1], min_val=MINB, max_val=MAXB)

            def block_step(i, q):
                pool.wait_ge(y_ready, i * XBUF + q + 1)
                pool.sem_inc(pool_seq, 1)
                to_out(ysb[q % 2], yrow[q % 2][:, 0:1], y_out[q % 2])

            for_blocks(pool, nb, block_step)

        @block.scalar
        def _(act):
            for dst, src in ((posb, pos), (pbb, projb), (w2[:], wqk), (ln96[:], lnw)):
                act.dma_start(dst, src).then_inc(small_in, 16)
            act.dma_start(cst[:], cst_d).then_inc(cst_in, 16)
            act.dma_start(hB[:], txtB).then_inc(txt_in, 16)
            for dst, src in ((lncol[:], lnc), (flnb[:], flnw), (wr_sb[:], wrt)):
                act.dma_start(dst, src).then_inc(late_in, 16)
            act.wait_ge(cst_in, 16)
            nc.scalar.activation(idb[:], ident, ACT.Copy).then_inc(bf_ready, 1)
            nc.scalar.activation(maskA[:], cst[:, C_MA:C_MA + SA], ACT.Copy).then_inc(bf_ready, 1)
            nc.scalar.activation(maskB[:], cst[:, C_MB:C_MB + SEQ], ACT.Copy).then_inc(bf_ready, 1)
            for k in range(2):
                act.wait_ge(emb_ready, k + 1)
                nc.scalar.activation(embT[:, k, :], bO[k][0:EC, 0:NBATCH * IMG], ACT.Copy).then_inc(embT_ready, 1)

            act.wait_ge(wo_in, 16)
            nc.scalar.activation(woH[:, :, :], wo32, ACT.Copy).then_inc(woh_ready, 1)

            def zt_copy(n, par):
                act.wait_ge(t_ready, n)
                nc.scalar.activation(zT[:, :, :], bT[par][0:EC, 0:2 * SEQ].rearrange("p (k s) -> p k s", k=2),
                                     ACT.Copy).then_inc(t_used, 1)

            def values(b):
                act.wait_ge(z_ready, 2 * (b + 1))
                if not is0(b):
                    act.wait_ge(e_ready, 4 * b)
                for v, z in ((vA, zA), (vB, zB)):
                    nc.scalar.activation(v[0][:, 0:E0], z[:, 0:E0], ACT.Copy)
                    nc.scalar.activation(v[0][:, E0 + E1:E0 + 2 * E1], z[:, E0:EMB], ACT.Copy).then_inc(v_ready, 1)

            def exps(b, rounds):
                for r in rounds:
                    act.wait_ge(max_ready, SPR * b + r + 1)
                    bank = bS[r % 2]
                    if r < 3:
                        for j in range(4):
                            h = 4 * r + j
                            last = nc.scalar.activation(PA[:, h, :], bank[:, j * SA:(j + 1) * SA], ACT.Exp,
                                                        bias=negmax[:, h:h + 1], accum_out=lsum[:, h:h + 1])
                    else:
                        for j in range(2):
                            q = 2 * (r - 3) + j
                            last = nc.scalar.activation(PB[:, q, :], bank[0:HB * SB, j * SEQ:(j + 1) * SEQ], ACT.Exp,
                                                        bias=negmax[0:HB * SB, 12 + q:13 + q],
                                                        accum_out=lsum[0:HB * SB, 12 + q:13 + q])
                    last.then_inc(exp_ready, 1)

            def t_copy(b, q):
                act.wait_ge(t_ready, t_before(b, q) + 1)
                dst, src = pt_round(q, 0, bT[BANK[q]])
                nc.scalar.activation(dst, src, ACT.Copy).then_inc(t_used, 1)

            def o_copy(b, g):
                act.wait_ge(o_ready, 4 * b + g + 1)
                dst, src = o_round(b, g, 0)
                nc.scalar.activation(dst, src, ACT.Copy, scale=lncol[:, 0:1]).then_inc(o_used, 1)

            def iteration(b, more=True):
                if is0(b):
                    exps(b, range(3, SPR))
                t_copy(b, 0)
                t_copy(b, 1)
                if not is0(b):
                    exps(b, range(3, SPR))
                if more:
                    zt_copy(t_before(b, "z") + 1, 1)
                o_copy(b, 0)
                t_copy(b, 2)
                o_copy(b, 1)
                o_copy(b, 2)
                if more:
                    exps(b + 1, (0,))
                t_copy(b, 3)
                t_copy(b, 4)
                if more:
                    exps(b + 1, (1,))
                o_copy(b, 3)
                if more:
                    values(b + 1)
                    exps(b + 1, (2,))

            zt_copy(1, 0)
            values(0)
            exps(0, range(3))
            act.wait_ge(late_in, 16 * 4)
            iteration(0)
            iteration(1)
            act.wait_ge(mat_in, 16)
            nc.scalar.activation(mat[:, :, :].rearrange("p m s -> p (m s)"), mat32, ACT.Copy).then_inc(mat_ready, 1)
            with act.Fori(2, LAST) as b:
                iteration(b)
            iteration(LAST, False)

            def bases(g):
                act.wait_ge(basepar_ready, g + 1)
                j0, j1, n = GROUPS[g]
                for j in range(j0, j1):
                    nc.scalar.activation(base[0:n, j, :], H[0:n, j, :], ACT.Identity, bias=nmb[0:n, j:j + 1],
                                         scale=rsq1[0:n, j:j + 1]).then_inc(base_ready, 1)

            def nt_copy(done, k, j0, m, n, bank):
                act.wait_ge(nT_sum, done)
                c = min(j0, NBATCH) * 128
                nc.scalar.activation(nT[:, k, c:c + m * n], bank[0:EC, 0:m * n], ACT.Copy).then_inc(nT_ready, 1)

            bases(0)
            for k in range(2):
                nt_copy(k + 1, k, 0, 4, 128, bS[k])
            for k in range(2):
                nt_copy(k + 3, k, 4, 3, 128, bT[k])
            act.wait_ge(nT_sum, 5)
            nc.scalar.activation(nT[:, :, (NBATCH - 1) * 128:NBATCH * 128], bO[1][0:EC, 0:256].rearrange("p (k n) -> p k n", k=2),
                                 ACT.Copy).then_inc(nT_ready, 1)
            bases(1)
            bases(2)
            act.wait_ge(le_ready, 1)
            nc.scalar.activation(lx[:, 0:NBATCH, :], lg[:, 0:NBATCH, :], ACT.Exp).then_inc(lx_ready, 1)
            for k in range(2):
                nt_copy(k + 6, k, NBATCH, NBT, BP, bS[k])
            bases(3)
            act.wait_ge(le_ready, 2)
            nc.scalar.activation(lx[0:BP, NBATCH:SLOTS, :], lg[0:BP, NBATCH:SLOTS, :], ACT.Exp).then_inc(lx_ready, 1)
            act.wait_ge(tab_ready, 1)
            nb = act.value_load(nbI[0:1, 0:1], min_val=MINB, max_val=MAXB)

            def block_step(i, q):
                act.wait_ge(h0_sum, i * XBUF + q + 1)
                nc.scalar.activation(hT[:, 0:4, :], bO[0][:, 0:4 * T].rearrange("p (c n) -> p c n", c=4), ACT.Relu).then_inc(h0_ready, 1)

            for_blocks(act, nb, block_step)

        @block.vector
        def _(dve):
            chain = [0]

            def link(ins):
                chain[0] += 1
                ins.then_inc(dve_step, 1)
                dve.wait_ge(dve_step, chain[0])

            def newton(x, y, t):
                link(nc.vector.tensor_tensor(t, y, y, ALU.mult))
                link(nc.vector.tensor_tensor(t, t, x, ALU.mult))
                link(nc.vector.tensor_scalar(t, t, -0.5, 1.5, ALU.mult, ALU.add))
                link(nc.vector.tensor_tensor(y, y, t, ALU.mult))

            nc.vector.memset(ones[:], 1.0).then_inc(ones_ready, 1)
            nc.vector.memset(one[:], 1.0)
            nc.vector.memset(oneX[:], 1.0)
            link(nc.vector.memset(mv[:, :, :, :].rearrange("p a b c -> p (a b c)"), 1.0))
            dve.wait_ge(small_in, 16 * 4)
            link(nc.vector.tensor_tensor(posb, posb, pbb, ALU.add))
            link(nc.vector.tensor_tensor(w2[:, :, :], w2[:, :, :], ln96[:, :].unsqueeze(2).to_broadcast([EC, 2, HEADS]), ALU.mult))
            link(nc.vector.tensor_tensor(w2[:, :, :], w2[:, :, :], w2[:, :, :], ALU.mult))
            nc.vector.tensor_scalar(w2[:, :, :], w2[:, :, :], float(EMB) ** -0.5, None, ALU.mult).then_inc(w2_ready, 1)
            dve.wait_ge(txt_in, 32)
            eps = 1e-5

            def add_patches(j):
                dve.wait_ge(tok_ready, j + 1)
                bank = (bT[0], bE, bJ, bO[1])[j]
                nc.vector.tensor_tensor(H[0:IMG, 2 * j:2 * j + 2, :],
                                        bank[0:IMG, 0:2 * EMB].rearrange("p (b e) -> p b e", b=2),
                                        posb.unsqueeze(1).to_broadcast([IMG, 2, EMB]), ALU.add).then_inc(tok_added, 1)
                dve.wait_ge(tok_added, j + 1)

            for b in range(NBATCH):
                nc.vector.bn_stats(st6[0:SB, 1, b, :], hB[:, b, :])

            def variances(b0, b1):
                for b in range(b0, b1):
                    last = nc.vector.bn_stats(st6[:, 0, b, :], H[:, b, :])
                link(last)
                for b in range(b0, b1):
                    nc.vector.bn_aggr(mv[:, 0, b, :], st6[:, 0, b, :])
                    last = nc.vector.bn_aggr(mv[0:SB, 1, b, :], st6[0:SB, 1, b, :])
                link(last)
                nc.vector.tensor_scalar(nmr[:, :, b0:b1], mv[:, :, b0:b1, 1], 1.0 + eps, eps * eps, ALU.mult, ALU.add).then_inc(var_ready, 1)

            def factors(b0, b1, k):
                x, y, t = nmr[:, :, b0:b1], rstd[:, :, b0:b1], nwz[:, :, b0:b1]
                dve.wait_ge(pow_ready, k)
                newton(x, y, t)
                link(nc.vector.tensor_scalar(x, mv[:, :, b0:b1, 0], -1.0, None, ALU.mult))
                link(nc.vector.tensor_tensor(x, x, y, ALU.mult))

            add_patches(0)
            variances(0, 2)
            factors(0, 2, 1)

            def z(b):
                nc.vector.tensor_scalar(zA[:, :], H[:, ds(b, 1), :].rearrange("p b e -> p (b e)"), rstd[:, 0, ds(b, 1)],
                                        nmr[:, 0, ds(b, 1)], ALU.mult, ALU.add).then_inc(z_ready, 1)
                nc.vector.tensor_scalar(zB[:, :], hB[:, ds(b, 1), :].rearrange("p b e -> p (b e)"), rstd[0:SB, 1, ds(b, 1)],
                                        nmr[0:SB, 1, ds(b, 1)], ALU.mult, ALU.add).then_inc(z_ready, 1)

            def row_max(b, r):
                dve.wait_ge(score_ready, SPR * b + r + 1)
                if r < 3:
                    nc.vector.tensor_reduce(negmax[:, 4 * r:4 * r + 4], bS[r % 2][:, :].rearrange("p (h s) -> p h s", h=4),
                                            X, ALU.max, negate=True).then_inc(max_ready, 1)
                else:
                    q = 12 + 2 * (r - 3)
                    nc.vector.tensor_reduce(negmax[0:HB * SB, q:q + 2], bS[r % 2][0:HB * SB, 0:2 * SEQ].rearrange("p (h s) -> p h s", h=2),
                                            X, ALU.max, negate=True).then_inc(max_ready, 1)

            def row_factor(b, r):
                dve.wait_ge(exp_ready, SPR * b + r + 1)
                n, q0, q1, c = (128, 4 * r, 4 * r + 4, C_NA) if r < 3 else (HB * SB, 6 + 2 * r, 8 + 2 * r, C_NB)
                nc.vector.reciprocal(rinv[0:n, q0:q1], lsum[0:n, q0:q1]).then_inc(rinv_ready, 1)
                dve.wait_ge(rinv_ready, SPR * b + r + 1)
                nc.vector.tensor_scalar(rn[0:n, q0:q1], rinv[0:n, q0:q1], cst[0:n, c:c + 1], None, ALU.mult).then_inc(rn_ready, 1)

            def t_low(b, q):
                dve.wait_ge(t_used, t_before(b, q) + 1)
                dst, src = pt_round(q, 1, bT[BANK[q]])
                nc.vector.tensor_tensor(dst, src, pt_round(q, 0, bT[0])[0], ALU.subtract).then_inc(tl_used, 1)

            def o_low(b, g):
                dve.wait_ge(o_used, 4 * b + g + 1)
                dst, src = o_round(b, g, 1)
                nc.vector.scalar_tensor_tensor(dst, src, lncol[:, 0:1], o_round(b, g, 0)[0], ALU.mult, ALU.subtract).then_inc(ol_used, 1)

            def e_copy(b, g):
                dve.wait_ge(e_ready, 4 * b + g + 1)
                dst, src = e_round(b, g, 0)
                nc.vector.tensor_scalar(dst, src, lncol[:, 1:2], None, ALU.mult).then_inc(eh_ready, 1)
                dve.wait_ge(eh_ready, 4 * b + g + 1)
                nc.vector.scalar_tensor_tensor(e_round(b, g, 1)[0], src, lncol[:, 1:2], dst, ALU.mult, ALU.subtract).then_inc(e_used, 1)

            def value_low(b):
                dve.wait_ge(v_ready, 2 * (b + 1))
                for v, z in ((vA, zA), (vB, zB)):
                    nc.vector.tensor_tensor(v[1][:, 0:E0], z[:, 0:E0], v[0][:, 0:E0], ALU.subtract)
                    part = slice(E0 + E1, E0 + 2 * E1)
                    nc.vector.tensor_tensor(v[1][:, part], z[:, E0:EMB], v[0][:, part], ALU.subtract).then_inc(vl_ready, 1)
                dve.wait_ge(vl_ready, 2 * (b + 1))

            def wte_sum(k):
                for s in range(WBUF):
                    dve.wait_ge(wte_in[s], 16 * (WCHUNKS // WBUF - 1))
                q = slice(k * EMB // 4, (k + 1) * EMB // 4)
                nc.vector.tensor_reduce(wsum[:, q], wbuf[:, :].rearrange("p (r e) -> p e r", e=EMB)[:, q, :], X,
                                        ALU.add).then_inc(wte_added, 1)

            def residual_b(i):
                dve.wait_ge(jb_ready, i + 1)
                j = NBATCH + i
                nc.vector.tensor_tensor(H[0:BP, j, :], JBANK[i][0:BP, 0:EMB], H[0:BP, j, :], ALU.add).then_inc(jb_used, 1)
                dve.wait_ge(jb_used, i + 1)

            def wte_total():
                dve.wait_ge(wte_added, 4)
                dve.wait_ge(wtail_in, 16)
                nc.vector.tensor_tensor(wsum[0:WTAIL, :], wsum[0:WTAIL, :], wtail[:, :], ALU.add).then_inc(acc_ready, 1)

            def residual(b):
                dve.wait_ge(j_ready, b + 1)
                row = H[:, ds(b, 1), :].rearrange("p b e -> p (b e)")
                nc.vector.tensor_tensor(row, bJ[:, 0:EMB], row, ALU.add).then_inc(j_used, 1)

            z(0)
            for j in range(1, 4):
                add_patches(j)
            dve.wait_ge(t_used, 1)
            for g in range(4):
                hs, ss, dst = (slice(4 * g, 4 * g + 4), slice(0, SA), AwA) if g < 3 else (slice(0, HEADS), slice(SA, SEQ), AwB)
                o = dst[:, 0, hs, :]
                nc.vector.tensor_tensor(o, zT[:, 0, ss].unsqueeze(1).to_broadcast(list(o.shape)),
                                        w2[:, 0, hs].unsqueeze(2).to_broadcast(list(o.shape)), ALU.mult).then_inc(aw0_ready, 1)
            row_max(0, 0)
            row_max(0, 1)
            row_factor(0, 0)
            row_max(0, 2)
            row_factor(0, 1)
            row_factor(0, 2)
            value_low(0)
            dve.wait_ge(t_ready, 1)
            z(1)
            dve.wait_ge(late_in, 16 * 4)

            def b_rows(b):
                row_max(b, 3)
                row_max(b, 4)
                row_factor(b, 3)
                row_factor(b, 4)

            def iteration(b, more):
                if is0(b):
                    b_rows(b)
                t_low(b, 0)
                t_low(b, 1)
                if is0(b):
                    variances(2, NBATCH)
                else:
                    b_rows(b)
                if not more:
                    dve.wait_ge(late_in, 64)
                    residual_b(0)
                e_copy(b, 0)
                o_low(b, 0)
                t_low(b, 2)
                e_copy(b, 1)
                o_low(b, 1)
                e_copy(b, 2)
                o_low(b, 2)
                if not more:
                    wte_sum(0)
                    wte_sum(1)
                if is0(b):
                    factors(2, NBATCH, 2)
                    dve.wait_ge(woh_ready, 1)
                    nc.vector.tensor_tensor(woL[:, :, :], wo32, woH[:, :, :], ALU.subtract).then_inc(wol_ready, 1)
                row_max(b + 1, 0)
                if not more:
                    residual_b(1)
                t_low(b, 3)
                row_factor(b + 1, 0)
                t_low(b, 4)
                row_max(b + 1, 1)
                e_copy(b, 3)
                o_low(b, 3)
                row_factor(b + 1, 1)
                if not more:
                    wte_sum(2)
                    wte_sum(3)
                    wte_total()
                value_low(b + 1)
                if more:
                    dve.wait_ge(t_ready, t_before(b, "z") + 1)
                    z(b + 2)
                row_max(b + 1, 2)
                row_factor(b + 1, 2)
                if not more:
                    dve.wait_ge(avg_sum, 1)
                    nc.vector.tensor_scalar(avg[:, :], bE[:, 0:2], 1.0 / VOCAB, None, ALU.mult).then_inc(avg_ready, 1)
                    dve.wait_ge(c_ready, 1)
                    nc.vector.tensor_copy(cS[:, :], bE[:, 0:EMB])
                    nc.vector.tensor_scalar(cN[:, :], bE[:, 0:EMB], cst[:, C_NA:C_NA + 1], -1.0, ALU.mult, ALU.mult).then_inc(c_used, 1)
                    dve.wait_ge(c_used, 1)
                residual(b)

            iteration(0, True)
            nc.vector.tensor_reduce(ws[:, 0, :], wo32[:, 0:HEADS, :].rearrange("p h e -> p e h"), X, ALU.add)
            nc.vector.tensor_reduce(ws[:, 1, :], wo32[:, HEADS:WCH, :].rearrange("p h e -> p e h"), X, ALU.add).then_inc(pay_free, 1)
            with dve.Fori(1, NBATCH - 2) as b:
                iteration(b, True)
            iteration(NBATCH - 2, False)
            def stats(g):
                j0, j1, n = GROUPS[g]
                if g == 0:
                    dve.wait_ge(hc_ready, 1)
                elif j0 < NBATCH:
                    link(nc.vector.tensor_tensor(H[:, j0, :], H[:, j0, :], cN[:, :], ALU.add))
                else:
                    for j in range(j0, j1):
                        i = j - NBATCH
                        last = nc.vector.scalar_tensor_tensor(H[0:n, j, :], cS[0:n, :], cst[0:n, C_NBP + i:C_NBP + i + 1],
                                                              H[0:n, j, :], ALU.mult, ALU.add)
                    link(last)
                for j in range(j0, j1):
                    last = nc.vector.bn_stats(fst[0:n, j, :], H[0:n, j, :])
                link(last)
                for j in range(j0, j1):
                    last = nc.vector.bn_aggr(fmv[0:n, j, :], fst[0:n, j, :])
                link(last)
                v = fmv[0:n, j0:j1, 1]
                link(nc.vector.tensor_scalar(var[0:n, 0, j0:j1], v, 1e-5, None, ALU.add))
                nc.vector.tensor_scalar(var[0:n, 1, j0:j1], v, 1.0 + 1e-6, 1e-11, ALU.mult, ALU.add).then_inc(var_ready, 1)

            def norms(g):
                j0, j1, n = GROUPS[g]
                dve.wait_ge(pow_ready, 3 + g)
                newton(var[0:n, :, j0:j1], rsq[0:n, :, j0:j1], nwt[0:n, :, j0:j1])
                for j in range(j0, j1):
                    last = nc.vector.tensor_scalar(norm[0:n, j, :], H[0:n, j, :], fmv[0:n, j, 0:1], rsq[0:n, 1, j:j + 1],
                                                   ALU.subtract, ALU.mult)
                link(last)
                nc.vector.tensor_tensor(norm[0:n, j0:j1, :], norm[0:n, j0:j1, :],
                                        flnb[0:n, :].unsqueeze(1).to_broadcast([n, j1 - j0, EMB]), ALU.mult).then_inc(norm_ready, 1)
                link(nc.vector.tensor_scalar(rsq1[0:n, j0:j1], rsq[0:n, 0, j0:j1], 1.0, None, ALU.add))
                nc.vector.scalar_tensor_tensor(nmb[0:n, j0:j1], fmv[0:n, j0:j1, 0], -1.0, rsq[0:n, 0, j0:j1], ALU.mult,
                                               ALU.mult).then_inc(basepar_ready, 1)

            def part(t, B):
                return t[0:BP, NBATCH:SLOTS] if B else t[:, 0:NBATCH]

            def routed(B):
                n, s = (BP, NBT) if B else (128, NBATCH)
                bc = [n, s, EXP]
                dve.wait_ge(lg_ready, B + 1)
                logits = bE[0:n, B * NBATCH * EXP:(B * NBATCH + s) * EXP].rearrange("p (j x) -> p j x", j=s)
                em = cst2[0:n, C_EM:C_EM + EXP].unsqueeze(1).to_broadcast(bc)
                l, t = part(lg, B), part(l1, B)
                link(nc.vector.tensor_reduce(part(lmax, B), logits, X, ALU.max))
                nc.vector.tensor_tensor(l, logits, part(lmax, B).unsqueeze(2).to_broadcast(bc), ALU.subtract).then_inc(le_ready, 1)
                dve.wait_ge(le_ready, B + 1)
                link(nc.vector.scalar_tensor_tensor(t, l, 0.0, em, ALU.is_ge, ALU.mult))
                link(nc.vector.tensor_reduce(part(lidx, B), t, X, ALU.min))
                nc.vector.tensor_tensor(part(oh, B), em, part(lidx, B).unsqueeze(2).to_broadcast(bc), ALU.is_equal).then_inc(oh_ready, 1)
                dve.wait_ge(lx_ready, B + 1)
                link(nc.vector.tensor_reduce(part(lsm, B), part(lx, B), X, ALU.add))
                link(nc.vector.reciprocal(pay[0:n, B * NBATCH:B * NBATCH + s, D_RP], part(lsm, B)))

            def keep(B):
                n, s = (BP, NBT) if B else (128, NBATCH)
                dve.wait_ge(oh_ready, B + 1)
                dve.wait_ge(rank_ready, B + 1)
                nc.vector.scalar_tensor_tensor(part(kp, B), (bJ, bO[1])[B][0:n, 0:s * EXP].rearrange("p (j x) -> p j x", j=s),
                                               float(CAP), part(oh, B), ALU.is_lt, ALU.mult).then_inc(kp_ready, 1)
                dve.wait_ge(kp_ready, B + 1)
                link(nc.vector.tensor_reduce(part(kept, B), part(kp, B), X, ALU.add))
                link(nc.vector.tensor_scalar(part(drop, B), part(kept, B), -1.0, 1.0, ALU.mult, ALU.add))

            def place(B):
                n, s = (BP, NBT) if B else (128, NBATCH)
                bc = [n, s, EXP]
                dve.wait_ge(grank_ready, B + 1)
                gk = bT[0][0:n, B * NBATCH * EXP:(B * NBATCH + s) * EXP].rearrange("p (j x) -> p j x", j=s)
                cnt = bT[0][:, SLOTS * EXP:(SLOTS + 1) * EXP]
                link(nc.vector.tensor_scalar(capI[:, B, :], cnt, float(T - 1), float(DIV), ALU.add, ALU.mult))
                link(nc.vector.tensor_scalar(capI[:, B, :], capI[:, B, :], 20, None, ALU.logical_shift_right))
                link(nc.vector.tensor_scalar(capF[:, B, :], capI[:, B, :], float(T), None, ALU.mult))
                t, u = part(l1, B), part(l2, B)
                if B:
                    link(nc.vector.tensor_tensor(capB[:, :], capF[:, 1, :], capF[:, 0, :], ALU.subtract))
                    link(nc.vector.tensor_tensor_scan(cum[:, 1, :], oneX[:, :], capB[:, :], cum[:, 0, EXP - 1:EXP], ALU.mult, ALU.add))
                    link(nc.vector.tensor_tensor(bex[:, :], cum[:, :, :].rearrange("p t x -> p (t x)"),
                                                 cst2[:, C_BI:C_BI + 1].to_broadcast([128, 2 * EXP]), ALU.is_le))
                    nc.vector.tensor_reduce(beC[:, :], bex[:, :], X, ALU.add).then_inc(be_ready, 1)
                    link(nc.vector.tensor_tensor(first[:, 1, :], cum[:, 1, :], capF[:, 1, :], ALU.subtract))
                    link(nc.vector.tensor_tensor(first[:, 1, :], first[:, 1, :], first[:, 0, :], ALU.subtract))
                    link(nc.vector.tensor_tensor(t, gk, capF[0:n, 0, :].unsqueeze(1).to_broadcast(bc), ALU.is_ge))
                    link(nc.vector.tensor_tensor(t, t, first[0:n, 1, :].unsqueeze(1).to_broadcast(bc), ALU.mult))
                    link(nc.vector.tensor_tensor(t, t, first[0:n, 0, :].unsqueeze(1).to_broadcast(bc), ALU.add))
                    link(nc.vector.tensor_tensor(u, gk, t, ALU.add))
                else:
                    link(nc.vector.tensor_tensor_scan(cum[:, 0, :], oneX[:, :], capF[:, 0, :], 0.0, ALU.mult, ALU.add))
                    link(nc.vector.tensor_tensor(first[:, 0, :], cum[:, 0, :], capF[:, 0, :], ALU.subtract))
                    link(nc.vector.tensor_tensor(u, gk, first[0:n, 0, :].unsqueeze(1).to_broadcast(bc), ALU.add))
                link(nc.vector.tensor_tensor(u, u, part(kp, B), ALU.mult))
                link(nc.vector.tensor_reduce(part(posF, B), u, X, ALU.add))
                nc.vector.scalar_tensor_tensor(part(posI, B), part(drop, B), float(BIG), part(posF, B), ALU.mult, ALU.add).then_inc(pos_ready, 1)
                if not B:
                    link(nc.vector.tensor_scalar(bex[0:1, 0:EXP], cum[0:1, 0, :], 0.0, None, ALU.is_le))
                    link(nc.vector.tensor_reduce(beC[0:1, :], bex[0:1, 0:EXP], X, ALU.add))
                    nc.vector.tensor_copy(be0[0:1, :], beC[0:1, :]).then_inc(be0_ready, 1)

            t_low(LAST, 0)
            t_low(LAST, 1)
            b_rows(LAST)
            e_copy(LAST, 0)
            o_low(LAST, 0)
            t_low(LAST, 2)
            e_copy(LAST, 1)
            o_low(LAST, 1)
            e_copy(LAST, 2)
            o_low(LAST, 2)
            stats(0)
            t_low(LAST, 3)
            t_low(LAST, 4)
            dve.wait_ge(cst2_in, 16)
            dve.wait_ge(mat_ready, 1)
            nc.vector.tensor_copy(pay[:, :, D_ROW], cst2[:, C_ROW:C_ROW + SLOTS])
            e_copy(LAST, 3)
            o_low(LAST, 3)
            norms(0)
            residual(LAST)
            dve.wait_ge(j_used, NBATCH)
            stats(1)
            stats(2)
            norms(1)
            norms(2)
            residual_b(2)
            stats(3)
            dve.wait_ge(ohz_ready, 2)
            routed(0)
            norms(3)
            keep(0)
            place(0)
            routed(1)
            keep(1)
            place(1)
            dve.wait_ge(be_row, 1)
            link(nc.vector.tensor_copy(beI[:, 0:MAXB], bS[1][0:1, 0:MAXB]))
            link(nc.vector.tensor_scalar(beI[:, 0:MAXB], beI[:, 0:MAXB], EXP - 1, None, ALU.bitwise_and))
            nc.vector.tensor_scalar(nbI[:, 0:1], cum[0:1, 1, EXP - 1:EXP], 1.0 / T, 0.25, ALU.mult, ALU.add).then_inc(tab_ready, 1)
            dve.wait_ge(base_ready, SLOTS)
            for j in range(SLOTS):
                n = 128 if j < NBATCH else BP
                nc.vector.scalar_tensor_tensor(drow[0:n, j, :], norm[0:n, j, :], pay[0:n, j, D_RP:D_RP + 1], base[0:n, j, :], ALU.mult, ALU.add)
            link(nc.vector.scalar_tensor_tensor(dropF[:, 0:NBATCH], kept[:, 0:NBATCH], float(BIG), pay[:, 0:NBATCH, D_ROW], ALU.mult, ALU.add))
            link(nc.vector.scalar_tensor_tensor(dropF[0:BP, NBATCH:SLOTS], kept[0:BP, NBATCH:SLOTS], float(BIG), pay[0:BP, NBATCH:SLOTS, D_ROW], ALU.mult, ALU.add))
            nc.vector.tensor_copy(dropI[:, 0:NBATCH], dropF[:, 0:NBATCH])
            nc.vector.tensor_copy(dropI[0:BP, NBATCH:SLOTS], dropF[0:BP, NBATCH:SLOTS]).then_inc(drop_ready, 1)

            dve.wait_ge(tab_ready, 1)
            nb = dve.value_load(nbI[0:1, 0:1], min_val=MINB, max_val=MAXB)

            def xt_copy(b):
                dve.wait_ge(xT_sum, b + 1)
                nc.vector.tensor_copy(xT, bT[1][0:EC, 0:2 * T].rearrange("p (k n) -> p k n", k=2)).then_inc(xT_ready, 1)

            xt_copy(0)

            def block_step(i, q):
                b, p = i * XBUF + q, q % 2
                dve.wait_ge(h1_sum, b + 1)
                nc.vector.tensor_scalar(hT[:, 4:6, :], bO[1][:, 0:2 * T].rearrange("p (c n) -> p c n", c=2), 0.0, None,
                                        ALU.max).then_inc(h1_ready, 1)
                xt_copy(b + 1)
                if q >= 2 or not is0(i):
                    dve.wait_ge(y_out[p], (i * 2 + q // 2) * 16)
                nc.vector.tensor_copy(yrow[p][:, :], xb[q][:, D_ROW:D_ROW + 1])
                dve.wait_ge(y_sum, b + 1)
                nc.vector.scalar_tensor_tensor(ysb[p], bE[0:T, 0:EMB], xb[q][:, D_RP:D_RP + 1], xb[q][:, D_BASE:D_BASE + EMB],
                                               ALU.mult, ALU.add).then_inc(y_ready, 1)

            for_blocks(dve, nb, block_step)

        @block.tensor
        def _(pe):
            SPLIT = ((0, 0), (1, 0), (0, 1))

            def mm(o, l, r, start=True, stop=True):
                return nc.tensor.matmul(o, l, r, start=start, stop=stop, skip_group_check=True)

            def stay_warm(bank, n):
                for _ in range(n):
                    mm(bank[:, :], ones[:, :], ones[:, :].unsqueeze(1).to_broadcast([128, 4, 128]))

            pe.wait_ge(ones_ready, 1)
            stay_warm(bS[0], 14)
            pe.wait_ge(pat_in, 32)
            for k2 in range(2):
                for k in range(6):
                    last = mm(bO[k2][0:EC, 0:NBATCH * IMG], pw_sb[:, k, k2 * EC:(k2 + 1) * EC], pat_sb[:, k, :], k == 0, k == 5)
                last.then_inc(emb_ready, 1)
            pe.wait_ge(cst_in, 16)
            pe.wait_ge(embT_ready, 2)
            for j in range(4):
                bank = (bT[0], bE, bJ, bO[1])[j]
                for c in range(4):
                    b, k = 2 * j + c // 2, c % 2
                    last = nc.tensor.transpose(bank[0:IMG, c * EC:(c + 1) * EC], embT[:, k, b * IMG:(b + 1) * IMG], ident[0:EC, 0:EC])
                last.then_inc(tok_ready, 1)

            HS = HB * SB
            mask4 = maskA[:, :].unsqueeze(1).to_broadcast([128, 4, SA])
            mask2 = maskB[0:HS, :].unsqueeze(1).to_broadcast([HS, 2, SEQ])

            def z_transpose(b, par):
                pe.wait_ge(z_ready, 2 * (b + 1))
                pe.wait_ge(cst_in, 16)
                for k in range(2):
                    nc.tensor.transpose(bT[par][0:EC, k * SEQ:k * SEQ + SA], zA[:, k * EC:(k + 1) * EC], ident)
                    last = nc.tensor.transpose(bT[par][0:EC, k * SEQ + SA:(k + 1) * SEQ], zB[:, k * EC:(k + 1) * EC], ident[0:SB, 0:SB])
                last.then_inc(t_ready, 1)

            def score(b, r, first=False):
                bank = bS[r % 2]
                if is0(b):
                    pe.wait_ge(aw0_ready, min(r + 1, 4))
                    pe.wait_ge(aw_ready, min(r + 1, 4))
                else:
                    pe.wait_ge(aw_ready, 8 * b - 4 + min(2 * r + 2, 8))
                if not first:
                    pe.wait_ge(exp_ready, SPR * b + max(r - 1, 0))
                if r < 3:
                    mm(bank[:, :].rearrange("p (h s) -> p h s", h=4), idb[:, :], mask4, True, False)
                    for j in range(4):
                        for k in range(2):
                            last = mm(bank[:, j * SA:(j + 1) * SA], AwA[:, k, 4 * r + j, :], zT[:, k, 0:SA], False, k == 1)
                else:
                    mm(bank[0:HS, 0:2 * SEQ].rearrange("p (h s) -> p h s", h=2), idb[0:HS, 0:HS], mask2, True, False)
                    for j in range(2):
                        q = 2 * (r - 3) + j
                        for k in range(2):
                            last = mm(bank[0:HS, j * SEQ:(j + 1) * SEQ], AwB[:, k, HB * q:HB * (q + 1), :].rearrange("p h s -> p (h s)"), zT[:, k, :], False, k == 1)
                last.then_inc(score_ready, 1)

            def p_transpose(b, q):
                if q < 4:
                    pe.wait_ge(p_ready, SPR * b + (q + 1 if q < 3 else SPR))
                if q == 1:
                    pe.wait_ge(t_used, TPB * b + 1)
                elif q == 2:
                    pe.wait_ge(tl_used, 5 * b + 2)
                elif q == 3:
                    pe.wait_ge(t_used, t_before(b, 2))
                bank = bT[BANK[q]]
                if q < 3:
                    for j in range(4):
                        last = nc.tensor.transpose(bank[:, j * SA:(j + 1) * SA], PA[:, 4 * q + j, :], ident)
                else:
                    for g in range(NG):
                        if q == 3:
                            last = nc.tensor.transpose(bank[:, g * HS:(g + 1) * HS], PB[:, g, 0:SA], ident[0:HS, 0:HS])
                        else:
                            last = nc.tensor.transpose(bank[0:SB, g * HS:(g + 1) * HS], PB[:, g, SA:SEQ], ident[0:HS, 0:HS])
                last.then_inc(t_ready, 1)

            def value(b, g):
                if g == 0:
                    pe.wait_ge(vl_ready, 2 * (b + 1))
                    if is0(b):
                        pe.wait_ge(tok_added, 4)
                        pe.wait_ge(vz_ready, 8)
                    else:
                        pe.wait_ge(ol_used, 4 * b)
                elif g > 1:
                    pe.wait_ge(ol_used, 4 * b + g - 1)
                pe.wait_ge(tl_used, 5 * b + (g + 1 if g < 3 else 5))
                o = bO[g % 2]
                for i, (x, y) in enumerate(SPLIT):
                    if g < 3:
                        last = mm(o[:, :].rearrange("p (h s) -> p h s", h=4), vA[x][:, 0:E0], PTA[y][:, 4 * g:4 * g + 4, :], i == 0, i == 2)
                    else:
                        oo = o[:, 0:HEADS * SB].rearrange("p (h s) -> p h s", h=HEADS)
                        mm(oo, vA[x][:, 0:E0], PTB0[y][:, :, :], i == 0, False)
                        last = mm(oo, vB[x][:, 0:E0], PTB1[y][:, :, :], False, i == 2)
                last.then_inc(o_ready, 1)
                if g or not is0(b):
                    pe.wait_ge(e_used, 4 * b + g)
                for odd in range(2):
                    part = slice(E0 + (1 - odd) * E1, E0 + (3 - odd) * E1)
                    for i, (x, y) in enumerate(SPLIT):
                        first, final = odd == 0 and i == 0, odd == 1 and i == 2
                        if g < 3:
                            last = mm(bE[:, 0:2 * SA].rearrange("p (h s) -> p h s", h=2), vA[x][:, part],
                                      PTA[y][:, 4 * g + odd:4 * g + 4:2, :], first, final)
                        else:
                            ee = bE[:, 0:6 * SB].rearrange("p (h s) -> p h s", h=6)
                            mm(ee, vA[x][:, part], PTB0[y][:, odd:HEADS:2, :], first, False)
                            last = mm(ee, vB[x][:, part], PTB1[y][:, odd:HEADS:2, :], False, final)
                last.then_inc(e_ready, 1)

            def project(b, c0, c1):
                if c0 == 0:
                    pe.wait_ge(wol_ready, 1)
                    if not is0(b):
                        pe.wait_ge(j_used, b)
                    pe.wait_ge(ol_used, 4 * b + 3)
                    pe.wait_ge(e_used, 4 * b + 3)
                for c in range(c0, c1):
                    for i, (x, y) in enumerate(SPLIT):
                        last = mm(bJ[:, 0:EMB], oTA[x][:, c, :], (woH, woL)[y][:, c, :], c == 0 and i == 0, c == WCH - 1 and i == 2)
                if c1 == WCH:
                    last.then_inc(j_ready, 1)

            def b_scores(b):
                score(b, 3)
                score(b, 4)

            def start(b):
                if is0(b):
                    b_scores(b)
                p_transpose(b, 0)
                p_transpose(b, 1)
                if not is0(b):
                    b_scores(b)

            stay_warm(bS[0], 16)
            z_transpose(0, 0)
            stay_warm(bS[0], 8)
            pe.wait_ge(bf_ready, 3)
            for r in range(3):
                score(0, r, r < 2)

            def wte_mean():
                pe.wait_ge(acc_ready, 1)
                pe.wait_ge(e_used, 4 * LAST)
                mm(bE[:, 0:1], wsum[:, 0:E0], one[:, :])
                mm(bE[0:E1, 1:2], wsum[:, E0:EMB], one[:, :])
                mm(bE[E1:128, 1:2], wsum[:, E0:EMB], one[:, :]).then_inc(avg_sum, 1)

            def mean_projected():
                pe.wait_ge(avg_ready, 1)
                for k in range(2):
                    last = mm(bE[:, 0:EMB], avg[:, k:k + 1].to_broadcast([128, 128]), ws[:, k, :], k == 0, k == 1)
                last.then_inc(c_ready, 1)

            def project_b(i, c0=0, c1=WCH):
                if c0 == 0:
                    done = 4 * (NBATCH if i == 2 else LAST - 1)
                    pe.wait_ge(ol_used, done)
                    pe.wait_ge(e_used, done)
                    if i < 2:
                        pe.wait_ge(j_used, LAST - 1)
                    if i == 1:
                        pe.wait_ge(jb_used, 1)
                for c in range(c0, c1):
                    for k, (x, y) in enumerate(SPLIT):
                        last = mm(JBANK[i][0:BP, 0:EMB], oTB[x][:, c, i * BP:(i + 1) * BP], (woH, woL)[y][:, c, :],
                                  c == 0 and k == 0, c == WCH - 1 and k == 2)
                if c1 == WCH:
                    last.then_inc(jb_ready, 1)

            def iteration(b, final=False):
                start(b)
                if final:
                    project_b(0)
                if is0(b):
                    pe.wait_ge(tok_added, 4)
                    stay_warm(bJ, 12)
                pe.wait_ge(tl_used, 5 * b + 1)
                z_transpose(b + 1, 1)
                value(b, 0)
                p_transpose(b, 2)
                value(b, 1)
                value(b, 2)
                if final:
                    project_b(1)
                if is0(b):
                    stay_warm(bJ, 14)
                pe.wait_ge(t_used, t_before(b, "z") + 1)
                score(b + 1, 0)
                p_transpose(b, 3)
                if final:
                    pe.wait_ge(jb_used, 2)
                project(b, 0, 4)
                p_transpose(b, 4)
                score(b + 1, 1)
                value(b, 3)
                project(b, 4, 10)
                score(b + 1, 2)
                if final:
                    project(b, 10, 12)
                    pe.wait_ge(exp_ready, SPR * (b + 1) + 2)
                    stay_warm(bS[1], 5)
                    wte_mean()
                    project(b, 12, 16)
                    stay_warm(bS[1], 8)
                    mean_projected()
                    project(b, 16, WCH)
                else:
                    project(b, 10, WCH)

            iteration(0)
            with pe.Fori(1, LAST - 1) as b:
                iteration(b)
            iteration(LAST - 1, True)
            start(LAST)
            pe.wait_ge(c_used, 1)
            value(LAST, 0)
            p_transpose(LAST, 2)
            value(LAST, 1)
            value(LAST, 2)
            p_transpose(LAST, 3)
            pe.wait_ge(exp_ready, SPR * NBATCH)
            stay_warm(bS[1], 5)
            project(LAST, 0, 4)
            p_transpose(LAST, 4)
            project(LAST, 4, 9)
            value(LAST, 3)
            project(LAST, 9, WCH)

            def logits(j0, j1, done):
                pe.wait_ge(nT_ready, done)
                for j in range(j0, j1):
                    n, c = (BP, NBATCH * 128 + (j - NBATCH) * BP) if j >= NBATCH else (128, j * 128)
                    for k in range(2):
                        last = mm(bE[0:n, j * EXP:(j + 1) * EXP], nT[:, k, c:c + n], wr_sb[:, k, :], k == 0, k == 1)
                if j1 in (NBATCH, SLOTS):
                    last.then_inc(lg_ready, 1)

            def n_transpose(j0, j1, k, bank, c0=0):
                n = 128 if j0 < NBATCH else BP
                for j in range(j0, j1):
                    c = c0 + (j - j0) * n
                    last = nc.tensor.transpose(bank[0:EC, c:c + n], norm[0:n, j, k * EC:(k + 1) * EC], ident[0:n, 0:n])
                return last

            tri = mat[:, M_TRI, :]

            def batch_rank(B):
                pe.wait_ge(oh_ready, B + 1)
                if not B:
                    pe.wait_ge(j_used, NBATCH)
                    mm(bJ[:, 0:NBATCH * EXP], tri, oh[:, 0:NBATCH, :].rearrange("p j x -> p (j x)")).then_inc(rank_ready, 1)
                    return
                for i in range(NBT):
                    o = bO[1][0:BP, i * EXP:(i + 1) * EXP]
                    mm(o, mat[:, M_BB + i, 0:BP], oh[:, NBATCH + i, :], True, False)
                    if i:
                        mm(o, mat[:, M_BX + i - 1, 0:BP], oh[:, NBATCH + i - 1, :], False, False)
                    own = [m for m, (ii, b) in enumerate(PAIRS) if ii == i]
                    for m in own:
                        last = mm(o, mat[:, M_BA + m, 0:BP], oh[:, PAIRS[m][1], :], False, m == own[-1])
                last.then_inc(rank_ready, 1)

            def expert_rank(B):
                pe.wait_ge(kp_ready, B + 1)
                gk, end = bT[0], (SLOTS + 1) * EXP
                lo, hi = (NBATCH, SLOTS) if B else (0, NBATCH)
                mm(gk[:, lo * EXP:hi * EXP], tri, kp[:, lo:hi, :].rearrange("p j x -> p (j x)"), not B, False)
                for j in range(lo, hi):
                    last = mm(gk[:, (j + 1) * EXP:end].rearrange("p (j x) -> p j x", x=EXP), ones[:, :],
                              kp[:, j, :].unsqueeze(1).to_broadcast([128, SLOTS - j, EXP]), False, j == SLOTS - 1)
                last.then_inc(grank_ready, 1)

            project_b(2, 0, 12)
            pe.wait_ge(t_used, TPB * NBATCH)
            pe.wait_ge(tl_used, 5 * NBATCH)
            pe.wait_ge(exp_ready, SPR * NBATCH)
            pe.wait_ge(norm_ready, 1)
            for k in range(2):
                n_transpose(0, 4, k, bS[k]).then_inc(nT_sum, 1)
            for k in range(2):
                n_transpose(4, 7, k, bT[k]).then_inc(nT_sum, 1)
            project_b(2, 12, WCH)
            pe.wait_ge(e_used, 4 * NBATCH)
            logits(0, 4, 2)
            logits(4, 7, 4)
            pe.wait_ge(norm_ready, 2)
            n_transpose(7, 8, 0, bO[1])
            n_transpose(7, 8, 1, bO[1], 128).then_inc(nT_sum, 1)
            logits(7, 8, 5)
            pe.wait_ge(mat_ready, 1)
            batch_rank(0)
            expert_rank(0)
            pe.wait_ge(norm_ready, len(GROUPS))
            for k in range(2):
                n_transpose(NBATCH, SLOTS, k, bS[k]).then_inc(nT_sum, 1)
            logits(NBATCH, SLOTS, 7)
            batch_rank(1)
            expert_rank(1)
            pe.wait_ge(be_ready, 1)
            mm(bS[1][0:1, 0:MAXB], beC[:, 0:1], ident[:, 0:MAXB]).then_inc(be_row, 1)
            stay_warm(bJ, 32)

            pe.wait_ge(tab_ready, 1)
            nb = pe.value_load(nbI[0:1, 0:1], min_val=MINB, max_val=MAXB)

            def x_transpose(q, at):
                pe.wait_ge(x_in[q], at)
                for k in range(2):
                    last = nc.tensor.transpose(bT[1][0:EC, k * T:(k + 1) * T], xb[q][:, k * EC:(k + 1) * EC], ident[0:T, 0:T])
                last.then_inc(xT_sum, 1)

            x_transpose(0, 16)

            def block_step(i, q):
                b, p, turn = i * XBUF + q, q % 2, (i * 2 + q // 2 + 1) * 16
                pe.wait_ge(xT_ready, b + 1)
                pe.wait_ge(wi_in[p], turn)
                for c in range(FC):
                    bank, cc = (bO[0], c) if c < 4 else (bO[1], c - 4)
                    for k in range(2):
                        last = mm(bank[:, cc * T:(cc + 1) * T], wi_sb[p][:, k, c, :], xT[:, k, :], k == 0, k == 1)
                    if c == 3:
                        last.then_inc(h0_sum, 1)
                last.then_inc(h1_sum, 1)
                x_transpose((q + 1) % XBUF, (i + 1 + (q + 1) // XBUF) * 16)
                pe.wait_ge(wox_in[p], turn)
                pe.wait_ge(h0_ready, b + 1)
                if not (is0(i) and q == 0):
                    pe.wait_ge(y_ready, b)
                for c in range(FC):
                    if c == 4:
                        pe.wait_ge(h1_ready, b + 1)
                    last = mm(bE[0:T, 0:EMB], hT[:, c, :], wo_x[p][:, c, :], c == 0, c == FC - 1)
                last.then_inc(y_sum, 1)

            for_blocks(pe, nb, block_step)


def constants():
    p = np.arange(128)
    c = np.zeros((128, NCST), np.float32)
    c[:, C_ID:C_ID + 128] = np.eye(128)
    c[:, C_MA:C_MA + SA] = np.where(p[None, :] > p[:, None], NEG, 0)
    c[:, C_MB:C_MB + SEQ] = np.where(np.arange(SEQ)[None, :] > SA + p[:, None] % SB, NEG, 0)
    c[:, C_NA] = 1.0 / (p + 1)
    c[:, C_NB] = 1.0 / (SA + p % SB + 1)
    for i in range(NBT):
        c[:, C_NBP + i] = -1.0 / (SA + (i * BP + p) % SB + 1)
    d = np.zeros((128, C_MAT), np.float32)
    d[:, C_EM:C_EM + EXP] = np.arange(EXP) - EXP
    for j in range(NBATCH):
        d[:, C_ROW + j] = j * SEQ + p
    for i in range(NBT):
        t = i * BP + p
        d[:, C_ROW + NBATCH + i] = np.where(p < BP, t // SB * SEQ + SA + t % SB, BIG)
    d[:, C_BI] = p * T
    m = np.zeros((128, NMAT, 128), np.float32)
    m[:, M_TRI] = p[:, None] < p[None, :]

    def batch(i):
        return np.where(p < BP, (i * BP + p) // SB, -1 - i)
    for i in range(NBT):
        same = batch(i)[:, None] == batch(i)[None, :]
        m[:, M_BB + i] = same & (p[:, None] < p[None, :]) & (p[:, None] < BP)
        if i:
            m[:, M_BX + i - 1] = batch(i - 1)[:, None] == batch(i)[None, :]
    for n, (i, b) in enumerate(PAIRS):
        m[:, M_BA + n] = (batch(i) == b)[None, :]
    return c, np.concatenate([d, m.reshape(128, NMAT * 128)], 1)


def kernel(**inputs):
    import concourse.bacc as bacc
    from concourse.bass_utils import run_bass_kernel_spmd as run

    a = {k: np.asarray(v) for k, v in inputs.items()}
    con = np.ascontiguousarray
    P, G = 16, 6
    x = a["x"].reshape(NBATCH, 3, G, P, G, P).transpose(0, 1, 3, 5, 2, 4).reshape(NBATCH, IMG, 768)
    pat = con(x.reshape(NBATCH * IMG, 6, 128).transpose(2, 1, 0))
    projw = con(a["L0_tok_proj_w"].reshape(EMB, 6, 128).transpose(2, 1, 0))
    txt, cut = a["txt"], SA - IMG
    tail = txt[:, cut:]
    ln = a["L0_attn_ln_w"]
    wo4 = a["L0_attn_W_o"].reshape(EMB, HEADS, EMB).transpose(1, 2, 0)
    wo_attn = np.concatenate([wo4[:, :E0], wo4[:, E0:].reshape(HEADS // 2, 128, EMB)], 0).transpose(1, 0, 2)
    cst, cst2 = constants()
    arrays = {
        "patches": pat, "projw": projw,
        "projb": con(np.broadcast_to(a["L0_tok_proj_b"], (IMG, EMB))), "pos": con(a["L0_tok_pos_embed"][0]),
        "txtA": con(txt[:, :cut].transpose(1, 0, 2)), "txtB": con(tail.transpose(1, 0, 2)),
        "txtBp": con(tail.reshape(NBT, BP, EMB).transpose(1, 0, 2)),
        "wqk": con(a["L0_attn_W_qk"].reshape(HEADS, 2, EC).transpose(2, 1, 0)),
        "lnw": con(ln.reshape(2, EC).T), "lnc": con(np.stack([ln[:E0], np.concatenate([ln[E0:], ln[E0:]])], 1)),
        "wte": a["L0_attn_wte"], "wo_attn": con(wo_attn),
        "flnw": con(np.broadcast_to(a["L0_ffn_ln_w"], (128, EMB))),
        "wrt": con(a["L0_ffn_w_router"].reshape(2, EC, EXP).transpose(1, 0, 2)),
        "wi": con(a["L0_ffn_wi"].reshape(EXP, 2, EC, FC, 128).transpose(0, 2, 1, 3, 4)),
        "wo": con(a["L0_ffn_wo"].reshape(EXP, FC, 128, EMB).transpose(0, 2, 1, 3)),
        "cst": cst, "cst2": cst2,
    }
    nc = bacc.Bacc("TRN2", target_bir_lowering=False, num_devices=1)
    args = [nc.dram_tensor("in_" + k, v.shape, mybir.dt.from_np(v.dtype), kind="ExternalInput").ap() for k, v in arrays.items()]
    out = nc.dram_tensor("out", (TOK, EMB), mybir.dt.float32, kind="ExternalOutput").ap()
    program(nc, *args, out)
    r = run(nc, [{"in_" + k: v for k, v in arrays.items()}], core_ids=[0])
    return r.results[0]["out"].reshape(NBATCH, SEQ, EMB)
```
